# Optimizing a Trainium2 kernel written in Bass

```python
import numpy as np
import jax
import jax.numpy as jnp

def _softmax(x, axis=-1):
    return jax.nn.softmax(x, axis=axis)

def _gelu(x):
    return jax.nn.gelu(x, approximate=True)

def _silu(x):
    return jax.nn.silu(x)

def _sigmoid(x):
    return jax.nn.sigmoid(x)

def _layernorm(x, axis=-1, eps=1e-05):
    m = jnp.mean(x, axis=axis, keepdims=True)
    v = jnp.var(x, axis=axis, keepdims=True)
    return (x - m) / jnp.sqrt(v + eps)

def _scatter_add(tgt, idx, src, axis=0):
    return tgt.at[idx].add(src)

def _segment_sum(src, seg, n):
    return jax.ops.segment_sum(src, seg, n)
kernel_name = 'mk_gnn_resnorm_d2_gnn_r32_9633d2'

def setup_inputs(seed: int=0):
    np.random.seed(seed)
    _w = jnp.asarray

    def _rec_inputs():
        import jax
        import jax.numpy as jnp
        _gk = jax.random.key(seed)
        x = 0.0001712 + 1 * jax.random.normal(jax.random.fold_in(_gk, 1), (3125, 16), jnp.float32)
        src = jax.random.randint(jax.random.fold_in(_gk, 2), (100000,), 0, 3125, jnp.int32)
        dst = jax.random.randint(jax.random.fold_in(_gk, 3), (100000,), 0, 3125, jnp.int32)
        _o = jnp.argsort(dst, stable=True)
        src = src[_o]
        dst = dst[_o]
        return (x, src, dst)
    x, src, dst = _rec_inputs()

    def _L0_gnn_setup():
        import jax, jax.numpy as jnp
        import numpy as np
        STALK_DIM = 16
        N_NODES = 50000
        N_EDGES = 12500
        HIDDEN = 64
        key = jax.random.key(seed)
        k1, k2, k3, k4 = jax.random.split(key, 4)
        d = STALK_DIM
        x = jax.random.normal(k1, (N_NODES, d), dtype=jnp.float32)
        edge_index = jax.random.randint(k2, (2, N_EDGES), 0, N_NODES, dtype=jnp.int64)
        W1 = jax.random.normal(k3, (HIDDEN, 2 * d), dtype=jnp.float32) * (1.0 / np.sqrt(2 * d))
        b1 = jnp.zeros((HIDDEN,), dtype=jnp.float32)
        W2 = jax.random.normal(k4, (d, HIDDEN), dtype=jnp.float32) * (1.0 / np.sqrt(HIDDEN))
        b2 = jnp.zeros((d,), dtype=jnp.float32)
        return {'x': x, 'edge_index': edge_index, 'W1': W1, 'b1': b1, 'W2': W2, 'b2': b2}
    _L0_gnn_all = _L0_gnn_setup()
    _L0_gnn_in = {k: v for k, v in _L0_gnn_all.items() if k in ('W1', 'b1', 'W2', 'b2')}
    del _L0_gnn_all

    def _L1_gnn_setup():
        import jax, jax.numpy as jnp
        import numpy as np
        BN_EPS = 1e-05

        def gcn_conv(x, edge_index, W, b, num_nodes):
            src, dst = (edge_index[0], edge_index[1])
            loop = jnp.arange(num_nodes, dtype=edge_index.dtype)
            src_f = jnp.concatenate([src, loop])
            dst_f = jnp.concatenate([dst, loop])
            deg = jax.ops.segment_sum(jnp.ones_like(dst_f, dtype=x.dtype), dst_f, num_segments=num_nodes)
            dinv = jnp.where(deg > 0, jax.lax.rsqrt(deg), 0.0)
            norm = dinv[src_f] * dinv[dst_f]
            h = x @ W
            msg = h[src_f] * norm[:, None]
            out = jax.ops.segment_sum(msg, dst_f, num_segments=num_nodes)
            return out + b
        key = jax.random.key(seed)
        k = jax.random.split(key, 6)
        N, E, D, H = (3125, 62500, 16, 32)
        x = jax.random.normal(k[0], (N, D), dtype=jnp.float32)
        edge_index = jax.random.randint(k[1], (2, E), 0, N, dtype=jnp.int64)
        W1 = jax.random.normal(k[2], (D, H), dtype=jnp.float32) / np.sqrt(D)
        b1 = jnp.zeros((H,), dtype=jnp.float32)
        gamma = jnp.ones((H,), dtype=jnp.float32)
        beta = jnp.zeros((H,), dtype=jnp.float32)
        W2 = jax.random.normal(k[3], (H, D), dtype=jnp.float32) / np.sqrt(H)
        b2 = jnp.zeros((D,), dtype=jnp.float32)
        return {'x': x, 'edge_index': edge_index, 'W1': W1, 'b1': b1, 'gamma': gamma, 'beta': beta, 'W2': W2, 'b2': b2, 'num_nodes': N}
    _L1_gnn_all = _L1_gnn_setup()
    _L1_gnn_in = {k: v for k, v in _L1_gnn_all.items() if k in ('W1', 'b1', 'gamma', 'beta', 'W2', 'b2')}
    del _L1_gnn_all
    return {'x': x, 'src': src, 'dst': dst, 'L0_gnn_W1': _L0_gnn_in['W1'], 'L0_gnn_b1': _L0_gnn_in['b1'], 'L0_gnn_W2': _L0_gnn_in['W2'], 'L0_gnn_b2': _L0_gnn_in['b2'], 'L1_gnn_W1': _L1_gnn_in['W1'], 'L1_gnn_b1': _L1_gnn_in['b1'], 'L1_gnn_gamma': _L1_gnn_in['gamma'], 'L1_gnn_beta': _L1_gnn_in['beta'], 'L1_gnn_W2': _L1_gnn_in['W2'], 'L1_gnn_b2': _L1_gnn_in['b2']}

def reference(x, src, dst, L0_gnn_W1, L0_gnn_b1, L0_gnn_W2, L0_gnn_b2, L1_gnn_W1, L1_gnn_b1, L1_gnn_gamma, L1_gnn_beta, L1_gnn_W2, L1_gnn_b2):
    import jax
    import jax.numpy as jnp

    def _L0_gnn_ref(x, edge_index, W1, b1, W2, b2):
        import jax, jax.numpy as jnp
        import numpy as np
        STALK_DIM = 16
        N_NODES = 50000
        N_EDGES = 12500
        HIDDEN = 64
        d = x.shape[1]
        n = x.shape[0]
        src, dst = (edge_index[0], edge_index[1])
        xs, xd = (x[src], x[dst])

        def reflection(a, b):
            h = jax.nn.relu(jnp.concatenate([a, b], axis=1) @ W1.T + b1)
            return h @ W2.T + b2

        def householder(v):
            vn = v / jnp.maximum(jnp.linalg.norm(v, axis=1, keepdims=True), 1e-12)
            return jnp.eye(d, dtype=v.dtype)[None] - 2.0 * vn[:, :, None] * vn[:, None, :]
        F_s = householder(reflection(xs, xd))
        F_d = householder(reflection(xd, xs))
        L_sd = -jnp.einsum('eki,ekj->eij', F_s, F_d)
        ones_e = jnp.ones(src.shape[0], dtype=x.dtype)
        deg = jnp.zeros(n, dtype=x.dtype).at[src].add(ones_e).at[dst].add(ones_e)
        deg_inv_sqrt = 1.0 / jnp.sqrt(jnp.maximum(deg, 1e-05))
        coef = deg_inv_sqrt[src] * deg_inv_sqrt[dst]
        msg_s = coef[:, None] * jnp.einsum('eij,ej->ei', L_sd, xd)
        msg_d = coef[:, None] * jnp.einsum('eji,ej->ei', L_sd, xs)
        out = x - jnp.zeros_like(x).at[src].add(msg_s) - jnp.zeros_like(x).at[dst].add(msg_d)
        return jax.nn.relu(out)

    def _L1_gnn_ref(x, edge_index, W1, b1, gamma, beta, W2, b2, num_nodes):
        import jax, jax.numpy as jnp
        import numpy as np
        BN_EPS = 1e-05

        def gcn_conv(x, edge_index, W, b, num_nodes):
            src, dst = (edge_index[0], edge_index[1])
            loop = jnp.arange(num_nodes, dtype=edge_index.dtype)
            src_f = jnp.concatenate([src, loop])
            dst_f = jnp.concatenate([dst, loop])
            deg = jax.ops.segment_sum(jnp.ones_like(dst_f, dtype=x.dtype), dst_f, num_segments=num_nodes)
            dinv = jnp.where(deg > 0, jax.lax.rsqrt(deg), 0.0)
            norm = dinv[src_f] * dinv[dst_f]
            h = x @ W
            msg = h[src_f] * norm[:, None]
            out = jax.ops.segment_sum(msg, dst_f, num_segments=num_nodes)
            return out + b
        h = gcn_conv(x, edge_index, W1, b1, num_nodes)
        mean = jnp.mean(h, axis=0)
        var = jnp.var(h, axis=0)
        h = (h - mean) * jax.lax.rsqrt(var + BN_EPS) * gamma + beta
        h = jax.nn.relu(h)
        out = gcn_conv(h, edge_index, W2, b2, num_nodes)
        return out
    edge_index = jnp.stack([src, dst])
    x = _layernorm(x + _L0_gnn_ref(x, edge_index, L0_gnn_W1, L0_gnn_b1, L0_gnn_W2, L0_gnn_b2), axis=-1)
    x = _layernorm(x + _L1_gnn_ref(x, edge_index, L1_gnn_W1, L1_gnn_b1, L1_gnn_gamma, L1_gnn_beta, L1_gnn_W2, L1_gnn_b2, 3125), axis=-1)
    return x

_drawn_inputs = setup_inputs


def setup_inputs(seed=0):
    import zlib

    import numpy as np

    out = dict(_drawn_inputs(seed))
    spreads = {'L0_gnn_b1': (0.0, 0.8),
     'L0_gnn_b2': (0.0, 0.556),
     'L1_gnn_b1': (0.0, 0.8),
     'L1_gnn_gamma': (1.0, 0.2),
     'L1_gnn_beta': (0.0, 0.1),
     'L1_gnn_b2': (0.0, 0.1)}
    factors = {}
    for name, (base, spread) in spreads.items():
        noise = np.random.default_rng([zlib.crc32(name.encode()), seed]).standard_normal(out[name].shape)
        drawn = base * np.exp(spread * noise) if base else spread * noise
        out[name] = jnp.asarray(drawn.astype(out[name].dtype))
    for name, factor in factors.items():
        out[name] = (out[name] * factor).astype(out[name].dtype)
    return out
```

```python
import concourse.bass as bass
from concourse import mybir
from contextlib import ExitStack

F32 = mybir.dt.float32
BF16 = mybir.dt.bfloat16
I32 = mybir.dt.int32
ALU = mybir.AluOpType
ACT = mybir.ActivationFunctionType
AX = mybir.AxisListType

P = 128
N_NODES = 3125
N_EDGES = 100000
D = 16
HID0 = 64
HID1 = 32
LO = 8
NB = -(-(N_NODES + 1) // LO)
NT = -(-NB // P)
TAIL = NB - (NT - 1) * P
PAD = N_NODES
QLO = 64
NQ = -(-(NB * LO) // QLO)
G = 4
NCH = -(-N_EDGES // (P * G)) * G
NG = NCH // G
RT = -(-NCH // P)
HG = 16
LN_EPS = 1e-5
KR = (N_NODES - (NT - 1) * P * LO) // LO


def gnn(nc, x, src, dst, w0_in, b0_in, w0_out, b0_out, w1, b1, gamma, beta, w2, b2, consts, out):
    with ExitStack() as ctx:
        def sb(name, shape, dt=F32):
            return ctx.enter_context(nc.sbuf_tensor(name, shape, dt))

        def sem(name):
            return ctx.enter_context(nc.semaphore(name))

        cst = sb("cst", [P, 2 * P + NB])
        ident = cst[:, 0:P]
        same_unit = cst[:, P:2 * P]
        iota_b = cst[:, 2 * P:2 * P + NB]
        zeros = sb("zeros", [P, P])
        iota_q = sb("iota_q", [P, QLO, HG], BF16)
        rows_i = sb("rows_i", [P, 2, RT, P], I32)
        rows_f = sb("rows_f", [P, 2, RT, P])
        node_i = sb("node_i", [P, 2, NCH], I32)
        part_i = sb("part_i", [P, 2, NCH], I32)
        a_f = sb("a_f", [P, 2, NCH])
        b_f = sb("b_f", [P, 2, NCH])
        q_bf = sb("q_bf", [P, 2, NCH], BF16)
        p_bf = sb("p_bf", [P, 2, NCH], BF16)
        w_hid = sb("w_hid", [64, 2 * HID0])
        w_ref = sb("w_ref", [2 * HID0, 2 * D])
        bias_hid = sb("bias_hid", [2 * HID0, 1])
        bias_ref = sb("bias_ref", [P, 2, D])
        bias_rep = sb("bias_rep", [P, G * 2, D])
        w1_diag = sb("w1_diag", [P, 2, P])
        w2_diag = sb("w2_diag", [P, 2, P])
        bn_vec = sb("bn_vec", [P, 3])
        bias_out = sb("bias_out", [P, D])
        oh_q = sb("oh_q", [P, 2, QLO, HG], BF16)
        oh_p = sb("oh_p", [P, 2, NQ, HG], BF16)
        hist = sb("hist", [NQ, 2, QLO])
        cnt = sb("cnt", [P, 2, NT, LO])
        dinv = sb("dinv", [P, 2, NT * LO])
        x_n = sb("x_n", [P, NT * LO, D])
        x1_n = sb("x1_n", [P, NT * LO, D])
        y_n = sb("y_n", [P, NT * LO, D])
        s_n = sb("s_n", [P, NT * LO, D])
        t_n = sb("t_n", [P, NT * LO, D])
        tab = sb("tab", [P, NT, LO, 2 * D])
        st = sb("st", [P, 4, NT * LO])
        al = sb("al", [P, NB])
        h_al = sb("h_al", [P, 2, NB])
        hc_al = sb("hc_al", [P, 2, NB])
        bn = sb("bn", [P, 8])
        idx_stage = sb("idx_stage", [P, 2, 2, G], I32)
        g_xy = sb("g_xy", [P, 2, G, 2, 2 * D])
        xT = sb("xT", [64, 2, G * P])
        hidT = sb("hidT", [P, 2, G * P])
        v = sb("v", [P, G * 2, D])
        prod = sb("prod", [P, G * 2, D])
        z = sb("z", [P, G, 2, D])
        msg = sb("msg", [P, 2, G * 2, D])
        n2 = sb("n2", [P, G * 2])
        cc = sb("cc", [P, G * 2])
        dots = sb("dots", [P, G * 2])
        oh_a = sb("oh_a", [P, 2, G * 2, LO])
        m8 = sb("m8", [P, 2, G * 2, LO, D])
        RING = 4
        oh_b = sb("oh_b", [P, RING, NB])
        hist_d = nc.dram_tensor("hist_d", (2, NQ * QLO), F32, kind="Internal").ap()
        table = [nc.dram_tensor(f"table{k}", (NB * LO, w), F32, kind="Internal").ap()
                 for k, w in enumerate((2 * D, D, D))]

        banks = [ctx.enter_context(nc.psum_tensor(f"bank{i}", [P, 512], F32)) for i in range(8)]
        acc = banks[0]
        p_tr = banks[1:3]
        p_hid = banks[3:5]
        p_ref = banks[5:7]
        misc = banks[7]

        loaded = sem("loaded")
        padded = sem("padded")
        dve = sem("dve_step")
        idx_rows = sem("idx_rows")
        idx_cols = sem("idx_cols")
        parts = sem("parts")
        oh_hist = [sem(f"oh_hist{s}") for s in range(2)]
        hist_used = [sem(f"hist_used{s}") for s in range(2)]
        hist_done = sem("hist_done")
        hist_sb = sem("hist_sb")
        hist_out = sem("hist_out")
        hist_in = sem("hist_in")
        deg_ready = sem("deg_ready")
        deg_root = sem("deg_root")
        tab_ready = [sem(f"tab_ready{k}") for k in range(3)]
        tab_out = [sem(f"tab_out{k}") for k in range(3)]
        staged = [sem(f"staged{u}") for u in range(2)]
        gathered = [sem(f"gathered{u}") for u in range(2)]
        g_free_dve = [sem(f"g_free_dve{u}") for u in range(2)]
        turned = [sem(f"turned{u}") for u in range(2)]
        x_ready = [sem(f"x_ready{u}") for u in range(2)]
        pre_ready = [sem(f"pre_ready{u}") for u in range(2)]
        hid_ready = [sem(f"hid_ready{u}") for u in range(2)]
        ref_ready = [sem(f"ref_ready{u}") for u in range(2)]
        v_taken = [sem(f"v_taken{u}") for u in range(2)]
        m_ready = [sem(f"m_ready{u}") for u in range(2)]
        oh_ready = [sem(f"oh_ready{r}") for r in range(RING)]
        oh_used = [sem(f"oh_used{r}") for r in range(RING)]
        l_staged = [[sem(f"l{k}_staged{u}") for u in range(2)] for k in range(2)]
        l_gathered = [[sem(f"l{k}_gathered{u}") for u in range(2)] for k in range(2)]
        l_free = [[sem(f"l{k}_free{u}") for u in range(2)] for k in range(2)]
        l_ready = [[sem(f"l{k}_ready{u}") for u in range(2)] for k in range(2)]
        l_oha = [sem(f"l{k}_oha") for k in range(2)]
        l_oh = [[sem(f"l{k}_oh{r}") for r in range(RING)] for k in range(2)]
        l_ohu = [[sem(f"l{k}_ohu{r}") for r in range(RING)] for k in range(2)]
        acc_ready = [sem(f"acc_ready{k}") for k in range(3)]
        al_ready = [sem(f"al_ready{k}") for k in range(5)]
        nl_ready = [sem(f"nl_ready{k}") for k in range(4)]
        root_in = [sem(f"root_in{k}") for k in range(3)]
        root_out = [sem(f"root_out{k}") for k in range(3)]
        agg_ready = sem("agg_ready")
        h_ready = sem("h_ready")
        sum_in = [sem(f"sum_in{k}") for k in range(2)]
        sum_out = [sem(f"sum_out{k}") for k in range(2)]
        bn_ready = sem("bn_ready")
        relu_ready = sem("relu_ready")
        u_ready = sem("u_ready")
        u_sb = sem("u_sb")
        out_ready = sem("out_ready")
        stored = sem("stored")

        n_loads = 0
        block = ctx.enter_context(nc.Block())

        @block.sync
        def _(sync):
            nonlocal n_loads

            def load(dst_ap, src_ap):
                nonlocal n_loads
                n_loads += 1
                nc.sync.dma_start(dst_ap, src_ap).then_inc(loaded, 16)

            sync.wait_ge(padded, 1)
            full = N_EDGES // P
            for s, e in enumerate((src, dst)):
                load(rows_i[:, s, 0:RT - 1, :], e[0:(RT - 1) * P * P].rearrange("(t r e) -> r t e", r=P, e=P))
                last = full - (RT - 1) * P
                load(rows_i[0:last, s, RT - 1, :], e[(RT - 1) * P * P:full * P].rearrange("(r e) -> r e", e=P))
                load(rows_i[last:last + 1, s, RT - 1, 0:N_EDGES - full * P],
                     e[full * P:N_EDGES].rearrange("(r e) -> r e", r=1))
            load(cst[:, :], consts)
            m = (NT - 1) * P * LO
            load(x_n[:, 0:(NT - 1) * LO, :].rearrange("p (t a) f -> p t (a f)", a=LO),
                 x[0:m, :].rearrange("(t b a) f -> b t (a f)", b=P, a=LO))
            k = (N_NODES - m) // LO
            load(x_n[0:k, (NT - 1) * LO:NT * LO, :].rearrange("p a f -> p (a f)"),
                 x[m:m + k * LO, :].rearrange("(b a) f -> b (a f)", a=LO))
            left = N_NODES - m - k * LO
            load(x_n[k:k + 1, (NT - 1) * LO:(NT - 1) * LO + left, :].rearrange("p a f -> p (a f)"),
                 x[m + k * LO:N_NODES, :].rearrange("(b a) f -> b (a f)", b=1))
            load(w_hid[0:D, 0:HID0], w0_in[0:D, :])
            load(w_hid[0:D, HID0:2 * HID0], w0_in[D:2 * D, :])
            load(w_hid[2 * D:3 * D, 0:HID0], w0_in[D:2 * D, :])
            load(w_hid[2 * D:3 * D, HID0:2 * HID0], w0_in[0:D, :])
            for s in range(2):
                load(w_ref[s * HID0:(s + 1) * HID0, s * D:(s + 1) * D], w0_out)
                load(bias_hid[s * HID0:(s + 1) * HID0, :], b0_in.unsqueeze(1))
                load(bias_ref[:, s, :], b0_out.unsqueeze(0).to_broadcast([P, D]))
            for a in range(LO):
                h, r = a // 4, a % 4
                load(w1_diag[a * D:(a + 1) * D, h, r * HID1:(r + 1) * HID1], w1)
                load(w2_diag[r * HID1:(r + 1) * HID1, h, a * D:(a + 1) * D], w2)
            for r in range(4):
                for j, vec in enumerate((b1, gamma, beta)):
                    load(bn_vec[r * HID1:(r + 1) * HID1, j:j + 1], vec.unsqueeze(1))
            load(bias_out[:, :], b2.unsqueeze(0).to_broadcast([P, D]))

            sync.wait_ge(hist_sb, 1)
            nc.sync.dma_start(hist_d.rearrange("s (p q) -> p s q", q=QLO), hist[:, :, :]).then_inc(hist_out, 16)
            sync.wait_ge(hist_out, 16)
            for s in range(2):
                nc.sync.dma_start(cnt[:, s, 0:NT - 1, :],
                                  hist_d[s, 0:m].rearrange("(t b a) -> b t a", b=P, a=LO)).then_inc(hist_in, 16)
                nc.sync.dma_start(cnt[0:TAIL, s, NT - 1, :],
                                  hist_d[s, m:NB * LO].rearrange("(b a) -> b a", a=LO)).then_inc(hist_in, 16)

            def store_table(k, tile):
                sync.wait_ge(tab_ready[k], 1)
                nc.sync.dma_start(table[k][0:m, :].rearrange("(t b a) f -> b t (a f)", b=P, a=LO),
                                  tile[:, 0:NT - 1, :]).then_inc(tab_out[k], 16)
                nc.sync.dma_start(table[k][m:NB * LO, :].rearrange("(b a) f -> b (a f)", a=LO),
                                  tile[0:TAIL, NT - 1, :]).then_inc(tab_out[k], 16)

            store_table(0, tab[:, :, :, :].rearrange("p t a f -> p t (a f)"))
            for k in (1, 2):
                store_table(k, y_n[:, :, :].rearrange("p (t a) f -> p t (a f)", a=LO))
            sync.wait_ge(out_ready, 1)
            nc.sync.dma_start(out[0:m, :].rearrange("(t b a) f -> b t (a f)", b=P, a=LO),
                              s_n[:, 0:(NT - 1) * LO, :].rearrange("p (t a) f -> p t (a f)", a=LO)).then_inc(stored, 16)
            nc.sync.dma_start(out[m:m + KR * LO, :].rearrange("(b a) f -> b (a f)", a=LO),
                              s_n[0:KR, (NT - 1) * LO:NT * LO, :].rearrange("p a f -> p (a f)")).then_inc(stored, 16)
            nc.sync.dma_start(out[m + KR * LO:N_NODES, :].rearrange("(b a) f -> b (a f)", b=1),
                              s_n[KR:KR + 1, (NT - 1) * LO:(NT - 1) * LO + left, :]
                              .rearrange("p a f -> p (a f)")).then_inc(stored, 16)
            sync.wait_ge(stored, 48)

        LOADED = 16 * n_loads

        @block.gpsimd
        def _(pool):
            pool.wait_ge(parts, 1)
            pool.wait_ge(tab_out[0], 32)
            for u in range(2):
                pool.sem_inc(g_free_dve[u], 1)
            with pool.Fori(0, NG // 2) as i:
                for u in range(2):
                    pool.wait_ge(turned[u], i + 1)
                    nc.gpsimd.tensor_copy(idx_stage[:, u, :, :],
                                          node_i[:, :, bass.ds(i * (2 * G) + u * G, G)]).then_inc(staged[u], 1)
                    pool.wait_ge(staged[u], i + 1)
                    pool.nop(nofuse=True)
                    pool.wait_ge(g_free_dve[u], i + 1)
                    pool.nop(nofuse=True)
                    for c in range(G):
                        for s in range(2):
                            nc.gpsimd.indirect_dma_start(
                                out=g_xy[:, u, c, s, :], out_offset=None, in_=table[0],
                                in_offset=bass.IndirectOffsetOnAxis(ap=idx_stage[:, u, s, c:c + 1], axis=0)
                            ).then_inc(gathered[u], 16)
            for k in range(2):
                pool.wait_ge(tab_out[k + 1], 32)
                for u in range(2):
                    pool.sem_inc(l_free[k][u], 1)
                with pool.Fori(0, NG // 2) as i:
                    for u in range(2):
                        pool.wait_ge(l_free[k][u], i + 1)
                        nc.gpsimd.tensor_copy(idx_stage[:, u, 0, :],
                                              node_i[:, 0, bass.ds(i * (2 * G) + u * G, G)]).then_inc(l_staged[k][u], 1)
                        pool.wait_ge(l_staged[k][u], i + 1)
                        pool.nop(nofuse=True)
                        for c in range(G):
                            nc.gpsimd.indirect_dma_start(
                                out=g_xy[:, u, c, 0, 0:D], out_offset=None, in_=table[k + 1],
                                in_offset=bass.IndirectOffsetOnAxis(ap=idx_stage[:, u, 0, c:c + 1], axis=0)
                            ).then_inc(l_gathered[k][u], 16)

        @block.scalar
        def _(act):
            act.wait_ge(deg_ready, 1)
            nc.scalar.activation(dinv[:, :, :], dinv[:, :, :], ACT.Sqrt).then_inc(deg_root, 1)

            def front(n, u):
                act.wait_ge(turned[u], n + 1)
                nc.scalar.activation(xT[:, u, :], p_tr[u][0:64, :], ACT.Copy).then_inc(x_ready[u], 1)
                act.wait_ge(pre_ready[u], n)
                nc.scalar.activation(hidT[:, u, :], p_hid[u][:, :], ACT.Relu,
                                     bias=bias_hid[:, 0:1]).then_inc(hid_ready[u], 1)

            act.wait_ge(loaded, LOADED)
            with act.Fori(0, NG // 2) as i:
                front(i + 1, 0)
                front(i + 1, 1)

            def root(k):
                act.wait_ge(root_in[k], 1)
                nc.scalar.activation(st[:, 2, :], st[:, 2, :], ACT.Sqrt).then_inc(root_out[k], 1)

            root(0)
            act.wait_ge(root_in[1], 1)
            nc.scalar.activation(bn[:, 3:4], bn[:, 3:4], ACT.Sqrt).then_inc(root_out[1], 1)
            act.wait_ge(bn_ready, 1)
            for h in range(2):
                nc.scalar.activation(h_al[:, h, :], hc_al[:, h, :], ACT.Relu, scale=bn[:, 5:6],
                                     bias=bn_vec[:, 2:3]).then_inc(relu_ready, 1)
            root(2)

        @block.vector
        def _(vec):
            n_steps = 0

            def step(ins, at=None):
                nonlocal n_steps
                n_steps += 1
                ins.then_inc(dve, 1)
                vec.wait_ge(dve, n_steps if at is None else at[0] * at[1] + n_steps)

            V = nc.vector
            for tile, value in ((rows_i, PAD), (x_n, 0.0), (w_hid, 0.0), (w_ref, 0.0), (w1_diag, 0.0), (w2_diag, 0.0),
                                (cnt, 0.0), (zeros, 0.0), (tab, 0.0), (s_n, 0.0)):
                ins = V.memset(tile[tuple(slice(None) for _ in tile.shape)], value)
            ins.then_inc(padded, 1)
            vec.wait_ge(padded, 1)
            vec.wait_ge(loaded, LOADED)
            V.tensor_copy(rows_f[:, :, :, :], rows_i[:, :, :, :]).then_inc(idx_rows, 1)
            step(V.tensor_copy(iota_q[:, :, :], iota_b[:, 0:QLO].unsqueeze(2).to_broadcast([P, QLO, HG])))
            vec.wait_ge(idx_cols, 1)
            for s in range(2):
                for t in range(2):
                    w = min(4 * P, NCH - t * 4 * P)
                    ins = V.tensor_copy(node_i[:, s, t * 4 * P:t * 4 * P + w], banks[1 + 2 * s + t][:, 0:w])
            step(ins)
            for mask, shift, to in ((LO - 1, None, a_f), (None, 3, b_f), (QLO - 1, None, q_bf), (None, 6, p_bf)):
                if shift is None:
                    step(V.tensor_scalar(part_i[:, :, :], node_i[:, :, :], mask, None, ALU.bitwise_and))
                else:
                    step(V.tensor_scalar(part_i[:, :, :], node_i[:, :, :], shift, None, ALU.logical_shift_right))
                step(V.tensor_copy(to[:, :, :], part_i[:, :, :]))
            V.tensor_copy(part_i[:, 0, 0:1], node_i[:, 0, 0:1]).then_inc(parts, 1)
            with vec.Fori(0, NCH // HG) as i:
                for s in range(2):
                    vec.wait_ge(hist_used[s], i + 1)
                    V.tensor_tensor(oh_q[:, s, :, :], q_bf[:, s, bass.ds(i * HG, HG)].unsqueeze(1).to_broadcast([P, QLO, HG]),
                                    iota_q[:, :, :], ALU.is_equal)
                    V.tensor_tensor(oh_p[:, s, :, :], p_bf[:, s, bass.ds(i * HG, HG)].unsqueeze(1).to_broadcast([P, NQ, HG]),
                                    iota_q[:, 0:NQ, :], ALU.is_equal).then_inc(oh_hist[s], 1)
            vec.wait_ge(hist_done, 1)
            V.tensor_copy(hist[:, :, :], misc[0:NQ, 0:2 * QLO].rearrange("p (s q) -> p s q", s=2)).then_inc(hist_sb, 1)
            vec.wait_ge(hist_in, 64)
            c2 = cnt[:, :, :, :].rearrange("p s t a -> p s (t a)")
            step(V.tensor_tensor(dinv[:, 0, :], c2[:, 0, :], c2[:, 1, :], ALU.add))
            V.tensor_scalar(dinv[:, 0, :], dinv[:, 0, :], 1e-5, None, ALU.max)
            V.tensor_scalar(dinv[:, 1, :], c2[:, 1, :], 1.0, None, ALU.add).then_inc(deg_ready, 1)
            vec.wait_ge(deg_root, 1)
            step(V.reciprocal(dinv[:, :, :], dinv[:, :, :]))
            d0 = dinv[:, 0, :].unsqueeze(2).to_broadcast([P, NT * LO, D])
            d1 = dinv[:, 1, :].unsqueeze(2).to_broadcast([P, NT * LO, D])
            tabv = tab[:, :, :, :].rearrange("p t a f -> p (t a) f")
            V.tensor_copy(tabv[:, :, 0:D], x_n[:, :, :])
            V.tensor_tensor(tabv[:, :, D:2 * D], x_n[:, :, :], d0, ALU.mult).then_inc(tab_ready[0], 1)

            def bcast(t):
                return t.unsqueeze(2).to_broadcast([P, G * 2, D])

            def reflect(n, u, at):
                vec.wait_ge(ref_ready[u], n)
                ins = V.tensor_tensor(v[:, :, :], p_ref[u][:, 0:G * 2 * D].rearrange("p (c f) -> p c f", f=D),
                                      bias_rep[:, :, :], ALU.add)
                ins.then_inc(v_taken[u], 1)
                vec.wait_ge(v_taken[u], n + 1)
                step(V.tensor_tensor(prod[:, :, :], v[:, :, :], v[:, :, :], ALU.mult), at)
                step(V.tensor_reduce(n2[:, :], prod[:, :, :], AX.X, ALU.add), at)
                step(V.tensor_scalar(n2[:, :], n2[:, :], 1e-24, 0.5, ALU.max, ALU.mult), at)
                step(V.reciprocal(cc[:, :], n2[:, :]), at)
                vec.wait_ge(gathered[u], n * (16 * 2 * G))
                y = g_xy[:, u, :, :, D:2 * D].rearrange("p c s f -> p (c s) f")
                step(V.tensor_tensor(prod[:, :, :], v[:, :, :], y, ALU.mult), at)
                step(V.tensor_reduce(dots[:, :], prod[:, :, :], AX.X, ALU.add), at)
                step(V.tensor_tensor(dots[:, :], dots[:, :], cc[:, :], ALU.mult), at)
                step(V.tensor_tensor(prod[:, :, :], v[:, :, :], bcast(dots[:, :]), ALU.mult), at)
                for s in range(2):
                    ins = V.tensor_tensor(z[:, :, 1 - s, :], g_xy[:, u, :, s, D:2 * D],
                                          prod[:, :, :].rearrange("p (c s) f -> p c s f", s=2)[:, :, s, :], ALU.subtract)
                ins.then_inc(g_free_dve[u], 1)
                vec.wait_ge(g_free_dve[u], n + 1)
                zz = z[:, :, :, :].rearrange("p c s f -> p (c s) f")
                step(V.tensor_tensor(prod[:, :, :], v[:, :, :], zz, ALU.mult), at)
                step(V.tensor_reduce(dots[:, :], prod[:, :, :], AX.X, ALU.add), at)
                step(V.tensor_tensor(dots[:, :], dots[:, :], cc[:, :], ALU.mult), at)
                step(V.tensor_tensor(prod[:, :, :], v[:, :, :], bcast(dots[:, :]), ALU.mult), at)
                V.tensor_tensor(msg[:, u, :, :], zz, prod[:, :, :], ALU.subtract)
                for s in range(2):
                    ins = V.tensor_tensor(oh_a[:, u, :, :].rearrange("p (c s) a -> p c s a", s=2)[:, :, s, :],
                                          a_f[:, s, bass.ds(at[2], G)].unsqueeze(2).to_broadcast([P, G, LO]),
                                          iota_b[:, 0:LO].unsqueeze(1).to_broadcast([P, G, LO]), ALU.is_equal)
                step(ins, at)
                V.tensor_tensor(m8[:, u, :, :, :], oh_a[:, u, :, :].unsqueeze(3).to_broadcast([P, G * 2, LO, D]),
                                msg[:, u, :, :].unsqueeze(2).to_broadcast([P, G * 2, LO, D]),
                                ALU.mult).then_inc(m_ready[u], 1)

            def one_hots(n, r0, sides, chunk, ready, used):
                for c in range(G):
                    for s in sides:
                        r = r0 % RING
                        vec.wait_ge(used[r], n + r0 // RING)
                        V.tensor_scalar(oh_b[:, r, :], iota_b, b_f[:, s, bass.ds(chunk + c, 1)], None,
                                        ALU.is_equal).then_inc(ready[r], 1)
                        r0 += 1
                return r0

            step(V.tensor_copy(bias_rep[:, :, :].rearrange("p (g s) f -> p g (s f)", s=2),
                               bias_ref[:, :, :].rearrange("p s f -> p (s f)").unsqueeze(1).to_broadcast([P, G, 2 * D])))
            SPG = 13
            before = n_steps
            with vec.Fori(0, NG // 2) as i:
                for u in range(2):
                    chunk = i * (2 * G) + u * G
                    reflect(i + 1, u, (i, 2 * SPG, chunk))
                    one_hots(i * (2 * 2 * G // RING) + 1, u * 2 * G, (0, 1), chunk, oh_ready, oh_used)
            assert n_steps == before + 2 * SPG, n_steps - before
            n_steps = before + NG * SPG

            def to_nodes(k):
                vec.wait_ge(acc_ready[k], 1)
                V.tensor_copy(al[:, :], acc[:, 0:NB]).then_inc(al_ready[k], 1)
                vec.wait_ge(nl_ready[k], 1)
                w = (NT - 1) * LO
                V.tensor_copy(s_n[:, 0:w, :], misc[:, 0:w * D].rearrange("p (c f) -> p c f", f=D))
                step(V.tensor_copy(s_n[0:TAIL, w:w + LO, :],
                                   misc[0:TAIL, w * D:(w + LO) * D].rearrange("p (c f) -> p c f", f=D)))

            def nbc(t):
                return t.unsqueeze(2).to_broadcast([P, NT * LO, D])

            def layer_norm(k, to, last=None):
                step(V.tensor_reduce(st[:, 0, :], s_n[:, :, :], AX.X, ALU.add))
                step(V.tensor_scalar(st[:, 1, :], st[:, 0, :], 1.0 / D, None, ALU.mult))
                step(V.tensor_tensor(s_n[:, :, :], s_n[:, :, :], nbc(st[:, 1, :]), ALU.subtract))
                step(V.tensor_tensor(t_n[:, :, :], s_n[:, :, :], s_n[:, :, :], ALU.mult))
                step(V.tensor_reduce(st[:, 0, :], t_n[:, :, :], AX.X, ALU.add))
                V.tensor_scalar(st[:, 2, :], st[:, 0, :], 1.0 / D, LN_EPS, ALU.mult, ALU.add).then_inc(root_in[k], 1)
                vec.wait_ge(root_out[k], 1)
                step(V.reciprocal(st[:, 3, :], st[:, 2, :]))
                ins = V.tensor_tensor(to[:, :, :], s_n[:, :, :], nbc(st[:, 3, :]), ALU.mult)
                if last is None:
                    step(ins)
                else:
                    ins.then_inc(last, 1)

            to_nodes(0)
            step(V.tensor_tensor(s_n[:, :, :], s_n[:, :, :], d0, ALU.mult))
            step(V.tensor_tensor(s_n[:, :, :], s_n[:, :, :], x_n[:, :, :], ALU.add))
            step(V.scalar_tensor_tensor(s_n[:, :, :].rearrange("p c f -> p (c f)"),
                                        s_n[:, :, :].rearrange("p c f -> p (c f)"), 0.0,
                                        x_n[:, :, :].rearrange("p c f -> p (c f)"), ALU.max, ALU.add))
            layer_norm(0, x1_n)
            V.tensor_tensor(y_n[:, :, :], x1_n[:, :, :], d1, ALU.mult).then_inc(tab_ready[1], 1)
            vec.wait_ge(tab_ready[1], 1)

            def aggregate(k):
                with vec.Fori(0, NG // 2) as i:
                    for u in range(2):
                        chunk = i * (2 * G) + u * G
                        V.tensor_tensor(oh_a[:, u, 0:G, :], a_f[:, 1, bass.ds(chunk, G)].unsqueeze(2).to_broadcast([P, G, LO]),
                                        iota_b[:, 0:LO].unsqueeze(1).to_broadcast([P, G, LO]), ALU.is_equal).then_inc(l_oha[k], 1)
                        vec.wait_ge(l_oha[k], i * 2 + u + 1)
                        vec.wait_ge(l_gathered[k][u], i * (16 * G) + 16 * G)
                        V.tensor_tensor(m8[:, u, 0:G, :, :], oh_a[:, u, 0:G, :].unsqueeze(3).to_broadcast([P, G, LO, D]),
                                        g_xy[:, u, :, 0, 0:D].unsqueeze(2).to_broadcast([P, G, LO, D]),
                                        ALU.mult).then_inc(l_ready[k][u], 1)
                        vec.wait_ge(l_ready[k][u], i + 1)
                        V.tensor_copy(st[0:1, 0, 0:1], st[0:1, 1, 0:1]).then_inc(l_free[k][u], 1)
                        one_hots(i * (2 * G // RING) + 1, u * G, (1,), chunk, l_oh[k], l_ohu[k])

            aggregate(0)
            to_nodes(1)
            step(V.tensor_tensor(s_n[:, :, :], s_n[:, :, :], y_n[:, :, :], ALU.add))
            V.tensor_tensor(s_n[:, :, :], s_n[:, :, :], d1, ALU.mult).then_inc(agg_ready, 1)
            vec.wait_ge(al_ready[3], 1)
            V.tensor_copy(al[:, :], misc[:, 0:NB]).then_inc(al_ready[4], 1)
            vec.wait_ge(h_ready, 1)
            for h in range(2):
                ins = V.tensor_scalar(h_al[:, h, :], banks[1 + h][:, 0:NB], bn_vec[:, 0:1], None, ALU.add)
            step(ins)

            def zero_padding(t):
                for a in range(N_NODES - (NB - 1) * LO, LO):
                    r = (a - 4) * HID1
                    ins = V.memset(t[r:r + HID1, 1, NB - 1:NB], 0.0)
                step(ins)

            zero_padding(h_al)
            hf = h_al[:, :, :].rearrange("p h b -> p (h b)")
            hcf = hc_al[:, :, :].rearrange("p h b -> p (h b)")
            V.tensor_reduce(bn[:, 0:1], hf, AX.X, ALU.add).then_inc(sum_in[0], 1)
            vec.wait_ge(sum_out[0], 1)
            step(V.tensor_scalar(bn[:, 1:2], p_hid[0][:, 0:1], 1.0 / N_NODES, None, ALU.mult))
            step(V.tensor_scalar(hcf, hf, bn[:, 1:2], None, ALU.subtract))
            zero_padding(hc_al)
            step(V.tensor_tensor(hf, hcf, hcf, ALU.mult))
            V.tensor_reduce(bn[:, 2:3], hf, AX.X, ALU.add).then_inc(sum_in[1], 1)
            vec.wait_ge(sum_out[1], 1)
            V.tensor_scalar(bn[:, 3:4], p_hid[1][:, 0:1], 1.0 / N_NODES, LN_EPS, ALU.mult, ALU.add).then_inc(root_in[1], 1)
            vec.wait_ge(root_out[1], 1)
            step(V.reciprocal(bn[:, 4:5], bn[:, 3:4]))
            V.tensor_tensor(bn[:, 5:6], bn[:, 4:5], bn_vec[:, 1:2], ALU.mult).then_inc(bn_ready, 1)
            vec.wait_ge(u_ready, 1)
            V.tensor_copy(al[:, :], misc[:, 0:NB]).then_inc(u_sb, 1)
            vec.wait_ge(nl_ready[3], 1)
            w = (NT - 1) * LO
            V.tensor_tensor(y_n[:, 0:w, :], p_ref[0][:, 0:w * D].rearrange("p (c f) -> p c f", f=D), d1[:, 0:w, :], ALU.mult)
            V.tensor_tensor(y_n[0:TAIL, w:w + LO, :], p_ref[0][0:TAIL, w * D:(w + LO) * D].rearrange("p (c f) -> p c f", f=D),
                            d1[0:TAIL, w:w + LO, :], ALU.mult).then_inc(tab_ready[2], 1)
            vec.wait_ge(tab_ready[2], 1)
            aggregate(1)
            to_nodes(2)
            step(V.tensor_tensor(s_n[:, :, :], s_n[:, :, :], y_n[:, :, :], ALU.add))
            step(V.tensor_tensor(s_n[:, :, :], s_n[:, :, :], d1, ALU.mult))
            step(V.tensor_tensor(s_n[:, :, :], s_n[:, :, :],
                                 bias_out[:, :].unsqueeze(1).to_broadcast([P, NT * LO, D]), ALU.add))
            step(V.tensor_tensor(s_n[:, :, :], s_n[:, :, :], x1_n[:, :, :], ALU.add))
            layer_norm(2, s_n, out_ready)

        @block.tensor
        def _(pe):
            M = nc.tensor.matmul
            pe.wait_ge(idx_rows, 1)
            for s in range(2):
                for t in range(RT):
                    r = min(P, NCH - t * P)
                    ins = nc.tensor.transpose(banks[1 + 2 * s + t // 4][:, (t % 4) * P:(t % 4) * P + r],
                                              rows_f[0:r, s, t, :], ident[0:r, 0:r])
            ins.then_inc(idx_cols, 1)
            M(misc[0:NQ, 0:2 * QLO], zeros[:, 0:NQ], zeros[:, 0:2 * QLO], start=True, stop=False, skip_group_check=True)
            for s in range(2):
                pe.sem_inc(hist_used[s], 1)
            with pe.Fori(0, NCH // HG) as i:
                for s in range(2):
                    pe.wait_ge(oh_hist[s], i + 1)
                    for c in range(HG):
                        ins = M(misc[0:NQ, s * QLO:(s + 1) * QLO], oh_p[:, s, :, c], oh_q[:, s, :, c], start=False, stop=False,
                                skip_group_check=True)
                    ins.then_inc(hist_used[s], 1)
            M(misc[0:NQ, 0:2 * QLO], zeros[:, 0:NQ], zeros[:, 0:2 * QLO], start=False, stop=True,
              skip_group_check=True).then_inc(hist_done, 1)

            def front(n, u):
                pe.wait_ge(gathered[u], n * (16 * 2 * G))
                pe.nop(nofuse=True)
                for c in range(G):
                    ins = nc.tensor.transpose(p_tr[u][0:64, c * P:(c + 1) * P],
                                              g_xy[:, u, c, :, :].rearrange("p s f -> p (s f)"), ident)
                ins.then_inc(turned[u], 1)
                pe.wait_ge(x_ready[u], n)
                M(p_hid[u][:, :], w_hid[:, :], xT[:, u, :], start=True, stop=True).then_inc(pre_ready[u], 1)
                pe.wait_ge(v_taken[u], n)
                pe.wait_ge(hid_ready[u], n)
                for c in range(G):
                    ins = M(p_ref[u][:, c * 2 * D:(c + 1) * 2 * D], hidT[:, u, c * P:(c + 1) * P], w_ref[:, :],
                            start=True, stop=True)
                ins.then_inc(ref_ready[u], 1)

            def scatter(n, u, i):
                pe.wait_ge(m_ready[u], n)
                for c in range(2 * G):
                    k = u * 2 * G + c
                    r = k % RING
                    pe.wait_ge(oh_ready[r], i * (2 * 2 * G // RING) + k // RING + 1)
                    ins = M(acc[:, 0:NB], m8[:, u, c, :, :].rearrange("p a f -> p (a f)"), oh_b[:, r, :],
                            start=False, stop=False, skip_group_check=True)
                    ins.then_inc(oh_used[r], 1)

            def clear():
                return M(acc[:, 0:NB], zeros[:, :], iota_b, start=True, stop=False, skip_group_check=True)

            def close(k):
                M(acc[:, 0:NB], zeros[:, :], iota_b, start=False, stop=True, skip_group_check=True).then_inc(acc_ready[k], 1)

            clear()
            for r in range(RING):
                pe.sem_inc(oh_used[r], 1)
            for u in range(2):
                pe.sem_inc(turned[u], 1)
                pe.sem_inc(v_taken[u], 1)
            front(1, 0)
            with pe.Fori(0, NG // 2 - 1) as i:
                front(i + 1, 1)
                scatter(i + 1, 0, i)
                front(i + 2, 0)
                scatter(i + 1, 1, i)
            n = NG // 2
            front(n, 1)
            scatter(n, 0, n - 1)
            scatter(n, 1, n - 1)
            close(0)

            def to_tiles(bank, src_t, done):
                for t in range(NT):
                    w = min(P, NB - t * P)
                    ins = nc.tensor.transpose(bank[0:w, t * P:(t + 1) * P], src_t[:, t * P:t * P + w], ident)
                ins.then_inc(done, 1)

            pe.wait_ge(al_ready[0], 1)
            to_tiles(misc, al, nl_ready[0])

            def aggregate(k):
                clear()
                for r in range(RING):
                    pe.sem_inc(l_ohu[k][r], 1)
                with pe.Fori(0, NG // 2) as i:
                    for u in range(2):
                        pe.wait_ge(l_ready[k][u], i + 1)
                        for c in range(G):
                            j = u * G + c
                            r = j % RING
                            pe.wait_ge(l_oh[k][r], i * (2 * G // RING) + j // RING + 1)
                            ins = M(acc[:, 0:NB], m8[:, u, c, :, :].rearrange("p a f -> p (a f)"), oh_b[:, r, :],
                                    start=False, stop=False, skip_group_check=True)
                            ins.then_inc(l_ohu[k][r], 1)
                close(k + 1)

            aggregate(0)
            pe.wait_ge(al_ready[1], 1)
            to_tiles(misc, al, nl_ready[1])
            pe.wait_ge(agg_ready, 1)
            for t in range(NT):
                w = min(P, NB - t * P)
                ins = nc.tensor.transpose(misc[:, t * P:t * P + w],
                                          s_n[0:w, t * LO:(t + 1) * LO, :].rearrange("p a f -> p (a f)"), ident[0:w, 0:w])
            ins.then_inc(al_ready[3], 1)
            pe.wait_ge(al_ready[4], 1)
            for h in range(2):
                ins = M(banks[1 + h][:, 0:NB], w1_diag[:, h, :], al[:, :], start=True, stop=True)
            ins.then_inc(h_ready, 1)
            for k, col in ((0, 0), (1, 2)):
                pe.wait_ge(sum_in[k], 1)
                M(p_hid[k][:, 0:1], same_unit, bn[:, col:col + 1], start=True, stop=True).then_inc(sum_out[k], 1)
            pe.wait_ge(relu_ready, 2)
            for h in range(2):
                ins = M(misc[:, 0:NB], w2_diag[:, h, :], h_al[:, h, :], start=(h == 0), stop=(h == 1))
            ins.then_inc(u_ready, 1)
            pe.wait_ge(u_sb, 1)
            to_tiles(p_ref[0], al, nl_ready[3])
            aggregate(1)
            pe.wait_ge(al_ready[2], 1)
            to_tiles(misc, al, nl_ready[2])


def kernel(**inputs):
    import numpy as _np
    import concourse.bacc as _bacc
    from concourse import mybir as _mybir
    from concourse.bass_utils import run_bass_kernel_spmd as _run

    nc = _bacc.Bacc("TRN2", target_bir_lowering=False, num_devices=1)
    shape_consts = _np.zeros((P, 2 * P + NB), _np.float32)
    shape_consts[:, 0:P] = _np.eye(P)
    shape_consts[:, P:2 * P] = _np.arange(P)[:, None] % HID1 == _np.arange(P)[None, :] % HID1
    shape_consts[:, 2 * P:] = _np.arange(NB)[None, :]
    given = {
        "x": inputs["x"], "src": inputs["src"], "dst": inputs["dst"],
        "w0_in": _np.asarray(inputs["L0_gnn_W1"]).T, "b0_in": inputs["L0_gnn_b1"],
        "w0_out": _np.asarray(inputs["L0_gnn_W2"]).T, "b0_out": inputs["L0_gnn_b2"],
        "w1": inputs["L1_gnn_W1"], "b1": inputs["L1_gnn_b1"], "gamma": inputs["L1_gnn_gamma"],
        "beta": inputs["L1_gnn_beta"], "w2": inputs["L1_gnn_W2"], "b2": inputs["L1_gnn_b2"],
        "shape_consts": shape_consts,
    }
    arrays, args = {}, []
    for name, a in given.items():
        a = _np.ascontiguousarray(a)
        arrays[f"in_{name}"] = a
        args.append(nc.dram_tensor(f"in_{name}", a.shape, _mybir.dt.from_np(a.dtype), kind="ExternalInput").ap())
    args.append(nc.dram_tensor("out_0", (N_NODES, D), F32, kind="ExternalOutput").ap())
    gnn(nc, *args)
    r = _run(nc, [arrays], core_ids=[0])
    return r.results[0]["out_0"]
```

```python
import concourse.bass as bass
from concourse import mybir
from contextlib import ExitStack

F32 = mybir.dt.float32
BF16 = mybir.dt.bfloat16
F16 = mybir.dt.float16
I32 = mybir.dt.int32
ALU = mybir.AluOpType
ACT = mybir.ActivationFunctionType
AX = mybir.AxisListType

P = 128
N_NODES = 3125
N_EDGES = 100000
D = 16
HID0 = 64
HID1 = 32
LO = 8
NB = -(-(N_NODES + 1) // LO)
NT = -(-NB // P)
TAIL = NB - (NT - 1) * P
PAD = N_NODES
QLO = 64
NQ = -(-(NB * LO) // QLO)
G = 4
NCH = -(-N_EDGES // (P * G)) * G
NG = NCH // G
RT = -(-NCH // P)
HG = 16
LN_EPS = 1e-5
WG = 32
WH = 16
NH = 2 * NG
LANES = 128
NHI = -(-NB * LO // LANES)
NKEY = NHI * WH
NA = NB * LO + WH
NBLK = 7
BLK = -(-NB * LO // NBLK)
WROW = 2 * HID0 + D
FRING = 8
MAX_COUNT = 256
KR = (N_NODES - (NT - 1) * P * LO) // LO


def gnn(nc, x, src, dst, w0_in, b0_in, w0_out, b0_out, w1, b1, gamma, beta, w2, b2, consts, out):
    with ExitStack() as ctx:
        def sb(name, shape, dt=F32):
            return ctx.enter_context(nc.sbuf_tensor(name, shape, dt))

        def sem(name):
            return ctx.enter_context(nc.semaphore(name))

        cst = sb("cst", [P, 2 * P + 1 + D + NKEY])
        ident = cst[:, 0:P]
        same_unit = cst[:, P:2 * P]
        lane32 = cst[:, 2 * P:2 * P + 1]
        same_feat = cst[:, 2 * P + 1:2 * P + 1 + D]
        iota_k = cst[:, 2 * P + 1 + D:]
        iota_b = iota_k[:, 0:NB]
        ones_col = iota_k[:, 1:2]
        h_base_i = sb("h_base_i", [P, 4], I32)
        g_base_i = sb("g_base_i", [P, 2], I32)
        h_base_f = sb("h_base_f", [P, 4])
        h_top = sb("h_top", [P, 4])
        g_top = sb("g_top", [P, 2])
        viol = sb("viol", [P, 8])
        flag = sb("flag", [1, 2], I32)
        g_base = sb("g_base", [P, NG], I32)
        h_base = sb("h_base", [P, NH], I32)
        key_f = sb("key_f", [P, NCH])
        lo_f = sb("lo_f", [P, NCH])
        iota_h = sb("iota_h", [P, NKEY], F16)
        zeros = sb("zeros", [P, P])
        w_hid = sb("w_hid", [64, 2 * HID0])
        w_ref = sb("w_ref", [2 * HID0, 2 * D])
        bias_hid = sb("bias_hid", [2 * HID0, 1])
        bias_ref = sb("bias_ref", [P, 2, D])
        bias_rep = sb("bias_rep", [P, G * 4, D])
        ones_row = sb("ones_row", [1, P])
        w1_diag = sb("w1_diag", [P, 2, P])
        w2_diag = sb("w2_diag", [P, 2, P])
        bn_vec = sb("bn_vec", [P, 3])
        bias_out = sb("bias_out", [P, D])
        dinv = sb("dinv", [P, 2, NT * LO])
        x_n = sb("x_n", [P, NT * LO, D])
        x1_n = sb("x1_n", [P, NT * LO, D])
        y_n = sb("y_n", [P, NT * LO, D])
        s_n = sb("s_n", [P, NT * LO, D])
        t_n = sb("t_n", [P, NT * LO, D])
        st = sb("st", [P, 4, NT * LO])
        al = sb("al", [P, NB])
        h_al = sb("h_al", [P, 2, NB])
        hc_al = sb("hc_al", [P, 2, NB])
        bn = sb("bn", [P, 8])
        stage = ExitStack()

        def esb(name, shape, dt=F32):
            return stage.enter_context(nc.sbuf_tensor(name, shape, dt))

        lo_stage = esb("lo_stage", [P, 8])
        oh_lo = esb("oh_lo", [P, 8, LANES], BF16)
        oh_key = esb("oh_key", [P, 8, NKEY], BF16)
        cnt_stage = esb("cnt_stage", [P, 4, NKEY], BF16)
        stage.close()
        y_hl = esb("y_hl", [P, NHI, D])
        r_hl = esb("r_hl", [P, NHI, D])
        y3 = esb("y3", [P, NHI, 3, D], BF16)
        agg3 = esb("agg3", [3 * D, NBLK * BLK])
        ctx.enter_context(stage.pop_all())
        room = ExitStack()
        stage = room
        node_i = esb("node_i", [P, 2, NCH], I32)
        a_f = esb("a_f", [P, 2, NCH])
        b_f = esb("b_f", [P, 2, NCH])
        dst_rel = esb("dst_rel", [P, NCH])
        lane_base = esb("lane_base", [P, NG])
        f_win = esb("f_win", [64, 4, WROW])
        stage = ExitStack()
        iota_q = esb("iota_q", [P, QLO, HG], BF16)
        cnt = esb("cnt", [P, 2, NT, LO])
        rows_i = esb("rows_i", [P, 2, RT, P], I32)
        rows_f = esb("rows_f", [P, 2, RT, P])
        dst_rows = esb("dst_rows", [P, 4, 2 * P], I32)
        part_i = esb("part_i", [P, 2, NCH], I32)
        q_bf = esb("q_bf", [P, 2, NCH], BF16)
        p_bf = esb("p_bf", [P, 2, NCH], BF16)
        oh_q = esb("oh_q", [P, 2, QLO, HG], BF16)
        oh_p = esb("oh_p", [P, 2, NQ, HG], BF16)
        hist = esb("hist", [NQ, 2, QLO])
        tab = esb("tab", [P, NT, LO, 2 * D])
        w_proj = esb("w_proj", [P, LO, 2 * HID0])
        xa = esb("xa", [P, NB])
        w_table = esb("w_table", [P, NT, LO, WROW])
        stage.close()
        idx_stage = esb("idx_stage", [P, 2, 2, G], I32)
        g_xy = esb("g_xy", [P, 2, G, 2, 2 * D])
        xT = esb("xT", [64, 2, G * P])
        hidT = esb("hidT", [P, 2, G * P])
        v = esb("v", [P, G * 2, D])
        prod = esb("prod", [P, G * 2, D])
        z = esb("z", [P, G, 2, D])
        msg = esb("msg", [P, 2, G * 2, D])
        n2 = esb("n2", [P, G * 2])
        cc = esb("cc", [P, G * 2])
        dots = esb("dots", [P, G * 2])
        oh_a = esb("oh_a", [P, 2, G * 2, LO])
        m8 = esb("m8", [P, 2, G * 2, LO, D])
        RING = 4
        oh_b = esb("oh_b", [P, RING, NB])
        stage.close()
        f_rows = esb("f_rows", [P, 2, 2 * G, 3 * D])
        f_xT = esb("f_xT", [64, 4, G * P])
        f_dst = esb("f_dst", [64, 4, G * P], I32)
        f_hid = esb("f_hid", [P, 2, G * P])
        f_sq = esb("f_sq", [P, 4 * G, D])
        f_prod = esb("f_prod", [P, 4 * G, D])
        f_z = esb("f_z", [P, 2 * G, 2, D])
        f_msg = esb("f_msg", [P, 2, 4 * G, D])
        f_n2 = esb("f_n2", [P, 4 * G])
        f_cc = esb("f_cc", [P, 4 * G])
        f_dots = esb("f_dots", [P, 4 * G])
        f_oha = esb("f_oha", [P, 2 * G, LO])
        f_m8 = esb("f_m8", [P, 2, 2 * G, LO, D])
        f_ohd = esb("f_ohd", [P, 2, 2 * G, WG])
        f_ohb = esb("f_ohb", [P, FRING, NB])
        f_stage = esb("f_stage", [P, 2, 2 * G], I32)
        acc_dst = esb("acc_dst", [D, NB * LO + WG])
        stage.close()
        room.close()
        counts = sb("counts", [P, NHI, NA], BF16)
        counts_f = counts[:, :, :].rearrange("p h n -> p (h n)").bitcast(F32)
        NZ = NHI * NA // 2
        ZP = NZ // 3
        hist_d = nc.dram_tensor("hist_d", (2, NQ * QLO), F32, kind="Internal").ap()
        table = [nc.dram_tensor(f"table{k}", (NB * LO, w), F32, kind="Internal").ap()
                 for k, w in enumerate((2 * D, D, D))]

        w_rows = nc.dram_tensor("w_rows", (NB * LO + WG, WROW), F32, kind="Internal").ap()
        dst_d = nc.dram_tensor("dst_d", (NCH * P,), I32, kind="Internal").ap()
        g_base_d = nc.dram_tensor("g_base_d", (NG,), I32, kind="Internal").ap()
        h_base_d = nc.dram_tensor("h_base_d", (NH,), I32, kind="Internal").ap()

        banks = [ctx.enter_context(nc.psum_tensor(f"bank{i}", [P, 512], F32)) for i in range(8)]
        acc = banks[0]
        p_tr = banks[1:3]
        p_hid = banks[3:5]
        p_ref = banks[5:7]
        misc = banks[7]

        loaded = sem("loaded")
        padded = sem("padded")
        dve = sem("dve_step")
        dve_fast = sem("dve_fast")
        dve_general = sem("dve_general")
        idx_rows = sem("idx_rows")
        idx_cols = sem("idx_cols")
        parts = sem("parts")
        oh_hist = [sem(f"oh_hist{s}") for s in range(2)]
        hist_used = [sem(f"hist_used{s}") for s in range(2)]
        hist_done = sem("hist_done")
        hist_sb = sem("hist_sb")
        hist_out = sem("hist_out")
        hist_in = sem("hist_in")
        deg_ready = sem("deg_ready")
        deg_root = sem("deg_root")
        tab_ready = [sem(f"tab_ready{k}") for k in range(3)]
        tab_out = [sem(f"tab_out{k}") for k in range(3)]
        staged = sem("staged")
        gathered = [sem(f"gathered{u}") for u in range(2)]
        g_free_dve = sem("g_free_dve")
        turned = sem("turned")
        x_ready = sem("x_ready")
        pre_ready = sem("pre_ready")
        hid_ready = sem("hid_ready")
        ref_ready = sem("ref_ready")
        v_taken = sem("v_taken")
        m_ready = sem("m_ready")
        oh_ready = sem("oh_ready")
        oh_used = sem("oh_used")
        l_staged = [sem(f"l_staged{k}") for k in range(2)]
        l_gathered = [[sem(f"l{k}_gathered{u}") for u in range(2)] for k in range(2)]
        l_free = [sem(f"l_free{k}") for k in range(2)]
        l_ready = [sem(f"l_ready{k}") for k in range(2)]
        l_oha = [sem(f"l{k}_oha") for k in range(2)]
        l_oh = [sem(f"l_oh{k}") for k in range(2)]
        l_ohu = [sem(f"l_ohu{k}") for k in range(2)]
        acc_ready = [sem(f"acc_ready{k}") for k in range(4)]
        al_ready = [sem(f"al_ready{k}") for k in range(5)]
        nl_ready = [sem(f"nl_ready{k}") for k in range(4)]
        root_in = [sem(f"root_in{k}") for k in range(3)]
        root_out = [sem(f"root_out{k}") for k in range(3)]
        agg_ready = sem("agg_ready")
        h_ready = sem("h_ready")
        sum_in = [sem(f"sum_in{k}") for k in range(2)]
        sum_out = [sem(f"sum_out{k}") for k in range(2)]
        bn_ready = sem("bn_ready")
        relu_ready = sem("relu_ready")
        u_ready = sem("u_ready")
        u_sb = sem("u_sb")
        out_ready = sem("out_ready")
        stored = sem("stored")

        base_ready = sem("base_ready")
        base_out = sem("base_out")
        base_in = sem("base_in")
        viol_ready = sem("viol_ready")
        viol_sum = sem("viol_sum")
        flag_ready = sem("flag_ready")
        xa_ps = sem("xa_ps")
        xa_sb = sem("xa_sb")
        proj_ps = sem("proj_ps")
        proj_sb = sem("proj_sb")
        proj_out = sem("proj_out")
        win_w = sem("win_w")
        f_in = [sem(f"f_in{q}") for q in range(4)]
        f_front = sem("f_front")
        f_staged = sem("f_staged")
        f_gath = [sem(f"f_gath{w}") for w in range(2)]
        f_free = sem("f_free")
        f_ohdt = sem("f_ohdt")
        f_turned = sem("f_turned")
        f_xready = sem("f_xready")
        f_pre = sem("f_pre")
        f_relu = sem("f_relu")
        f_ref = sem("f_ref")
        f_sqd = sem("f_sqd")
        f_sqr = sem("f_sqr")
        f_done = sem("f_done")
        f_mready = sem("f_mready")
        f_winps = sem("f_winps")
        f_oh = sem("f_oh")
        f_ohu = sem("f_ohu")
        f_wadd = sem("f_wadd")
        sp_act = [sem(f"sp_act{k}") for k in range(2)]
        dst_nl = sem("dst_nl")
        zeroed = sem("zeroed")
        c_los = sem("c_los")
        c_lo = sem("c_lo")
        c_key = sem("c_key")
        c_ps = sem("c_ps")
        dst_added = sem("dst_added")
        c_sb = sem("c_sb")
        c_added = sem("c_added")
        hl_in = [sem(f"hl_in{k}") for k in range(2)]
        y3_ready = [sem(f"y3_ready{k}") for k in range(2)]
        sp_ps = [sem(f"sp_ps{k}") for k in range(2)]
        sp_sb = [sem(f"sp_sb{k}") for k in range(2)]

        n_loads = 0
        block = ctx.enter_context(nc.Block())

        @block.sync
        def _(sync):
            nonlocal n_loads

            def load(dst_ap, src_ap):
                nonlocal n_loads
                n_loads += 1
                nc.sync.dma_start(dst_ap, src_ap).then_inc(loaded, 16)

            sync.wait_ge(padded, 1)
            full = N_EDGES // P
            for s, e in enumerate((src, dst)):
                load(rows_i[:, s, 0:RT - 1, :], e[0:(RT - 1) * P * P].rearrange("(t r e) -> r t e", r=P, e=P))
                last = full - (RT - 1) * P
                load(rows_i[0:last, s, RT - 1, :], e[(RT - 1) * P * P:full * P].rearrange("(r e) -> r e", e=P))
                load(rows_i[last:last + 1, s, RT - 1, 0:N_EDGES - full * P],
                     e[full * P:N_EDGES].rearrange("(r e) -> r e", r=1))
            load(cst[:, :], consts)
            per_row = 2 * G * P
            whole = N_EDGES // per_row
            load(dst_rows[0:whole, :, :].rearrange("p h e -> p (h e)"),
                 dst[0:whole * per_row].rearrange("(p e) -> p e", e=per_row))
            load(dst_rows[whole:whole + 1, :, :].rearrange("p h e -> p (h e)")[:, 0:N_EDGES - whole * per_row],
                 dst[whole * per_row:N_EDGES].rearrange("(p e) -> p e", p=1))
            for q in range(4):
                load(f_win[0:D, q, 0:HID0], w0_in[0:D, :])
                load(f_win[0:D, q, HID0:2 * HID0], w0_in[D:2 * D, :])
            for a in range(LO):
                load(w_proj[a * D:(a + 1) * D, a, 0:HID0], w0_in[D:2 * D, :])
                load(w_proj[a * D:(a + 1) * D, a, HID0:2 * HID0], w0_in[0:D, :])
            m = (NT - 1) * P * LO
            load(x_n[:, 0:(NT - 1) * LO, :].rearrange("p (t a) f -> p t (a f)", a=LO),
                 x[0:m, :].rearrange("(t b a) f -> b t (a f)", b=P, a=LO))
            k = (N_NODES - m) // LO
            load(x_n[0:k, (NT - 1) * LO:NT * LO, :].rearrange("p a f -> p (a f)"),
                 x[m:m + k * LO, :].rearrange("(b a) f -> b (a f)", a=LO))
            left = N_NODES - m - k * LO
            load(x_n[k:k + 1, (NT - 1) * LO:(NT - 1) * LO + left, :].rearrange("p a f -> p (a f)"),
                 x[m + k * LO:N_NODES, :].rearrange("(b a) f -> b (a f)", b=1))
            load(w_hid[0:D, 0:HID0], w0_in[0:D, :])
            load(w_hid[0:D, HID0:2 * HID0], w0_in[D:2 * D, :])
            load(w_hid[2 * D:3 * D, 0:HID0], w0_in[D:2 * D, :])
            load(w_hid[2 * D:3 * D, HID0:2 * HID0], w0_in[0:D, :])
            for s in range(2):
                load(w_ref[s * HID0:(s + 1) * HID0, s * D:(s + 1) * D], w0_out)
                load(bias_hid[s * HID0:(s + 1) * HID0, :], b0_in.unsqueeze(1))
                load(bias_ref[:, s, :], b0_out.unsqueeze(0).to_broadcast([P, D]))
            for a in range(LO):
                h, r = a // 4, a % 4
                load(w1_diag[a * D:(a + 1) * D, h, r * HID1:(r + 1) * HID1], w1)
                load(w2_diag[r * HID1:(r + 1) * HID1, h, a * D:(a + 1) * D], w2)
            for r in range(4):
                for j, vec in enumerate((b1, gamma, beta)):
                    load(bn_vec[r * HID1:(r + 1) * HID1, j:j + 1], vec.unsqueeze(1))
            load(bias_out[:, :], b2.unsqueeze(0).to_broadcast([P, D]))

            sync.wait_ge(base_ready, 1)
            nc.sync.dma_start(g_base_d.rearrange("(p h) -> p h", h=2), g_base_i[0:NG // 2, :]).then_inc(base_out, 16)
            nc.sync.dma_start(h_base_d.rearrange("(p h) -> p h", h=4), h_base_i[0:NG // 2, :]).then_inc(base_out, 16)
            nc.sync.dma_start(dst_d.rearrange("(p e) -> p e", p=NG // 2),
                              dst_rows[0:NG // 2, :, :].rearrange("p h e -> p (h e)")).then_inc(base_out, 16)
            sync.wait_ge(base_out, 48)
            nc.sync.dma_start(g_base[:, :], g_base_d.unsqueeze(0).to_broadcast([P, NG])).then_inc(base_in, 16)
            nc.sync.dma_start(h_base[:, :], h_base_d.unsqueeze(0).to_broadcast([P, NH])).then_inc(base_in, 16)

            sync.wait_ge(hist_sb, 1)
            nc.sync.dma_start(hist_d.rearrange("s (p q) -> p s q", q=QLO), hist[:, :, :]).then_inc(hist_out, 16)
            sync.wait_ge(hist_out, 16)
            for s in range(2):
                nc.sync.dma_start(cnt[:, s, 0:NT - 1, :],
                                  hist_d[s, 0:m].rearrange("(t b a) -> b t a", b=P, a=LO)).then_inc(hist_in, 16)
                nc.sync.dma_start(cnt[0:KR, s, NT - 1, :],
                                  hist_d[s, m:m + KR * LO].rearrange("(b a) -> b a", a=LO)).then_inc(hist_in, 16)
                nc.sync.dma_start(cnt[KR:KR + 1, s, NT - 1, 0:left],
                                  hist_d[s, m + KR * LO:N_NODES].rearrange("(b a) -> b a", b=1)).then_inc(hist_in, 16)

            def store_table(k, tile):
                sync.wait_ge(tab_ready[k], 1)
                nc.sync.dma_start(table[k][0:m, :].rearrange("(t b a) f -> b t (a f)", b=P, a=LO),
                                  tile[:, 0:NT - 1, :]).then_inc(tab_out[k], 16)
                nc.sync.dma_start(table[k][m:NB * LO, :].rearrange("(b a) f -> b (a f)", a=LO),
                                  tile[0:TAIL, NT - 1, :]).then_inc(tab_out[k], 16)

            store_table(0, tab[:, :, :, :].rearrange("p t a f -> p t (a f)"))
            sync.wait_ge(proj_sb, 1)
            wt = w_table[:, :, :, :].rearrange("p t a f -> p t (a f)")
            nc.sync.dma_start(w_rows[0:m, :].rearrange("(t b a) f -> b t (a f)", b=P, a=LO), wt[:, 0:NT - 1, :]).then_inc(proj_out, 16)
            nc.sync.dma_start(w_rows[m:NB * LO, :].rearrange("(b a) f -> b (a f)", a=LO), wt[0:TAIL, NT - 1, :]).then_inc(proj_out, 16)
            nc.sync.dma_start(w_rows[NB * LO:NB * LO + WG, :].rearrange("n (k f) -> n k f", k=2),
                              zeros[0:WG, 0:WROW // 2].unsqueeze(1).to_broadcast([WG, 2, WROW // 2])).then_inc(proj_out, 16)
            sync.wait_ge(proj_out, 48)
            sync.wait_ge(flag_ready, 1)
            fast = sync.value_load(flag[0:1, 0:1], min_val=0, max_val=1)
            with sync.If(fast > 0):
                with sync.Fori(0, NG // 4) as i:
                    for q in range(4):
                        sync.wait_ge(f_front, i * 4 + q + 1)
                        sync.nop(nofuse=True)
                        base = sync.value_load(g_base[0:1, bass.ds(i * 4 + q, 1)], min_val=0, max_val=NB * LO - 1)
                        nc.sync.dma_start(f_win[32:64, q, :], w_rows[bass.ds(base, WG), :]).then_inc(f_in[q], 16)
                        nc.sync.dma_start(f_dst[32:64, q, :],
                                          dst_d[bass.ds(i * (4 * G * P) + q * G * P, G * P)].unsqueeze(0)
                                          .to_broadcast([WG, G * P])).then_inc(f_in[q], 16)

            for k in (1, 2):
                store_table(k, y_n[:, :, :].rearrange("p (t a) f -> p t (a f)", a=LO))
                with sync.If(fast > 0):
                    sync.wait_ge(tab_out[k], 32)
                    nc.sync.dma_start(y_hl[:, 0:NHI - 1, :],
                                      table[k][0:(NHI - 1) * LANES, :].rearrange("(h l) f -> l h f", l=LANES)).then_inc(hl_in[k - 1], 16)
                    nc.sync.dma_start(y_hl[0:NB * LO - (NHI - 1) * LANES, NHI - 1, :],
                                      table[k][(NHI - 1) * LANES:NB * LO, :]).then_inc(hl_in[k - 1], 16)
            sync.wait_ge(out_ready, 1)
            nc.sync.dma_start(out[0:m, :].rearrange("(t b a) f -> b t (a f)", b=P, a=LO),
                              s_n[:, 0:(NT - 1) * LO, :].rearrange("p (t a) f -> p t (a f)", a=LO)).then_inc(stored, 16)
            nc.sync.dma_start(out[m:m + KR * LO, :].rearrange("(b a) f -> b (a f)", a=LO),
                              s_n[0:KR, (NT - 1) * LO:NT * LO, :].rearrange("p a f -> p (a f)")).then_inc(stored, 16)
            nc.sync.dma_start(out[m + KR * LO:N_NODES, :].rearrange("(b a) f -> b (a f)", b=1),
                              s_n[KR:KR + 1, (NT - 1) * LO:(NT - 1) * LO + left, :]
                              .rearrange("p a f -> p (a f)")).then_inc(stored, 16)
            sync.wait_ge(stored, 48)

        LOADED = 16 * n_loads

        @block.gpsimd
        def _(pool):
            pool.wait_ge(parts, 1)
            pool.wait_ge(tab_out[0], 32)
            pool.wait_ge(flag_ready, 1)
            pool.wait_ge(proj_out, 48)
            fast = pool.value_load(flag[0:1, 0:1], min_val=0, max_val=1)
            with pool.If(fast > 0):
                for w in range(2):
                    pool.sem_inc(f_free, 1)
                with pool.Fori(0, NG // 4) as i:
                    for w in range(2):
                        pool.wait_ge(f_free, i * 2 + w + 1)
                        nc.gpsimd.tensor_copy(f_stage[:, w, :],
                                              node_i[:, 0, bass.ds(i * (4 * G) + w * 2 * G, 2 * G)]).then_inc(f_staged, 1)
                        pool.wait_ge(f_staged, i * 2 + w + 1)
                        pool.nop(nofuse=True)
                        for c in range(2 * G):
                            nc.gpsimd.indirect_dma_start(
                                out=f_rows[:, w, c, 0:2 * D], out_offset=None, in_=table[0],
                                in_offset=bass.IndirectOffsetOnAxis(ap=f_stage[:, w, c:c + 1], axis=0)
                            ).then_inc(f_gath[w], 16)
                pool.wait_ge(acc_ready[3], 1)
                pool.wait_ge(dst_added, 1)
                nc.gpsimd.memset(counts_f[:, 0:ZP], 0.0).then_inc(zeroed, 1)
                for _ in range(8):
                    pool.sem_inc(c_lo, 1)
                with pool.Fori(0, NCH // 8) as i:
                    pool.wait_ge(c_lo, i * 8 + 8)
                    pool.nop(nofuse=True)
                    nc.gpsimd.tensor_copy(lo_stage[:, :], lo_f[:, bass.ds(i * 8, 8)]).then_inc(c_los, 1)
                    pool.wait_ge(c_los, i + 1)
                    pool.nop(nofuse=True)
                    for r in range(8):
                        if r % 2 == 0:
                            pool.wait_ge(c_ps, i * 4 + r // 2 + 1)
                            pool.nop(nofuse=True)
                        nc.gpsimd.tensor_scalar(oh_lo[:, r, :], iota_k[:, 0:LANES], lo_stage[:, r:r + 1], None,
                                                ALU.is_equal).then_inc(c_lo, 1)
            with pool.Else():
                for u in range(2):
                    pool.sem_inc(g_free_dve, 1)
                with pool.Fori(0, NG // 2) as i:
                    for u in range(2):
                        pool.wait_ge(turned, 2 * i + u + 1)
                        nc.gpsimd.tensor_copy(idx_stage[:, u, :, :],
                                              node_i[:, :, bass.ds(i * (2 * G) + u * G, G)]).then_inc(staged, 1)
                        pool.wait_ge(staged, 2 * i + u + 1)
                        pool.nop(nofuse=True)
                        pool.wait_ge(g_free_dve, 2 * i + u + 1)
                        pool.nop(nofuse=True)
                        for c in range(G):
                            for s in range(2):
                                nc.gpsimd.indirect_dma_start(
                                    out=g_xy[:, u, c, s, :], out_offset=None, in_=table[0],
                                    in_offset=bass.IndirectOffsetOnAxis(ap=idx_stage[:, u, s, c:c + 1], axis=0)
                                ).then_inc(gathered[u], 16)
                for k in range(2):
                    pool.wait_ge(tab_out[k + 1], 32)
                    for u in range(2):
                        pool.sem_inc(l_free[k], 1)
                    with pool.Fori(0, NG // 2) as i:
                        for u in range(2):
                            pool.wait_ge(l_free[k], 2 * i + u + 1)
                            nc.gpsimd.tensor_copy(idx_stage[:, u, 0, :],
                                                  node_i[:, 0, bass.ds(i * (2 * G) + u * G, G)]).then_inc(l_staged[k], 1)
                            pool.wait_ge(l_staged[k], 2 * i + u + 1)
                            pool.nop(nofuse=True)
                            for c in range(G):
                                nc.gpsimd.indirect_dma_start(
                                    out=g_xy[:, u, c, 0, 0:D], out_offset=None, in_=table[k + 1],
                                    in_offset=bass.IndirectOffsetOnAxis(ap=idx_stage[:, u, 0, c:c + 1], axis=0)
                                ).then_inc(l_gathered[k][u], 16)

        @block.scalar
        def _(act):
            act.wait_ge(deg_ready, 1)
            nc.scalar.activation(dinv[:, :, :], dinv[:, :, :], ACT.Sqrt).then_inc(deg_root, 1)

            def front(n, u):
                act.wait_ge(turned, 2 * n + u + 1)
                nc.scalar.activation(xT[:, u, :], p_tr[u][0:64, :], ACT.Copy).then_inc(x_ready, 1)
                act.wait_ge(pre_ready, 2 * n + u - 1)
                nc.scalar.activation(hidT[:, u, :], p_hid[u][:, :], ACT.Relu,
                                     bias=bias_hid[:, 0:1]).then_inc(hid_ready, 1)

            act.wait_ge(loaded, LOADED)
            act.wait_ge(xa_ps, 1)
            nc.scalar.activation(xa[:, :], misc[:, 0:NB], ACT.Copy).then_inc(xa_sb, 1)
            for t in range(NT):
                w = min(P, NB - t * P)
                for h in range(2):
                    act.wait_ge(proj_ps, 2 * t + h + 1)
                    nc.scalar.activation(w_table[0:w, t, 4 * h:4 * h + 4, 0:2 * HID0],
                                         p_tr[h][0:w, :].rearrange("p (a n) -> p a n", a=4), ACT.Copy).then_inc(win_w, 1)

            act.wait_ge(flag_ready, 1)
            act.wait_ge(proj_out, 48)
            act.wait_ge(tab_out[0], 32)
            fast = act.value_load(flag[0:1, 0:1], min_val=0, max_val=1)

            def fast_front(i, w):
                for gg in range(2):
                    q = 2 * w + gg
                    act.wait_ge(f_turned, i * 4 + q + 1)
                    nc.scalar.activation(f_xT[0:32, q, :], p_tr[gg][0:32, :], ACT.Copy).then_inc(f_xready, 1)
                    act.wait_ge(f_pre, i * 4 + q + 1)
                    nc.scalar.activation(f_hid[:, gg, :], p_hid[gg][:, :], ACT.Relu,
                                         bias=bias_hid[:, 0:1]).then_inc(f_relu, 1)
                act.wait_ge(f_ref, i * 2 + w + 1)
                nc.scalar.activation(f_rows[:, w, :, 2 * D:3 * D],
                                     p_ref[w][:, 4 * G * D:6 * G * D].rearrange("p (c f) -> p c f", f=D), ACT.Copy).then_inc(f_sqr, 1)
                act.wait_ge(f_sqd, i * 2 + w + 1)
                nc.scalar.activation(f_sq[:, :, :], p_ref[w][:, 0:4 * G * D].rearrange("p (c f) -> p c f", f=D),
                                     ACT.Square).then_inc(f_sqr, 1)

            with act.If(fast > 0):
                with act.Fori(0, NG // 4) as i:
                    fast_front(i, 0)
                    fast_front(i, 1)
                with act.Fori(0, NH // 4) as i:
                    for r in range(4):
                        act.wait_ge(c_ps, i * 4 + r + 5)
                        act.nop(nofuse=True)
                        act.wait_ge(c_added, i * 4 + r + 1)
                        nc.scalar.activation(cnt_stage[:, r, :], banks[1 + r][:, 0:NKEY], ACT.Copy).then_inc(c_sb, 1)
            with act.Else():
                with act.Fori(0, NG // 2) as i:
                    front(i + 1, 0)
                    front(i + 1, 1)

            def root(k):
                act.wait_ge(root_in[k], 1)
                nc.scalar.activation(st[:, 2, :], st[:, 2, :], ACT.Sqrt).then_inc(root_out[k], 1)

            def product(k):
                with act.If(fast > 0):
                    for blk in range(1, NBLK, 2):
                        act.wait_ge(sp_ps[k], blk + 1)
                        nc.scalar.activation(agg3[:, blk * BLK:(blk + 1) * BLK], banks[blk][0:3 * D, 0:BLK],
                                             ACT.Copy).then_inc(sp_act[k], 1)

            root(0)
            product(0)
            act.wait_ge(root_in[1], 1)
            nc.scalar.activation(bn[:, 3:4], bn[:, 3:4], ACT.Sqrt).then_inc(root_out[1], 1)
            act.wait_ge(bn_ready, 1)
            for h in range(2):
                nc.scalar.activation(h_al[:, h, :], hc_al[:, h, :], ACT.Relu, scale=bn[:, 5:6],
                                     bias=bn_vec[:, 2:3]).then_inc(relu_ready, 1)
            product(1)
            root(2)

        @block.vector
        def _(vec):
            counted = {dve: 0, dve_fast: 0, dve_general: 0}

            def step(ins, at=None, on=dve):
                counted[on] += 1
                ins.then_inc(on, 1)
                vec.wait_ge(on, counted[on] if at is None else at[0] * at[1] + counted[on])

            V = nc.vector
            for tile, value in ((rows_i, PAD), (x_n, 0.0), (w_hid, 0.0), (w_ref, 0.0), (w1_diag, 0.0), (w2_diag, 0.0),
                                (cnt, 0.0), (zeros, 0.0), (ones_row, 1.0), (dst_rows, PAD), (f_win, 0.0),
                                (w_proj, 0.0), (viol, 0.0), (tab, 0.0), (s_n, 0.0)):
                ins = V.memset(tile[tuple(slice(None) for _ in tile.shape)], value)
            ins.then_inc(padded, 1)
            vec.wait_ge(padded, 1)
            vec.wait_ge(loaded, LOADED)
            V.tensor_copy(rows_f[:, :, :, :], rows_i[:, :, :, :]).then_inc(idx_rows, 1)
            step(V.tensor_copy(iota_q[:, :, :], iota_b[:, 0:QLO].unsqueeze(2).to_broadcast([P, QLO, HG])))
            halves = NG // 2
            step(V.tensor_reduce(h_base_i[0:halves, :], dst_rows[0:halves, :, :], AX.X, ALU.min))
            V.tensor_reduce(h_top[0:halves, :], dst_rows[0:halves, :, :], AX.X, ALU.max)
            step(V.tensor_scalar(h_base_i[0:halves, :], h_base_i[0:halves, :], -2, None, ALU.bitwise_and))
            step(V.tensor_copy(h_base_f[0:halves, :], h_base_i[0:halves, :]))
            hb = h_base_f[0:halves, :].rearrange("p (g h) -> p g h", h=2)
            ht = h_top[0:halves, :].rearrange("p (g h) -> p g h", h=2)
            V.tensor_tensor(g_top[0:halves, :], ht[:, :, 0], ht[:, :, 1], ALU.max)
            V.tensor_tensor(g_base_i[0:halves, :], hb[:, :, 0], hb[:, :, 1], ALU.min).then_inc(base_ready, 1)
            vec.wait_ge(base_ready, 1)
            V.tensor_tensor(viol[0:halves, 0:4], h_top[0:halves, :], h_base_f[0:halves, :], ALU.subtract)
            step(V.tensor_tensor(viol[0:halves, 4:6], g_top[0:halves, :], g_base_i[0:halves, :], ALU.subtract))
            step(V.tensor_scalar(viol[0:halves, 0:4], viol[0:halves, 0:4], float(WH), None, ALU.is_ge))
            step(V.tensor_scalar(viol[0:halves, 4:6], viol[0:halves, 4:6], float(WG), None, ALU.is_ge))
            vec.wait_ge(idx_cols, 1)
            for s in range(2):
                for t in range(2):
                    w = min(4 * P, NCH - t * 4 * P)
                    ins = V.tensor_copy(node_i[:, s, t * 4 * P:t * 4 * P + w], banks[1 + 2 * s + t][:, 0:w])
            step(ins)
            for mask, shift, to in ((LO - 1, None, a_f), (None, 3, b_f), (QLO - 1, None, q_bf), (None, 6, p_bf)):
                if shift is None:
                    step(V.tensor_scalar(part_i[:, :, :], node_i[:, :, :], mask, None, ALU.bitwise_and))
                else:
                    step(V.tensor_scalar(part_i[:, :, :], node_i[:, :, :], shift, None, ALU.logical_shift_right))
                step(V.tensor_copy(to[:, :, :], part_i[:, :, :]))
            step(V.tensor_scalar(part_i[:, 0, :], node_i[:, 0, :], LANES - 1, None, ALU.bitwise_and))
            step(V.tensor_copy(lo_f[:, :], part_i[:, 0, :]))
            step(V.tensor_scalar(part_i[:, 0, :], node_i[:, 0, :], 7, None, ALU.logical_shift_right))
            vec.wait_ge(base_in, 32)
            step(V.tensor_tensor(dst_rel[:, :].rearrange("p (h c) -> p h c", c=2),
                                 node_i[:, 1, :].rearrange("p (h c) -> p h c", c=2),
                                 h_base[:, :].unsqueeze(2).to_broadcast([P, NH, 2]), ALU.subtract))
            step(V.scalar_tensor_tensor(key_f[:, :], part_i[:, 0, :], float(WH), dst_rel[:, :], ALU.mult, ALU.add))
            step(V.tensor_tensor(dst_rel[:, :].rearrange("p (g c) -> p g c", c=G),
                                 node_i[:, 1, :].rearrange("p (g c) -> p g c", c=G),
                                 g_base[:, :].unsqueeze(2).to_broadcast([P, NG, G]), ALU.subtract))
            step(V.tensor_scalar(lane_base[:, :], g_base[:, :], lane32, None, ALU.add))
            step(V.tensor_copy(iota_h[:, :], iota_k))
            V.tensor_copy(part_i[:, 0, 0:1], node_i[:, 0, 0:1]).then_inc(parts, 1)
            with vec.Fori(0, NCH // HG) as i:
                for s in range(2):
                    vec.wait_ge(hist_used[s], i + 1)
                    V.tensor_tensor(oh_q[:, s, :, :], q_bf[:, s, bass.ds(i * HG, HG)].unsqueeze(1).to_broadcast([P, QLO, HG]),
                                    iota_q[:, :, :], ALU.is_equal)
                    V.tensor_tensor(oh_p[:, s, :, :], p_bf[:, s, bass.ds(i * HG, HG)].unsqueeze(1).to_broadcast([P, NQ, HG]),
                                    iota_q[:, 0:NQ, :], ALU.is_equal).then_inc(oh_hist[s], 1)
            vec.wait_ge(hist_done, 1)
            V.tensor_copy(hist[:, :, :], misc[0:NQ, 0:2 * QLO].rearrange("p (s q) -> p s q", s=2)).then_inc(hist_sb, 1)
            vec.wait_ge(hist_in, 96)
            c2 = cnt[:, :, :, :].rearrange("p s t a -> p s (t a)")
            step(V.tensor_reduce(viol[:, 6:7], c2[:, 1, :], AX.X, ALU.max))
            step(V.tensor_scalar(viol[:, 6:7], viol[:, 6:7], MAX_COUNT + 0.5, None, ALU.is_ge))
            V.tensor_reduce(viol[:, 7:8], viol[:, 0:7], AX.X, ALU.add).then_inc(viol_ready, 1)
            step(V.tensor_tensor(dinv[:, 0, :], c2[:, 0, :], c2[:, 1, :], ALU.add))
            V.tensor_scalar(dinv[:, 0, :], dinv[:, 0, :], 1e-5, None, ALU.max)
            V.tensor_scalar(dinv[:, 1, :], c2[:, 1, :], 1.0, None, ALU.add).then_inc(deg_ready, 1)
            vec.wait_ge(deg_root, 1)
            step(V.reciprocal(dinv[:, :, :], dinv[:, :, :]))
            d0 = dinv[:, 0, :].unsqueeze(2).to_broadcast([P, NT * LO, D])
            d1 = dinv[:, 1, :].unsqueeze(2).to_broadcast([P, NT * LO, D])
            tabv = tab[:, :, :, :].rearrange("p t a f -> p (t a) f")
            V.tensor_copy(tabv[:, :, 0:D], x_n[:, :, :])
            V.tensor_tensor(tabv[:, :, D:2 * D], x_n[:, :, :], d0, ALU.mult).then_inc(tab_ready[0], 1)
            vec.wait_ge(win_w, 2 * NT)
            V.tensor_tensor(w_table[:, :, :, 2 * HID0:].rearrange("p t a f -> p (t a) f"),
                            x_n[:, :, :], d0, ALU.mult).then_inc(proj_sb, 1)
            vec.wait_ge(viol_sum, 1)
            V.tensor_scalar(flag[0:1, 0:1], p_hid[0][0:1, 0:1], 0.5, None, ALU.is_le).then_inc(flag_ready, 1)
            vec.wait_ge(flag_ready, 1)
            vec.wait_ge(proj_out, 48)
            vec.wait_ge(tab_out[0], 32)
            fast = vec.value_load(flag[0:1, 0:1], min_val=0, max_val=1)

            def bcast(t):
                return t.unsqueeze(2).to_broadcast([P, G * 2, D])

            def reflect(n, u, at):
                vec.wait_ge(ref_ready, 2 * n + u - 1)
                ins = V.tensor_tensor(v[:, :, :], p_ref[u][:, 0:G * 2 * D].rearrange("p (c f) -> p c f", f=D),
                                      bias_rep[:, 0:2 * G, :], ALU.add)
                ins.then_inc(v_taken, 1)
                vec.wait_ge(v_taken, 2 * n + u + 1)
                step(V.tensor_tensor(prod[:, :, :], v[:, :, :], v[:, :, :], ALU.mult), at, dve_general)
                step(V.tensor_reduce(n2[:, :], prod[:, :, :], AX.X, ALU.add), at, dve_general)
                step(V.tensor_scalar(n2[:, :], n2[:, :], 1e-24, 0.5, ALU.max, ALU.mult), at, dve_general)
                step(V.reciprocal(cc[:, :], n2[:, :]), at, dve_general)
                vec.wait_ge(gathered[u], n * (16 * 2 * G))
                y = g_xy[:, u, :, :, D:2 * D].rearrange("p c s f -> p (c s) f")
                step(V.tensor_tensor(prod[:, :, :], v[:, :, :], y, ALU.mult), at, dve_general)
                step(V.tensor_reduce(dots[:, :], prod[:, :, :], AX.X, ALU.add), at, dve_general)
                step(V.tensor_tensor(dots[:, :], dots[:, :], cc[:, :], ALU.mult), at, dve_general)
                step(V.tensor_tensor(prod[:, :, :], v[:, :, :], bcast(dots[:, :]), ALU.mult), at, dve_general)
                for s in range(2):
                    ins = V.tensor_tensor(z[:, :, 1 - s, :], g_xy[:, u, :, s, D:2 * D],
                                          prod[:, :, :].rearrange("p (c s) f -> p c s f", s=2)[:, :, s, :], ALU.subtract)
                ins.then_inc(g_free_dve, 1)
                vec.wait_ge(g_free_dve, 2 * n + u + 1)
                zz = z[:, :, :, :].rearrange("p c s f -> p (c s) f")
                step(V.tensor_tensor(prod[:, :, :], v[:, :, :], zz, ALU.mult), at, dve_general)
                step(V.tensor_reduce(dots[:, :], prod[:, :, :], AX.X, ALU.add), at, dve_general)
                step(V.tensor_tensor(dots[:, :], dots[:, :], cc[:, :], ALU.mult), at, dve_general)
                step(V.tensor_tensor(prod[:, :, :], v[:, :, :], bcast(dots[:, :]), ALU.mult), at, dve_general)
                V.tensor_tensor(msg[:, u, :, :], zz, prod[:, :, :], ALU.subtract)
                for s in range(2):
                    ins = V.tensor_tensor(oh_a[:, u, :, :].rearrange("p (c s) a -> p c s a", s=2)[:, :, s, :],
                                          a_f[:, s, bass.ds(at[2], G)].unsqueeze(2).to_broadcast([P, G, LO]),
                                          iota_b[:, 0:LO].unsqueeze(1).to_broadcast([P, G, LO]), ALU.is_equal)
                step(ins, at, dve_general)
                V.tensor_tensor(m8[:, u, :, :, :], oh_a[:, u, :, :].unsqueeze(3).to_broadcast([P, G * 2, LO, D]),
                                msg[:, u, :, :].unsqueeze(2).to_broadcast([P, G * 2, LO, D]),
                                ALU.mult).then_inc(m_ready, 1)

            def one_hots(n, r0, sides, chunk, ready, used):
                for c in range(G):
                    for s in sides:
                        r = r0 % RING
                        vec.wait_ge(used, n + r0)
                        V.tensor_scalar(oh_b[:, r, :], iota_b, b_f[:, s, bass.ds(chunk + c, 1)], None,
                                        ALU.is_equal).then_inc(ready, 1)
                        r0 += 1
                return r0

            step(V.tensor_copy(bias_rep[:, :, :].rearrange("p (g s) f -> p g (s f)", s=2),
                               bias_ref[:, :, :].rearrange("p s f -> p (s f)").unsqueeze(1).to_broadcast([P, 2 * G, 2 * D])))

            def fb(t):
                return t.unsqueeze(2).to_broadcast([P, 4 * G, D])

            def dst_one_hots(i, w):
                for gg in range(2):
                    q = 2 * w + gg
                    vec.wait_ge(f_in[q], i * 32 + 32)
                    V.tensor_scalar(f_xT[32:64, q, :], f_dst[32:64, q, :], lane_base[32:64, bass.ds(i * 4 + q, 1)], None,
                                    ALU.is_equal).then_inc(f_ohdt, 1)

            def add_windows(i, w):
                vec.wait_ge(f_winps, i * 2 + w + 1)
                for gg in range(2):
                    base = vec.value_load(g_base[0:1, bass.ds(i * 4 + 2 * w + gg, 1)], min_val=0, max_val=NB * LO - 1)
                    k = 2 * w + gg
                    V.tensor_tensor(acc_dst[:, bass.ds(base, WG)], acc_dst[:, bass.ds(base, WG)],
                                    misc[0:D, k * WG:(k + 1) * WG], ALU.add).then_inc(f_wadd, 1)
                    vec.wait_ge(f_wadd, i * 4 + 2 * w + gg + 1)

            def fast_pair(i, w, after, adds, at):
                if after is not None:
                    dst_one_hots(*after)
                vec.wait_ge(f_sqr, i * 4 + 2 * w + 2)
                V.tensor_reduce(f_n2[:, :], f_sq[:, :, :], AX.X, ALU.add).then_inc(f_sqd, 1)
                vec.wait_ge(f_sqd, i * 2 + w + 2)
                step(V.tensor_scalar(f_n2[:, :], f_n2[:, :], 1e-24, 0.5, ALU.max, ALU.mult), at, dve_fast)
                V.reciprocal(f_cc[:, :], f_n2[:, :])
                v_ps = p_ref[w][:, 0:4 * G * D].rearrange("p (c f) -> p c f", f=D)
                y_all = f_rows[:, w, :, D:3 * D]
                step(V.tensor_tensor(f_prod[:, :, :].rearrange("p (c s) f -> p c (s f)", s=2),
                                     p_ref[w][:, 0:4 * G * D].rearrange("p (c n) -> p c n", n=2 * D), y_all, ALU.mult), at, dve_fast)
                step(V.tensor_reduce(f_dots[:, :], f_prod[:, :, :], AX.X, ALU.add), at, dve_fast)
                step(V.tensor_tensor(f_dots[:, :], f_dots[:, :], f_cc[:, :], ALU.mult), at, dve_fast)
                step(V.tensor_tensor(f_prod[:, :, :], v_ps, fb(f_dots[:, :]), ALU.mult), at, dve_fast)
                for s in range(2):
                    ins = V.tensor_tensor(f_z[:, :, 1 - s, :], f_rows[:, w, :, (1 + s) * D:(2 + s) * D],
                                          f_prod[:, :, :].rearrange("p (c s) f -> p c s f", s=2)[:, :, s, :], ALU.subtract)
                ins.then_inc(f_free, 1)
                vec.wait_ge(f_free, i * 2 + w + 3)
                zz = f_z[:, :, :, :].rearrange("p c s f -> p (c s) f")
                step(V.tensor_tensor(f_prod[:, :, :], v_ps, zz, ALU.mult), at, dve_fast)
                step(V.tensor_reduce(f_dots[:, :], f_prod[:, :, :], AX.X, ALU.add), at, dve_fast)
                step(V.tensor_tensor(f_dots[:, :], f_dots[:, :], f_cc[:, :], ALU.mult), at, dve_fast)
                V.tensor_tensor(f_prod[:, :, :], v_ps, fb(f_dots[:, :]), ALU.mult).then_inc(f_done, 1)
                vec.wait_ge(f_done, i * 2 + w + 3)
                V.tensor_tensor(f_msg[:, w, :, :], zz, f_prod[:, :, :], ALU.subtract)
                chunk = i * (4 * G) + w * 2 * G
                V.tensor_tensor(f_ohd[:, w, :, :], dst_rel[:, bass.ds(chunk, 2 * G)].unsqueeze(2).to_broadcast([P, 2 * G, WG]),
                                iota_k[:, 0:WG].unsqueeze(1).to_broadcast([P, 2 * G, WG]), ALU.is_equal)
                step(V.tensor_tensor(f_oha[:, :, :], a_f[:, 0, bass.ds(chunk, 2 * G)].unsqueeze(2).to_broadcast([P, 2 * G, LO]),
                                     iota_k[:, 0:LO].unsqueeze(1).to_broadcast([P, 2 * G, LO]), ALU.is_equal), at, dve_fast)
                if adds is not None:
                    add_windows(*adds)
                V.tensor_tensor(f_m8[:, w, :, :, :], f_oha[:, :, :].unsqueeze(3).to_broadcast([P, 2 * G, LO, D]),
                                f_msg[:, w, :, :].rearrange("p (c s) f -> p c s f", s=2)[:, :, 0, :]
                                .unsqueeze(2).to_broadcast([P, 2 * G, LO, D]), ALU.mult).then_inc(f_mready, 1)
                for c in range(2 * G):
                    k = w * 2 * G + c
                    r = k % FRING
                    vec.wait_ge(f_ohu, i * (4 * G) + k + 1)
                    V.tensor_scalar(f_ohb[:, r, :], iota_b, b_f[:, 0, bass.ds(chunk + c, 1)], None,
                                    ALU.is_equal).then_inc(f_oh, 1)

            def nodes_from(bank, on):
                w = (NT - 1) * LO
                V.tensor_copy(s_n[:, 0:w, :], bank[:, 0:w * D].rearrange("p (c f) -> p c f", f=D))
                step(V.tensor_copy(s_n[0:TAIL, w:w + LO, :],
                                   bank[0:TAIL, w * D:(w + LO) * D].rearrange("p (c f) -> p c f", f=D)), on=on)

            def to_nodes(k):
                vec.wait_ge(acc_ready[k], 1)
                V.tensor_copy(al[:, :], acc[:, 0:NB]).then_inc(al_ready[k], 1)
                vec.wait_ge(nl_ready[k], 1)
                nodes_from(misc, dve_general)

            FSP = 9
            SPG = 13
            with vec.If(fast > 0):
                step(V.memset(acc_dst[:, :], 0.0), on=dve_fast)
                for _ in range(2):
                    vec.sem_inc(f_done, 1)
                vec.sem_inc(f_sqd, 1)
                dst_one_hots(0, 0)
                before = counted[dve_fast]
                fast_pair(0, 0, (0, 1), None, None)
                assert counted[dve_fast] == before + FSP
                before = counted[dve_fast]
                with vec.Fori(0, NG // 4 - 1) as i:
                    fast_pair(i, 1, (i + 1, 0), (i, 0), (i, 2 * FSP))
                    fast_pair(i + 1, 0, (i + 1, 1), (i, 1), (i, 2 * FSP))
                counted[dve_fast] = before + (NG // 4 - 1) * 2 * FSP
                fast_pair(NG // 4 - 1, 1, None, (NG // 4 - 1, 0), None)
                add_windows(NG // 4 - 1, 1)
                vec.wait_ge(acc_ready[3], 1)
                V.tensor_copy(al[:, :], acc[:, 0:NB]).then_inc(al_ready[0], 1)
                vec.wait_ge(nl_ready[0], 1)
                nodes_from(misc, dve_fast)
                vec.wait_ge(dst_nl, 1)
                w = (NT - 1) * LO
                V.tensor_tensor(s_n[:, 0:w, :], s_n[:, 0:w, :], p_ref[0][:, 0:w * D].rearrange("p (c f) -> p c f", f=D), ALU.add)
                V.tensor_tensor(s_n[0:TAIL, w:w + LO, :], s_n[0:TAIL, w:w + LO, :],
                                p_ref[0][0:TAIL, w * D:(w + LO) * D].rearrange("p (c f) -> p c f", f=D),
                                ALU.add).then_inc(dst_added, 1)
                vec.wait_ge(dst_added, 1)
                V.memset(counts_f[:, ZP:NZ], 0.0)
                vec.wait_ge(zeroed, 1)
                for r in range(4):
                    vec.sem_inc(c_added, 1)
                with vec.Fori(0, NH // 4) as i:
                    for r in range(8):
                        vec.wait_ge(c_ps, i * 4 + r // 2 + 1)
                        V.tensor_scalar(oh_key[:, r, :], iota_h[:, :], key_f[:, bass.ds(i * 8 + r, 1)], None,
                                        ALU.is_equal).then_inc(c_key, 1)
                    for r in range(4):
                        base = vec.value_load(h_base[0:1, bass.ds(i * 4 + r, 1)], min_val=0, max_val=NB * LO - 1)
                        vec.wait_ge(c_sb, i * 4 + r + 5)
                        V.tensor_tensor(counts[:, :, bass.ds(base, WH)], counts[:, :, bass.ds(base, WH)],
                                        cnt_stage[:, r, :].rearrange("p (h d) -> p h d", d=WH), ALU.add).then_inc(c_added, 1)
                        vec.wait_ge(c_added, i * 4 + r + 5)
                step(V.memset(y_hl[:, :, :], 0.0), on=dve_fast)
            with vec.Else():
                before = counted[dve_general]
                with vec.Fori(0, NG // 2) as i:
                    for u in range(2):
                        chunk = i * (2 * G) + u * G
                        reflect(i + 1, u, (i, 2 * SPG, chunk))
                        one_hots(i * (2 * 2 * G) + 1, u * 2 * G, (0, 1), chunk, oh_ready, oh_used)
                assert counted[dve_general] == before + 2 * SPG
                counted[dve_general] = before + NG * SPG
                to_nodes(0)

            def nbc(t):
                return t.unsqueeze(2).to_broadcast([P, NT * LO, D])

            def layer_norm(k, to, last=None):
                step(V.tensor_reduce(st[:, 0, :], s_n[:, :, :], AX.X, ALU.add))
                step(V.tensor_scalar(st[:, 1, :], st[:, 0, :], 1.0 / D, None, ALU.mult))
                step(V.tensor_tensor(s_n[:, :, :], s_n[:, :, :], nbc(st[:, 1, :]), ALU.subtract))
                step(V.tensor_tensor(t_n[:, :, :], s_n[:, :, :], s_n[:, :, :], ALU.mult))
                step(V.tensor_reduce(st[:, 0, :], t_n[:, :, :], AX.X, ALU.add))
                V.tensor_scalar(st[:, 2, :], st[:, 0, :], 1.0 / D, LN_EPS, ALU.mult, ALU.add).then_inc(root_in[k], 1)
                vec.wait_ge(root_out[k], 1)
                step(V.reciprocal(st[:, 3, :], st[:, 2, :]))
                ins = V.tensor_tensor(to[:, :, :], s_n[:, :, :], nbc(st[:, 3, :]), ALU.mult)
                if last is None:
                    step(ins)
                else:
                    ins.then_inc(last, 1)

            step(V.tensor_tensor(s_n[:, :, :], s_n[:, :, :], d0, ALU.mult))
            step(V.tensor_tensor(s_n[:, :, :], s_n[:, :, :], x_n[:, :, :], ALU.add))
            step(V.scalar_tensor_tensor(s_n[:, :, :].rearrange("p c f -> p (c f)"),
                                        s_n[:, :, :].rearrange("p c f -> p (c f)"), 0.0,
                                        x_n[:, :, :].rearrange("p c f -> p (c f)"), ALU.max, ALU.add))
            layer_norm(0, x1_n)
            V.tensor_tensor(y_n[:, :, :], x1_n[:, :, :], d1, ALU.mult).then_inc(tab_ready[1], 1)
            vec.wait_ge(tab_ready[1], 1)

            def aggregate(k):
                with vec.Fori(0, NG // 2) as i:
                    for u in range(2):
                        chunk = i * (2 * G) + u * G
                        V.tensor_tensor(oh_a[:, u, 0:G, :], a_f[:, 1, bass.ds(chunk, G)].unsqueeze(2).to_broadcast([P, G, LO]),
                                        iota_b[:, 0:LO].unsqueeze(1).to_broadcast([P, G, LO]), ALU.is_equal).then_inc(l_oha[k], 1)
                        vec.wait_ge(l_oha[k], i * 2 + u + 1)
                        vec.wait_ge(l_gathered[k][u], i * (16 * G) + 16 * G)
                        V.tensor_tensor(m8[:, u, 0:G, :, :], oh_a[:, u, 0:G, :].unsqueeze(3).to_broadcast([P, G, LO, D]),
                                        g_xy[:, u, :, 0, 0:D].unsqueeze(2).to_broadcast([P, G, LO, D]),
                                        ALU.mult).then_inc(l_ready[k], 1)
                        vec.wait_ge(l_ready[k], 2 * i + u + 1)
                        V.tensor_copy(st[0:1, 0, 0:1], st[0:1, 1, 0:1]).then_inc(l_free[k], 1)
                        one_hots(i * (2 * G) + 1, u * G, (1,), chunk, l_oh[k], l_ohu[k])

            def product(k):
                vec.wait_ge(hl_in[k], 32)
                step(V.tensor_copy(y3[:, :, 0, :], y_hl[:, :, :]), on=dve_fast)
                step(V.tensor_tensor(r_hl[:, :, :], y_hl[:, :, :], y3[:, :, 0, :], ALU.subtract), on=dve_fast)
                step(V.tensor_copy(y3[:, :, 1, :], r_hl[:, :, :]), on=dve_fast)
                V.tensor_tensor(y3[:, :, 2, :], r_hl[:, :, :], y3[:, :, 1, :], ALU.subtract).then_inc(y3_ready[k], 1)
                for blk in range(0, NBLK, 2):
                    vec.wait_ge(sp_ps[k], blk + 1)
                    V.tensor_copy(agg3[:, blk * BLK:(blk + 1) * BLK], banks[blk][0:3 * D, 0:BLK]).then_inc(sp_sb[k], 1)
                vec.wait_ge(nl_ready[k + 1], 1)
                nodes_from(misc, dve_fast)

            def sum_over_edges(k):
                with vec.If(fast > 0):
                    product(k)
                with vec.Else():
                    aggregate(k)
                    to_nodes(k + 1)

            sum_over_edges(0)
            step(V.tensor_tensor(s_n[:, :, :], s_n[:, :, :], y_n[:, :, :], ALU.add))
            V.tensor_tensor(s_n[:, :, :], s_n[:, :, :], d1, ALU.mult).then_inc(agg_ready, 1)
            vec.wait_ge(al_ready[3], 1)
            V.tensor_copy(al[:, :], misc[:, 0:NB]).then_inc(al_ready[4], 1)
            vec.wait_ge(h_ready, 1)
            for h in range(2):
                ins = V.tensor_scalar(h_al[:, h, :], banks[1 + h][:, 0:NB], bn_vec[:, 0:1], None, ALU.add)
            step(ins)

            def zero_padding(t):
                for a in range(N_NODES - (NB - 1) * LO, LO):
                    r = (a - 4) * HID1
                    ins = V.memset(t[r:r + HID1, 1, NB - 1:NB], 0.0)
                step(ins)

            zero_padding(h_al)
            hf = h_al[:, :, :].rearrange("p h b -> p (h b)")
            hcf = hc_al[:, :, :].rearrange("p h b -> p (h b)")
            V.tensor_reduce(bn[:, 0:1], hf, AX.X, ALU.add).then_inc(sum_in[0], 1)
            vec.wait_ge(sum_out[0], 1)
            step(V.tensor_scalar(bn[:, 1:2], p_hid[0][:, 0:1], 1.0 / N_NODES, None, ALU.mult))
            step(V.tensor_scalar(hcf, hf, bn[:, 1:2], None, ALU.subtract))
            zero_padding(hc_al)
            step(V.tensor_tensor(hf, hcf, hcf, ALU.mult))
            V.tensor_reduce(bn[:, 2:3], hf, AX.X, ALU.add).then_inc(sum_in[1], 1)
            vec.wait_ge(sum_out[1], 1)
            V.tensor_scalar(bn[:, 3:4], p_hid[1][:, 0:1], 1.0 / N_NODES, LN_EPS, ALU.mult, ALU.add).then_inc(root_in[1], 1)
            vec.wait_ge(root_out[1], 1)
            step(V.reciprocal(bn[:, 4:5], bn[:, 3:4]))
            V.tensor_tensor(bn[:, 5:6], bn[:, 4:5], bn_vec[:, 1:2], ALU.mult).then_inc(bn_ready, 1)
            vec.wait_ge(u_ready, 1)
            V.tensor_copy(al[:, :], misc[:, 0:NB]).then_inc(u_sb, 1)
            vec.wait_ge(nl_ready[3], 1)
            w = (NT - 1) * LO
            V.tensor_tensor(y_n[:, 0:w, :], p_ref[0][:, 0:w * D].rearrange("p (c f) -> p c f", f=D), d1[:, 0:w, :], ALU.mult)
            V.tensor_tensor(y_n[0:TAIL, w:w + LO, :], p_ref[0][0:TAIL, w * D:(w + LO) * D].rearrange("p (c f) -> p c f", f=D),
                            d1[0:TAIL, w:w + LO, :], ALU.mult).then_inc(tab_ready[2], 1)
            vec.wait_ge(tab_ready[2], 1)
            sum_over_edges(1)
            step(V.tensor_tensor(s_n[:, :, :], s_n[:, :, :], y_n[:, :, :], ALU.add))
            step(V.tensor_tensor(s_n[:, :, :], s_n[:, :, :], d1, ALU.mult))
            step(V.tensor_tensor(s_n[:, :, :], s_n[:, :, :],
                                 bias_out[:, :].unsqueeze(1).to_broadcast([P, NT * LO, D]), ALU.add))
            step(V.tensor_tensor(s_n[:, :, :], s_n[:, :, :], x1_n[:, :, :], ALU.add))
            layer_norm(2, s_n, out_ready)

        @block.tensor
        def _(pe):
            M = nc.tensor.matmul
            pe.wait_ge(idx_rows, 1)
            for s in range(2):
                for t in range(RT):
                    r = min(P, NCH - t * P)
                    ins = nc.tensor.transpose(banks[1 + 2 * s + t // 4][:, (t % 4) * P:(t % 4) * P + r],
                                              rows_f[0:r, s, t, :], ident[0:r, 0:r])
            ins.then_inc(idx_cols, 1)
            M(misc[0:NQ, 0:2 * QLO], zeros[:, 0:NQ], zeros[:, 0:2 * QLO], start=True, stop=False, skip_group_check=True)
            for s in range(2):
                pe.sem_inc(hist_used[s], 1)
            with pe.Fori(0, NCH // HG) as i:
                for s in range(2):
                    pe.wait_ge(oh_hist[s], i + 1)
                    for c in range(HG):
                        ins = M(misc[0:NQ, s * QLO:(s + 1) * QLO], oh_p[:, s, :, c], oh_q[:, s, :, c], start=False, stop=False,
                                skip_group_check=True)
                    ins.then_inc(hist_used[s], 1)
            M(misc[0:NQ, 0:2 * QLO], zeros[:, 0:NQ], zeros[:, 0:2 * QLO], start=False, stop=True,
              skip_group_check=True).then_inc(hist_done, 1)

            pe.wait_ge(viol_ready, 1)
            M(p_hid[0][0:1, 0:1], viol[:, 7:8], ones_col, start=True, stop=True).then_inc(viol_sum, 1)
            pe.wait_ge(hist_sb, 1)
            for t in range(NT):
                w = min(P, NB - t * P)
                ins = nc.tensor.transpose(misc[:, t * P:t * P + w],
                                          x_n[0:w, t * LO:(t + 1) * LO, :].rearrange("p a f -> p (a f)"), ident[0:w, 0:w])
            ins.then_inc(xa_ps, 1)
            pe.wait_ge(xa_sb, 1)
            for t in range(NT):
                w = min(P, NB - t * P)
                for h in range(2):
                    if t:
                        pe.wait_ge(win_w, 2 * (t - 1) + h + 1)
                    M(p_tr[h][0:w, :], xa[:, t * P:t * P + w], w_proj[:, 4 * h:4 * h + 4, :].rearrange("p a n -> p (a n)"),
                      start=True, stop=True).then_inc(proj_ps, 1)

            def fast_front(i, w):
                pe.wait_ge(f_gath[w], i * (16 * 2 * G) + 16 * 2 * G)
                pe.nop(nofuse=True)
                for gg in range(2):
                    for c in range(G):
                        ins = nc.tensor.transpose(p_tr[gg][0:32, c * P:(c + 1) * P],
                                                  f_rows[:, w, gg * G + c, 0:2 * D], ident)
                    ins.then_inc(f_turned, 1)
                for gg in range(2):
                    q = 2 * w + gg
                    pe.wait_ge(f_ohdt, i * 4 + q + 1)
                    pe.wait_ge(f_xready, i * 4 + q + 1)
                    M(p_hid[gg][:, :], f_win[:, q, 0:2 * HID0], f_xT[:, q, :], start=True, stop=True).then_inc(f_pre, 1)
                pe.wait_ge(f_done, i * 2 + w + 1)
                for gg in range(2):
                    q = 2 * w + gg
                    for c in range(G):
                        k = 4 * G * D + (gg * G + c) * D
                        ins = M(p_ref[w][:, k:k + D], f_xT[:, q, c * P:(c + 1) * P], f_win[:, q, 2 * HID0:WROW],
                                start=True, stop=True)
                    ins.then_inc(f_front, 1)
                M(p_ref[w][:, 0:4 * G * D], ones_row[:, :], bias_rep[0:1, :, :].rearrange("p c f -> p (c f)"),
                  start=True, stop=False, skip_group_check=True)
                for gg in range(2):
                    pe.wait_ge(f_relu, i * 4 + 2 * w + gg + 1)
                    for c in range(G):
                        k = (gg * G + c) * 2 * D
                        ins = M(p_ref[w][:, k:k + 2 * D], f_hid[:, gg, c * P:(c + 1) * P], w_ref[:, :],
                                start=False, stop=(gg == 1 and c == G - 1), skip_group_check=True)
                ins.then_inc(f_ref, 1)

            def fast_scatter(i, w):
                pe.wait_ge(f_mready, i * 2 + w + 1)
                for gg in range(2):
                    k = 2 * w + gg
                    for c in range(G):
                        cc = gg * G + c
                        ins = M(misc[0:D, k * WG:(k + 1) * WG], f_msg[:, w, 2 * cc + 1, :], f_ohd[:, w, cc, :],
                                start=(c == 0), stop=(c == G - 1))
                ins.then_inc(f_winps, 1)
                for c in range(2 * G):
                    k = w * 2 * G + c
                    r = k % FRING
                    pe.wait_ge(f_oh, i * (4 * G) + k + 1)
                    M(acc[:, 0:NB], f_m8[:, w, c, :, :].rearrange("p a f -> p (a f)"), f_ohb[:, r, :],
                      start=False, stop=False, skip_group_check=True).then_inc(f_ohu, 1)

            def front(n, u):
                pe.wait_ge(gathered[u], n * (16 * 2 * G))
                pe.nop(nofuse=True)
                for c in range(G):
                    ins = nc.tensor.transpose(p_tr[u][0:64, c * P:(c + 1) * P],
                                              g_xy[:, u, c, :, :].rearrange("p s f -> p (s f)"), ident)
                ins.then_inc(turned, 1)
                pe.wait_ge(x_ready, 2 * n + u - 1)
                M(p_hid[u][:, :], w_hid[:, :], xT[:, u, :], start=True, stop=True).then_inc(pre_ready, 1)
                pe.wait_ge(v_taken, 2 * n + u - 1)
                pe.wait_ge(hid_ready, 2 * n + u - 1)
                for c in range(G):
                    ins = M(p_ref[u][:, c * 2 * D:(c + 1) * 2 * D], hidT[:, u, c * P:(c + 1) * P], w_ref[:, :],
                            start=True, stop=True)
                ins.then_inc(ref_ready, 1)

            def scatter(n, u, i):
                pe.wait_ge(m_ready, 2 * n + u - 1)
                for c in range(2 * G):
                    k = u * 2 * G + c
                    r = k % RING
                    pe.wait_ge(oh_ready, i * (2 * 2 * G) + k + 1)
                    ins = M(acc[:, 0:NB], m8[:, u, c, :, :].rearrange("p a f -> p (a f)"), oh_b[:, r, :],
                            start=False, stop=False, skip_group_check=True)
                    ins.then_inc(oh_used, 1)

            def clear():
                return M(acc[:, 0:NB], zeros[:, :], iota_b, start=True, stop=False, skip_group_check=True)

            def close(k):
                M(acc[:, 0:NB], zeros[:, :], iota_b, start=False, stop=True, skip_group_check=True).then_inc(acc_ready[k], 1)

            def to_tiles(bank, src_t, done):
                for t in range(NT):
                    w = min(P, NB - t * P)
                    ins = nc.tensor.transpose(bank[0:w, t * P:(t + 1) * P], src_t[:, t * P:t * P + w], ident)
                ins.then_inc(done, 1)

            pe.wait_ge(flag_ready, 1)
            fast = pe.value_load(flag[0:1, 0:1], min_val=0, max_val=1)
            with pe.If(fast > 0):
                clear()
                for r in range(FRING):
                    pe.sem_inc(f_ohu, 1)
                for q in range(4):
                    pe.sem_inc(f_front, 1)
                fast_front(0, 0)
                with pe.Fori(0, NG // 4 - 1) as i:
                    fast_front(i, 1)
                    fast_scatter(i, 0)
                    fast_front(i + 1, 0)
                    fast_scatter(i, 1)
                n = NG // 4 - 1
                fast_front(n, 1)
                fast_scatter(n, 0)
                fast_scatter(n, 1)
                close(3)
                pe.wait_ge(f_wadd, NG)
                for t in range(NT):
                    w = min(P, NB - t * P)
                    for a in range(LO):
                        k = t * P * LO + a
                        ins = nc.tensor.transpose(p_ref[0][0:w, (t * LO + a) * D:(t * LO + a + 1) * D],
                                                  acc_dst[:, k:k + LO * (w - 1) + 1:LO], ident[0:D, 0:D])
                ins.then_inc(dst_nl, 1)
                pe.wait_ge(al_ready[0], 1)
                to_tiles(misc, al, nl_ready[0])
                for r in range(4):
                    pe.sem_inc(c_ps, 1)
                    pe.sem_inc(c_sb, 1)
                with pe.Fori(0, NH // 4) as i:
                    for r in range(4):
                        pe.wait_ge(c_sb, i * 4 + r + 1)
                        for c in range(2):
                            pe.wait_ge(c_lo, i * 8 + 2 * r + c + 9)
                            pe.wait_ge(c_key, i * 8 + 2 * r + c + 1)
                            ins = M(banks[1 + r][:, 0:NKEY], oh_lo[:, 2 * r + c, :], oh_key[:, 2 * r + c, :],
                                    start=(c == 0), stop=(c == 1))
                        ins.then_inc(c_ps, 1)
            with pe.Else():
                clear()
                for r in range(RING):
                    pe.sem_inc(oh_used, 1)
                for u in range(2):
                    pe.sem_inc(turned, 1)
                    pe.sem_inc(v_taken, 1)
                front(1, 0)
                with pe.Fori(0, NG // 2 - 1) as i:
                    front(i + 1, 1)
                    scatter(i + 1, 0, i)
                    front(i + 2, 0)
                    scatter(i + 1, 1, i)
                n = NG // 2
                front(n, 1)
                scatter(n, 0, n - 1)
                scatter(n, 1, n - 1)
                close(0)

                pe.wait_ge(al_ready[0], 1)
                to_tiles(misc, al, nl_ready[0])

            def aggregate(k):
                clear()
                for r in range(RING):
                    pe.sem_inc(l_ohu[k], 1)
                with pe.Fori(0, NG // 2) as i:
                    for u in range(2):
                        pe.wait_ge(l_ready[k], 2 * i + u + 1)
                        for c in range(G):
                            j = u * G + c
                            r = j % RING
                            pe.wait_ge(l_oh[k], i * (2 * G) + j + 1)
                            ins = M(acc[:, 0:NB], m8[:, u, c, :, :].rearrange("p a f -> p (a f)"), oh_b[:, r, :],
                                    start=False, stop=False, skip_group_check=True)
                            ins.then_inc(l_ohu[k], 1)
                close(k + 1)

            def product(k):
                pe.wait_ge(y3_ready[k], 1)
                if k == 0:
                    pe.wait_ge(c_added, NH + 4)
                for blk in range(NBLK):
                    for hi in range(NHI):
                        ins = M(banks[blk][0:3 * D, 0:BLK], y3[:, hi, :, :].rearrange("p s f -> p (s f)"),
                                counts[:, hi, blk * BLK:(blk + 1) * BLK], start=(hi == 0), stop=(hi == NHI - 1))
                    ins.then_inc(sp_ps[k], 1)
                pe.wait_ge(sp_sb[k], (NBLK + 1) // 2)
                pe.wait_ge(sp_act[k], NBLK // 2)
                for t in range(NT):
                    w = min(P, NB - t * P)
                    for a in range(LO):
                        n0 = t * P * LO + a
                        ins = M(misc[0:w, (t * LO + a) * D:(t * LO + a + 1) * D], agg3[:, n0:n0 + LO * (w - 1) + 1:LO],
                                same_feat[0:3 * D, :], start=True, stop=True)
                ins.then_inc(nl_ready[k + 1], 1)

            def sum_over_edges(k):
                with pe.If(fast > 0):
                    product(k)
                with pe.Else():
                    aggregate(k)
                    pe.wait_ge(al_ready[k + 1], 1)
                    to_tiles(misc, al, nl_ready[k + 1])

            sum_over_edges(0)
            pe.wait_ge(agg_ready, 1)
            for t in range(NT):
                w = min(P, NB - t * P)
                ins = nc.tensor.transpose(misc[:, t * P:t * P + w],
                                          s_n[0:w, t * LO:(t + 1) * LO, :].rearrange("p a f -> p (a f)"), ident[0:w, 0:w])
            ins.then_inc(al_ready[3], 1)
            pe.wait_ge(al_ready[4], 1)
            for h in range(2):
                ins = M(banks[1 + h][:, 0:NB], w1_diag[:, h, :], al[:, :], start=True, stop=True)
            ins.then_inc(h_ready, 1)
            for k, col in ((0, 0), (1, 2)):
                pe.wait_ge(sum_in[k], 1)
                M(p_hid[k][:, 0:1], same_unit, bn[:, col:col + 1], start=True, stop=True).then_inc(sum_out[k], 1)
            pe.wait_ge(relu_ready, 2)
            for h in range(2):
                ins = M(misc[:, 0:NB], w2_diag[:, h, :], h_al[:, h, :], start=(h == 0), stop=(h == 1))
            ins.then_inc(u_ready, 1)
            pe.wait_ge(u_sb, 1)
            to_tiles(p_ref[0], al, nl_ready[3])
            sum_over_edges(1)


def kernel(**inputs):
    import numpy as _np
    import concourse.bacc as _bacc
    from concourse import mybir as _mybir
    from concourse.bass_utils import run_bass_kernel_spmd as _run

    nc = _bacc.Bacc("TRN2", target_bir_lowering=False, num_devices=1)
    lane = _np.arange(P)
    shape_consts = _np.concatenate([
        _np.eye(P), lane[:, None] % HID1 == lane[None, :] % HID1, lane[:, None] % 32,
        lane[:, None] % D == _np.arange(D)[None, :], _np.tile(_np.arange(NKEY), (P, 1)),
    ], axis=1, dtype=_np.float32)
    given = {
        "x": inputs["x"], "src": inputs["src"], "dst": inputs["dst"],
        "w0_in": _np.asarray(inputs["L0_gnn_W1"]).T, "b0_in": inputs["L0_gnn_b1"],
        "w0_out": _np.asarray(inputs["L0_gnn_W2"]).T, "b0_out": inputs["L0_gnn_b2"],
        "w1": inputs["L1_gnn_W1"], "b1": inputs["L1_gnn_b1"], "gamma": inputs["L1_gnn_gamma"],
        "beta": inputs["L1_gnn_beta"], "w2": inputs["L1_gnn_W2"], "b2": inputs["L1_gnn_b2"],
        "shape_consts": shape_consts,
    }
    arrays, args = {}, []
    for name, a in given.items():
        a = _np.ascontiguousarray(a)
        arrays[f"in_{name}"] = a
        args.append(nc.dram_tensor(f"in_{name}", a.shape, _mybir.dt.from_np(a.dtype), kind="ExternalInput").ap())
    args.append(nc.dram_tensor("out_0", (N_NODES, D), F32, kind="ExternalOutput").ap())
    gnn(nc, *args)
    r = _run(nc, [arrays], core_ids=[0])
    return r.results[0]["out_0"]
```

```python
import concourse.bass as bass
from concourse import mybir
from contextlib import ExitStack
import math

F32 = mybir.dt.float32
BF16 = mybir.dt.bfloat16
F16 = mybir.dt.float16
I32 = mybir.dt.int32
ALU = mybir.AluOpType
ACT = mybir.ActivationFunctionType
AX = mybir.AxisListType
SP = mybir.EngineType.SP
DVE = mybir.EngineType.DVE

P = 128
N_NODES = 3125
N_EDGES = 100000
D = 16
HID0 = 64
HID1 = 32
LO = 8
NB = -(-(N_NODES + 1) // LO)
NT = -(-NB // P)
TAIL = NB - (NT - 1) * P
PAD = N_NODES
QLO = 64
NQ = -(-(NB * LO) // QLO)
G = 4
NCH = -(-N_EDGES // (P * G)) * G
NG = NCH // G
RT = -(-NCH // P)
HG = 28
LN_EPS = 1e-5
WG = 32
WH = 14
NH = 2 * NG
LANES = 128
NHI = -(-NB * LO // LANES)
NKEY = NHI * WH
NIOTA = max(NB, NKEY)
HALVES = 16
AHEAD = 3
POOLS_HALVES = (1, 3, 5)
NA = NB * LO + WH
NBLK = 7
BLK = -(-NB * LO // NBLK)
WROW = 2 * HID0 + D
SPLIT = 3
PIECE_PARTS = (0, 1, 2, 2, 2, 2, 0, 1)
PIECE_WEIGHTS = (1, 1, 1, 0, 2, 3, 0, 0)
PIECES = len(PIECE_PARTS)
KDST = SPLIT * WG
KLAST = 2 * D
YS = PIECES * D // 2
FROW = YS + D
NPAIR = NG // 2
SLOTS = 4
TURNS = NPAIR // SLOTS
GP = 2
FRING = 16
MAX_COUNT = 256
BASES_ARE_NODES = "a base is the smallest destination of its edges, made even, or zero: a node's number"
KR = (N_NODES - (NT - 1) * P * LO) // LO


def gnn(nc, x, src, dst, w0_in, b0_in, w0_out, b0_out, w1, b1, gamma, beta, w2, b2, consts, out):
    with ExitStack() as ctx:
        def sb(name, shape, dt=F32):
            return ctx.enter_context(nc.sbuf_tensor(name, shape, dt))

        def sem(name):
            return ctx.enter_context(nc.semaphore(name))

        cst = sb("cst", [P, 2 * P + 1 + D + SPLIT + NIOTA])
        ident = cst[:, 0:P]
        same_unit = cst[:, P:2 * P]
        lane32 = cst[:, 2 * P:2 * P + 1]
        same_feat = cst[:, 2 * P + 1:2 * P + 1 + D]
        part_of = cst[:, 2 * P + 1 + D:2 * P + 1 + D + SPLIT]
        iota_k = cst[:, 2 * P + 1 + D + SPLIT:]
        iota_b = iota_k[:, 0:NB]
        ones_col = iota_k[:, 1:2]
        h_base_i = sb("h_base_i", [P, 4], I32)
        g_base_i = sb("g_base_i", [P, 2], I32)
        g_base_f = sb("g_base_f", [P, 2])
        h_base_f = sb("h_base_f", [P, 4])
        h_top = sb("h_top", [P, 4])
        g_top = sb("g_top", [P, 2])
        viol = sb("viol", [P, 8])
        flag = sb("flag", [1, 2], I32)
        g_base = sb("g_base", [P, GP + NG], I32)
        h_base = sb("h_base", [P, NH], I32)
        key_f = sb("key_f", [P, NCH])
        lo_f = sb("lo_f", [P, NCH])
        iota_h = sb("iota_h", [P, NKEY], F16)
        zeros = sb("zeros", [P, P])
        ident_b = sb("ident_b", [P, P], BF16)
        w_all = sb("w_all", [P, 2 * HID0], BF16)
        no_rows = sb("no_rows", [WG, WROW], BF16)
        w_hid = sb("w_hid", [64, 2 * HID0])
        w_ref = sb("w_ref", [2 * HID0, 2 * D])
        bias_hid = sb("bias_hid", [2 * HID0, 1])
        bias_ref = sb("bias_ref", [P, 2, D])
        bias3 = sb("bias3", [3, 4 * G * D], BF16)
        bias_f = sb("bias_f", [3, D])
        bias_rest = sb("bias_rest", [3, D])
        bias_parts = sb("bias_parts", [3, 3, D], BF16)
        ones3 = sb("ones3", [3, P], BF16)
        w1_diag = sb("w1_diag", [P, 2, P])
        w2_diag = sb("w2_diag", [P, 2, P])
        bn_vec = sb("bn_vec", [P, 3])
        bias_out = sb("bias_out", [P, D])
        dinv = sb("dinv", [P, 2, NT * LO])
        x_n = sb("x_n", [P, NT * LO, D])
        x1_n = sb("x1_n", [P, NT * LO, D])
        y_n = sb("y_n", [P, NT * LO, D])
        s_n = sb("s_n", [P, NT * LO, D])
        t_n = sb("t_n", [P, NT * LO, D])
        st = sb("st", [P, 4, NT * LO])
        al = sb("al", [P, NB])
        h_al = sb("h_al", [P, 2, NB])
        hc_al = sb("hc_al", [P, 2, NB])
        bn = sb("bn", [P, 8])
        y_hl = t_n[:, 0:NHI, :]
        r_hl = hc_al[:, :, :].rearrange("p h b -> p (h b)")[:, 0:NHI * D].rearrange("p (h f) -> p h f", f=D)
        y3 = (h_al[:, :, :].rearrange("p h b -> p (h b)")[:, 0:NHI * SPLIT * D // 2].bitcast(BF16)
              .rearrange("p (h s f) -> p h s f", s=SPLIT, f=D))
        stage = ExitStack()
        words = {}

        def esb(name, shape, dt=F32):
            size = (2 if dt in (BF16, F16) else 4) * math.prod(shape[1:])
            words[stage] = words.get(stage, 0) + -(-size // 64) * 16
            return stage.enter_context(nc.sbuf_tensor(name, shape, dt))

        agg3 = esb("agg3", [3 * D, NBLK * BLK])
        stage.close()
        lo_stage = esb("lo_stage", [P, 16])
        oh_lo = esb("oh_lo", [P, 8, 2, LANES], BF16)
        oh_key = esb("oh_key", [P, 8, 2, NKEY], BF16)
        cnt_stage = esb("cnt_stage", [P, 4, NKEY], BF16)
        ctx.enter_context(stage.pop_all())
        room = ExitStack()
        stage = room
        node_i = esb("node_i", [P, 2, NCH], I32)
        a_f = esb("a_f", [P, 2, NCH])
        b_f = esb("b_f", [P, 2, NCH])
        dst_rel = esb("dst_rel", [P, NCH])
        f_win = esb("f_win", [P, 2 * SLOTS, WROW], BF16)
        stage = ExitStack()
        words[stage] = 0
        rows_i = esb("rows_i", [P, 2, RT, P], I32)
        rows_f = esb("rows_f", [P, 2, RT, P])
        iota_q = esb("iota_q", [P, QLO, HG], BF16)
        cnt = esb("cnt", [P, 2, NT, LO])
        dst_rows = esb("dst_rows", [P, 4, 2 * P], I32)
        part_i = esb("part_i", [P, 2, NCH], I32)
        q_bf = esb("q_bf", [P, 2, NCH], BF16)
        p_bf = esb("p_bf", [P, 2, NCH], BF16)
        oh_q = esb("oh_q", [P, 2, QLO, HG], BF16)
        oh_p = esb("oh_p", [P, 2, NQ, HG], BF16)
        hist = esb("hist", [NQ, 2, QLO])
        tab = esb("tab", [P, NT, LO, 2 * D])
        w_proj = esb("w_proj", [P, LO, 2 * HID0])
        xa = esb("xa", [P, NB])
        w_f32 = esb("w_f32", [P, 2 * HID0])
        w_parts = esb("w_parts", [P, SPLIT, 2 * HID0], BF16)
        rel_rows = esb("rel_rows", [P, 2, G * P], BF16)
        f_tab = esb("f_tab", [P, NT * LO, FROW])
        x_rest = esb("x_rest", [P, NT * LO, D])
        xp_rest = esb("xp_rest", [P, NT * LO, D])
        w_table = esb("w_table", [P, SPLIT, NT * LO, WROW], BF16)
        table_words = words[room] + words[stage]
        w_proj_f = esb("w_proj_f", [P, NT * LO, 2 * HID0])
        stage.close()
        bias_rep = esb("bias_rep", [P, G * 4, D])
        idx_stage = esb("idx_stage", [P, 2, 2, G], I32)
        g_xy = esb("g_xy", [P, 2, G, 2, 2 * D])
        xT = esb("xT", [64, 2, G * P])
        hidT = esb("hidT", [P, 2, G * P])
        v = esb("v", [P, G * 2, D])
        prod = esb("prod", [P, G * 2, D])
        z = esb("z", [P, G, 2, D])
        msg = esb("msg", [P, 2, G * 2, D])
        n2 = esb("n2", [P, G * 2])
        cc = esb("cc", [P, G * 2])
        dots = esb("dots", [P, G * 2])
        oh_a = esb("oh_a", [P, 2, G * 2, LO])
        m8 = esb("m8", [P, 2, G * 2, LO, D])
        RING = 4
        oh_b = esb("oh_b", [P, RING, NB])
        stage.close()
        words[stage] = 0
        f_rows = esb("f_rows", [P, SLOTS, 2 * G, FROW + D])
        f_stage = esb("f_stage", [P, SLOTS, 2 * G], I32)
        f_xT = esb("f_xT", [P, 2, G * P], BF16)
        f_ohT = esb("f_ohT", [P, 2 * SLOTS, G * P], BF16)
        f_dst = esb("f_dst", [P, 2 * SLOTS, G * P], BF16)
        f_hid = esb("f_hid", [P, 2, G * P])
        f_sq = esb("f_sq", [P, 2, 4 * G, D])
        f_prod = esb("f_prod", [P, 4 * G, D])
        f_z = esb("f_z", [P, 2 * G, 2, D])
        f_msg = esb("f_msg", [P, 2, 4 * G, D])
        f_n2 = esb("f_n2", [P, 4 * G])
        f_cc = esb("f_cc", [P, 4 * G])
        f_dots = esb("f_dots", [P, 4 * G])
        f_oha = esb("f_oha", [P, 2 * G, LO])
        f_m8 = esb("f_m8", [P, 2, 2 * G, LO, D])
        f_ohd = esb("f_ohd", [P, 2, 2 * G, WG])
        f_ohb = esb("f_ohb", [P, FRING, NB])
        acc_dst = esb("acc_dst", [D, NB * LO + WG])
        edge_words = words[room] + words[stage]
        stage.close()
        room.close()
        counts = sb("counts", [P, NHI, NA], BF16)
        counts_f = counts[:, :, :].rearrange("p h n -> p (h n)").bitcast(F32)
        words_end = NHI * NA // 2
        share = edge_words // 2
        shares = ((0, share), (share, share + share // 2), (share + share // 2, edge_words))
        hist_d = nc.dram_tensor("hist_d", (2, NQ * QLO), F32, kind="Internal").ap()
        table = [nc.dram_tensor(f"table{k}", (NB * LO, w), F32, kind="Internal").ap()
                 for k, w in enumerate((2 * D, D, D))]
        f_table = nc.dram_tensor("f_table", (NB * LO, FROW), F32, kind="Internal").ap()
        w_rows = nc.dram_tensor("w_rows", (SPLIT, NB * LO + WG, WROW), BF16, kind="Internal").ap()
        dst_d = nc.dram_tensor("dst_d", (NCH * P,), BF16, kind="Internal").ap()
        g_base_d = nc.dram_tensor("g_base_d", (NG,), I32, kind="Internal").ap()
        h_base_d = nc.dram_tensor("h_base_d", (NH,), I32, kind="Internal").ap()

        banks = [ctx.enter_context(nc.psum_tensor(f"bank{i}", [P, 512], F32)) for i in range(8)]
        acc = banks[0]
        p_tr = banks[1:3]
        p_hid = banks[3:5]
        p_ref = banks[5:7]
        misc = banks[7]

        loaded = sem("loaded")
        idx_in = sem("idx_in")
        nodes_in = sem("nodes_in")
        padded = sem("padded")
        padded_pool = sem("padded_pool")
        pool_step = sem("pool_step")
        w_ready = sem("w_ready")
        q_ready = sem("q_ready")
        rel_ready = sem("rel_ready")
        rel_out = sem("rel_out")
        xp_ready = sem("xp_ready")
        parts_ready = sem("parts_ready")
        f_tab_out = sem("f_tab_out")
        dve = sem("dve_step")
        dve_fast = sem("dve_fast")
        dve_general = sem("dve_general")
        idx_rows = sem("idx_rows")
        idx_cols = sem("idx_cols")
        parts = sem("parts")
        oh_hist = [sem(f"oh_hist{s}") for s in range(2)]
        hist_used = [sem(f"hist_used{s}") for s in range(2)]
        hist_done = sem("hist_done")
        hist_sb = sem("hist_sb")
        hist_out = sem("hist_out")
        hist_in = sem("hist_in")
        deg_ready = sem("deg_ready")
        deg_root = sem("deg_root")
        tab_ready = [sem(f"tab_ready{k}") for k in range(3)]
        tab_out = [sem(f"tab_out{k}") for k in range(3)]
        staged = sem("staged")
        gathered = [sem(f"gathered{u}") for u in range(2)]
        g_free_dve = sem("g_free_dve")
        turned = sem("turned")
        x_ready = sem("x_ready")
        pre_ready = sem("pre_ready")
        hid_ready = sem("hid_ready")
        ref_ready = sem("ref_ready")
        v_taken = sem("v_taken")
        m_ready = sem("m_ready")
        oh_ready = sem("oh_ready")
        oh_used = sem("oh_used")
        l_staged = [sem(f"l_staged{k}") for k in range(2)]
        l_gathered = [[sem(f"l{k}_gathered{u}") for u in range(2)] for k in range(2)]
        l_free = [sem(f"l_free{k}") for k in range(2)]
        l_ready = [sem(f"l_ready{k}") for k in range(2)]
        l_oha = [sem(f"l{k}_oha") for k in range(2)]
        l_oh = [sem(f"l_oh{k}") for k in range(2)]
        l_ohu = [sem(f"l_ohu{k}") for k in range(2)]
        acc_ready = [sem(f"acc_ready{k}") for k in range(4)]
        al_ready = [sem(f"al_ready{k}") for k in range(5)]
        nl_ready = [sem(f"nl_ready{k}") for k in range(4)]
        root_in = [sem(f"root_in{k}") for k in range(3)]
        root_out = [sem(f"root_out{k}") for k in range(3)]
        agg_ready = sem("agg_ready")
        h_ready = sem("h_ready")
        sum_in = [sem(f"sum_in{k}") for k in range(2)]
        sum_out = [sem(f"sum_out{k}") for k in range(2)]
        bn_ready = sem("bn_ready")
        relu_ready = sem("relu_ready")
        u_ready = sem("u_ready")
        u_sb = sem("u_sb")
        out_ready = sem("out_ready")
        stored = sem("stored")

        base_ready = sem("base_ready")
        base_out = sem("base_out")
        base_in = sem("base_in")
        viol_ready = sem("viol_ready")
        viol_sum = sem("viol_sum")
        flag_ready = sem("flag_ready")
        xa_ps = sem("xa_ps")
        xa_sb = sem("xa_sb")
        proj_ps = sem("proj_ps")
        proj_sb = sem("proj_sb")
        proj_out = sem("proj_out")
        win_w = sem("win_w")
        f_in = [sem(f"f_in{q}") for q in range(2 * SLOTS)]
        f_front = sem("f_front")
        f_staged = sem("f_staged")
        f_gath = [sem(f"f_gath{m}") for m in range(SLOTS)]
        f_free = sem("f_free")
        f_ohdt = sem("f_ohdt")
        f_turned = sem("f_turned")
        f_xready = sem("f_xready")
        f_pre = sem("f_pre")
        f_relu = sem("f_relu")
        f_ref = sem("f_ref")
        f_sqd = sem("f_sqd")
        f_sqr = sem("f_sqr")
        f_done = sem("f_done")
        f_mready = sem("f_mready")
        f_winps = sem("f_winps")
        f_oh = sem("f_oh")
        f_ohu = sem("f_ohu")
        f_wadd = sem("f_wadd")
        dst_nl = sem("dst_nl")
        zeroed = sem("zeroed")
        c_los = sem("c_los")
        c_lo = sem("c_lo")
        c_key = sem("c_key")
        c_ps = sem("c_ps")
        dst_added = sem("dst_added")
        c_sb = sem("c_sb")
        c_added = sem("c_added")
        hl_in = [sem(f"hl_in{k}") for k in range(2)]
        y3_ready = [sem(f"y3_ready{k}") for k in range(2)]
        sp_ps = [sem(f"sp_ps{k}") for k in range(2)]
        sp_sb = [sem(f"sp_sb{k}") for k in range(2)]
        sp_act = [sem(f"sp_act{k}") for k in range(2)]

        n_loads = {}
        PROJ_OUT = 16 * (2 * SPLIT + 1)
        block = ctx.enter_context(nc.Block())

        @block.sync
        def _(sync):
            def load(dst_ap, src_ap, which=None):
                which = which or loaded
                n_loads[which] = n_loads.get(which, 0) + 16
                nc.sync.dma_start(dst_ap, src_ap).then_inc(which, 16)

            m = (NT - 1) * P * LO
            left = N_NODES - m - KR * LO
            sync.wait_ge(padded, 1)
            full = N_EDGES // P
            for s, e in enumerate((src, dst)):
                load(rows_i[:, s, 0:RT - 1, :], e[0:(RT - 1) * P * P].rearrange("(t r e) -> r t e", r=P, e=P), idx_in)
                last = full - (RT - 1) * P
                load(rows_i[0:last, s, RT - 1, :], e[(RT - 1) * P * P:full * P].rearrange("(r e) -> r e", e=P), idx_in)
                load(rows_i[last:last + 1, s, RT - 1, 0:N_EDGES - full * P],
                     e[full * P:N_EDGES].rearrange("(r e) -> r e", r=1), idx_in)
            load(cst[:, :], consts, idx_in)
            per_row = 2 * G * P
            whole = N_EDGES // per_row
            load(dst_rows[0:whole, :, :].rearrange("p h e -> p (h e)"),
                 dst[0:whole * per_row].rearrange("(p e) -> p e", e=per_row), idx_in)
            load(dst_rows[whole:whole + 1, :, :].rearrange("p h e -> p (h e)")[:, 0:N_EDGES - whole * per_row],
                 dst[whole * per_row:N_EDGES].rearrange("(p e) -> p e", p=1), idx_in)
            sync.wait_ge(padded_pool, 1)
            load(x_n[:, 0:(NT - 1) * LO, :].rearrange("p (t a) f -> p t (a f)", a=LO),
                 x[0:m, :].rearrange("(t b a) f -> b t (a f)", b=P, a=LO), nodes_in)
            load(x_n[0:KR, (NT - 1) * LO:NT * LO, :].rearrange("p a f -> p (a f)"),
                 x[m:m + KR * LO, :].rearrange("(b a) f -> b (a f)", a=LO), nodes_in)
            load(x_n[KR:KR + 1, (NT - 1) * LO:(NT - 1) * LO + left, :].rearrange("p a f -> p (a f)"),
                 x[m + KR * LO:N_NODES, :].rearrange("(b a) f -> b (a f)", b=1), nodes_in)
            for h in range(2):
                load(w_f32[:, h * HID0:(h + 1) * HID0],
                     w0_in[h * D:(h + 1) * D, :].unsqueeze(0).to_broadcast([PIECES, D, HID0]), nodes_in)
            for a in range(LO):
                load(w_proj[a * D:(a + 1) * D, a, 0:HID0], w0_in[D:2 * D, :], nodes_in)
                load(w_proj[a * D:(a + 1) * D, a, HID0:2 * HID0], w0_in[0:D, :], nodes_in)

            sync.wait_ge(base_ready, 1)
            nc.sync.dma_start(g_base_d.rearrange("(p h) -> p h", h=2), g_base_i[0:NG // 2, :]).then_inc(base_out, 16)
            nc.sync.dma_start(h_base_d.rearrange("(p h) -> p h", h=4), h_base_i[0:NG // 2, :]).then_inc(base_out, 16)
            sync.wait_ge(base_out, 32)
            nc.sync.dma_start(g_base[:, GP:], g_base_d.unsqueeze(0).to_broadcast([P, NG])).then_inc(base_in, 16)
            nc.sync.dma_start(h_base[:, :], h_base_d.unsqueeze(0).to_broadcast([P, NH])).then_inc(base_in, 16)
            sync.wait_ge(rel_ready, 1)
            nc.sync.dma_start(dst_d.rearrange("(p e) -> p e", p=NG // 2),
                              rel_rows[0:NG // 2, :, :].rearrange("p h e -> p (h e)")).then_inc(rel_out, 16)

            load(w_hid[0:D, 0:HID0], w0_in[0:D, :])
            load(w_hid[0:D, HID0:2 * HID0], w0_in[D:2 * D, :])
            load(w_hid[2 * D:3 * D, 0:HID0], w0_in[D:2 * D, :])
            load(w_hid[2 * D:3 * D, HID0:2 * HID0], w0_in[0:D, :])
            for s in range(2):
                load(w_ref[s * HID0:(s + 1) * HID0, s * D:(s + 1) * D], w0_out)
                load(bias_hid[s * HID0:(s + 1) * HID0, :], b0_in.unsqueeze(1))
                load(bias_ref[:, s, :], b0_out.unsqueeze(0).to_broadcast([P, D]))
            load(bias_f[:, :], b0_out.unsqueeze(0).to_broadcast([3, D]))
            for a in range(LO):
                h, r = a // 4, a % 4
                load(w1_diag[a * D:(a + 1) * D, h, r * HID1:(r + 1) * HID1], w1)
                load(w2_diag[r * HID1:(r + 1) * HID1, h, a * D:(a + 1) * D], w2)
            for r in range(4):
                for j, vec in enumerate((b1, gamma, beta)):
                    load(bn_vec[r * HID1:(r + 1) * HID1, j:j + 1], vec.unsqueeze(1))
            load(bias_out[:, :], b2.unsqueeze(0).to_broadcast([P, D]))

            sync.wait_ge(hist_sb, 1)
            nc.sync.dma_start(hist_d.rearrange("s (p q) -> p s q", q=QLO), hist[:, :, :]).then_inc(hist_out, 16)
            sync.wait_ge(hist_out, 16)
            for s in range(2):
                nc.sync.dma_start(cnt[:, s, 0:NT - 1, :],
                                  hist_d[s, 0:m].rearrange("(t b a) -> b t a", b=P, a=LO)).then_inc(hist_in, 16)
                nc.sync.dma_start(cnt[0:KR, s, NT - 1, :],
                                  hist_d[s, m:m + KR * LO].rearrange("(b a) -> b a", a=LO)).then_inc(hist_in, 16)
                nc.sync.dma_start(cnt[KR:KR + 1, s, NT - 1, 0:left],
                                  hist_d[s, m + KR * LO:N_NODES].rearrange("(b a) -> b a", b=1)).then_inc(hist_in, 16)

            def store_table(k, tile):
                sync.wait_ge(tab_ready[k], 1 if k else 2)
                nc.sync.dma_start(table[k][0:m, :].rearrange("(t b a) f -> b t (a f)", b=P, a=LO),
                                  tile[:, 0:NT - 1, :]).then_inc(tab_out[k], 16)
                nc.sync.dma_start(table[k][m:NB * LO, :].rearrange("(b a) f -> b (a f)", a=LO),
                                  tile[0:TAIL, NT - 1, :]).then_inc(tab_out[k], 16)

            sync.wait_ge(xp_ready, 6)
            sync.wait_ge(tab_ready[0], 1)
            ft = f_tab[:, :, :].rearrange("p (t a) f -> p t (a f)", a=LO)
            nc.sync.dma_start(f_table[0:m, :].rearrange("(t b a) f -> b t (a f)", b=P, a=LO),
                              ft[:, 0:NT - 1, :]).then_inc(f_tab_out, 16)
            nc.sync.dma_start(f_table[m:NB * LO, :].rearrange("(b a) f -> b (a f)", a=LO),
                              ft[0:TAIL, NT - 1, :]).then_inc(f_tab_out, 16)
            sync.wait_ge(proj_sb, 1)
            for k in range(SPLIT):
                wt = w_table[:, k, :, :].rearrange("p (t a) f -> p t (a f)", a=LO)
                nc.sync.dma_start(w_rows[k, 0:m, :].rearrange("(t b a) f -> b t (a f)", b=P, a=LO),
                                  wt[:, 0:NT - 1, :]).then_inc(proj_out, 16)
                nc.sync.dma_start(w_rows[k, m:NB * LO, :].rearrange("(b a) f -> b (a f)", a=LO),
                                  wt[0:TAIL, NT - 1, :]).then_inc(proj_out, 16)
            nc.sync.dma_start(w_rows[:, NB * LO:NB * LO + WG, :].rearrange("k n f -> n k f"),
                              no_rows[:, :].unsqueeze(1).to_broadcast([WG, SPLIT, WROW])).then_inc(proj_out, 16)
            sync.wait_ge(proj_out, PROJ_OUT)
            sync.wait_ge(rel_out, 16)
            sync.wait_ge(flag_ready, 1)
            fast = sync.value_load(flag[0:1, 0:1], min_val=0, max_val=1)
            with sync.If(fast > 0):
                def windows(i, slots):
                    n = 2 * len(slots)
                    _, bases = nc.values_load_multi_w_load_instructions(
                        g_base[0:1, bass.ds(i * (2 * SLOTS) + GP, n)], engines=(SP,), min_val=0, max_val=NB * LO - 1,
                        skip_runtime_bounds_check_because=BASES_ARE_NODES)
                    for q in range(n):
                        sync.wait_ge(f_front, i * (2 * SLOTS) + q + 1)
                        sync.nop(nofuse=True)
                        nc.sync.dma_start(f_win[0:KDST, q, :], w_rows[:, bass.ds(bases[q], WG), :]).then_inc(f_in[q], 16)
                        nc.sync.dma_start(f_dst[0:KDST, q, :],
                                          dst_d[bass.ds(i * (2 * SLOTS * G * P) + q * G * P, G * P)].unsqueeze(0)
                                          .to_broadcast([KDST, G * P])).then_inc(f_in[q], 16)

                with sync.Fori(0, TURNS) as i:
                    windows(i, range(SLOTS))
                windows(TURNS, range(NPAIR - TURNS * SLOTS))
            with sync.Else():
                store_table(0, tab[:, :, :, :].rearrange("p t a f -> p t (a f)"))

            for k in (1, 2):
                store_table(k, y_n[:, :, :].rearrange("p (t a) f -> p t (a f)", a=LO))
                with sync.If(fast > 0):
                    sync.wait_ge(tab_out[k], 32)
                    nc.sync.dma_start(y_hl[:, 0:NHI - 1, :],
                                      table[k][0:(NHI - 1) * LANES, :].rearrange("(h l) f -> l h f", l=LANES)).then_inc(hl_in[k - 1], 16)
                    nc.sync.dma_start(y_hl[0:NB * LO - (NHI - 1) * LANES, NHI - 1, :],
                                      table[k][(NHI - 1) * LANES:NB * LO, :]).then_inc(hl_in[k - 1], 16)
            sync.wait_ge(out_ready, 1)
            nc.sync.dma_start(out[0:m, :].rearrange("(t b a) f -> b t (a f)", b=P, a=LO),
                              s_n[:, 0:(NT - 1) * LO, :].rearrange("p (t a) f -> p t (a f)", a=LO)).then_inc(stored, 16)
            nc.sync.dma_start(out[m:m + KR * LO, :].rearrange("(b a) f -> b (a f)", a=LO),
                              s_n[0:KR, (NT - 1) * LO:NT * LO, :].rearrange("p a f -> p (a f)")).then_inc(stored, 16)
            nc.sync.dma_start(out[m + KR * LO:N_NODES, :].rearrange("(b a) f -> b (a f)", b=1),
                              s_n[KR:KR + 1, (NT - 1) * LO:(NT - 1) * LO + left, :]
                              .rearrange("p a f -> p (a f)")).then_inc(stored, 16)
            sync.wait_ge(stored, 48)
        @block.gpsimd
        def _(pool):
            for tile in (x_n, w_proj, cnt, w_hid, w_ref, w1_diag, w2_diag):
                ins = nc.gpsimd.memset(tile[tuple(slice(None) for _ in tile.shape)], 0.0)
            ins.then_inc(padded_pool, 1)
            pool.wait_ge(nodes_in, n_loads[nodes_in])
            pool.wait_ge(padded, 2)
            pieces = f_tab[:, :, 0:YS].bitcast(BF16)
            nc.gpsimd.tensor_copy(pieces[:, :, 0:D], x_n[:, :, :]).then_inc(xp_ready, 1)
            pool.wait_ge(xp_ready, 1)
            nc.gpsimd.tensor_tensor(xp_rest[:, :, :], x_n[:, :, :], pieces[:, :, 0:D], ALU.subtract).then_inc(xp_ready, 1)
            pool.wait_ge(xp_ready, 2)
            nc.gpsimd.tensor_copy(pieces[:, :, D:2 * D], xp_rest[:, :, :]).then_inc(xp_ready, 1)
            pool.wait_ge(xp_ready, 3)
            nc.gpsimd.tensor_tensor(pieces[:, :, 2 * D:3 * D], xp_rest[:, :, :], pieces[:, :, D:2 * D],
                                    ALU.subtract).then_inc(xp_ready, 1)
            pool.wait_ge(xp_ready, 4)
            nc.gpsimd.tensor_copy(pieces[:, :, 3 * D:6 * D].rearrange("p n (k f) -> p n k f", f=D),
                                  pieces[:, :, 2 * D:3 * D].unsqueeze(2).to_broadcast([P, NT * LO, 3, D])).then_inc(xp_ready, 1)
            nc.gpsimd.tensor_copy(pieces[:, :, 6 * D:8 * D], pieces[:, :, 0:2 * D]).then_inc(xp_ready, 1)
            part_t = w_table[:, :, :, 0:2 * HID0]
            pool.wait_ge(win_w, 2 * NT)
            for t in range(NT):
                w = min(P, NB - t * P)
                k = slice(t * LO, (t + 1) * LO)
                nc.gpsimd.tensor_tensor(w_proj_f[0:w, k, :], w_proj_f[0:w, k, :], part_t[0:w, 0, k, :],
                                        ALU.subtract).then_inc(pool_step, 1)
                pool.wait_ge(pool_step, 3 * t + 1)
                nc.gpsimd.tensor_copy(part_t[0:w, 1, k, :], w_proj_f[0:w, k, :]).then_inc(pool_step, 1)
                pool.wait_ge(pool_step, 3 * t + 2)
                nc.gpsimd.tensor_tensor(part_t[0:w, 2, k, :], w_proj_f[0:w, k, :], part_t[0:w, 1, k, :],
                                        ALU.subtract).then_inc(pool_step, 1)
            pool.wait_ge(pool_step, 3 * NT)
            nc.gpsimd.memset(no_rows[:, :], 0.0)
            nc.gpsimd.memset(counts_f[:, table_words:words_end], 0.0).then_inc(parts_ready, 1)
            pool.wait_ge(parts, 1)
            pool.wait_ge(f_tab_out, 32)
            pool.wait_ge(flag_ready, 1)
            fast = pool.value_load(flag[0:1, 0:1], min_val=0, max_val=1)
            with pool.If(fast > 0):
                for _ in range(SLOTS):
                    pool.sem_inc(f_free, 1)

                def gather(i, m):
                    j = i * SLOTS + m
                    pool.wait_ge(f_free, j + 1)
                    nc.gpsimd.tensor_copy(f_stage[:, m, :], node_i[:, 0, bass.ds(j * (2 * G), 2 * G)]).then_inc(f_staged, 1)
                    pool.wait_ge(f_staged, j + 1)
                    pool.nop(nofuse=True)
                    for c in range(2 * G):
                        nc.gpsimd.indirect_dma_start(
                            out=f_rows[:, m, c, 0:FROW], out_offset=None, in_=f_table,
                            in_offset=bass.IndirectOffsetOnAxis(ap=f_stage[:, m, c:c + 1], axis=0)
                        ).then_inc(f_gath[m], 16)

                with pool.Fori(0, TURNS) as i:
                    for m in range(SLOTS):
                        gather(i, m)
                for m in range(NPAIR - TURNS * SLOTS):
                    gather(TURNS, m)
                pool.wait_ge(acc_ready[3], 1)
                pool.wait_ge(dst_added, 1)
                nc.gpsimd.memset(counts_f[:, shares[0][0]:shares[0][1]], 0.0).then_inc(zeroed, 1)
                for _ in range(8):
                    pool.sem_inc(c_lo, 1)
                with pool.Fori(0, NH // 8) as i:
                    pool.wait_ge(c_lo, i * 8 + 8)
                    pool.nop(nofuse=True)
                    nc.gpsimd.tensor_copy(lo_stage[:, :], lo_f[:, bass.ds(i * 16, 16)]).then_inc(c_los, 1)
                    pool.wait_ge(c_los, i + 1)
                    pool.nop(nofuse=True)
                    for r in range(8):
                        pool.wait_ge(c_ps, i * 8 + r + 1)
                        pool.nop(nofuse=True)
                        for c in range(1 + (r in POOLS_HALVES)):
                            ins = nc.gpsimd.tensor_scalar(oh_lo[:, r, c, :], iota_k[:, 0:LANES],
                                                          lo_stage[:, 2 * r + c:2 * r + c + 1], None, ALU.is_equal)
                        ins.then_inc(c_lo, 1)
            with pool.Else():
                pool.wait_ge(proj_out, PROJ_OUT)
                pool.wait_ge(tab_out[0], 32)
                for u in range(2):
                    pool.sem_inc(g_free_dve, 1)
                with pool.Fori(0, NG // 2) as i:
                    for u in range(2):
                        pool.wait_ge(turned, 2 * i + u + 1)
                        nc.gpsimd.tensor_copy(idx_stage[:, u, :, :],
                                              node_i[:, :, bass.ds(i * (2 * G) + u * G, G)]).then_inc(staged, 1)
                        pool.wait_ge(staged, 2 * i + u + 1)
                        pool.nop(nofuse=True)
                        pool.wait_ge(g_free_dve, 2 * i + u + 1)
                        pool.nop(nofuse=True)
                        for c in range(G):
                            for s in range(2):
                                nc.gpsimd.indirect_dma_start(
                                    out=g_xy[:, u, c, s, :], out_offset=None, in_=table[0],
                                    in_offset=bass.IndirectOffsetOnAxis(ap=idx_stage[:, u, s, c:c + 1], axis=0)
                                ).then_inc(gathered[u], 16)
                for k in range(2):
                    pool.wait_ge(tab_out[k + 1], 32)
                    for u in range(2):
                        pool.sem_inc(l_free[k], 1)
                    with pool.Fori(0, NG // 2) as i:
                        for u in range(2):
                            pool.wait_ge(l_free[k], 2 * i + u + 1)
                            nc.gpsimd.tensor_copy(idx_stage[:, u, 0, :],
                                                  node_i[:, 0, bass.ds(i * (2 * G) + u * G, G)]).then_inc(l_staged[k], 1)
                            pool.wait_ge(l_staged[k], 2 * i + u + 1)
                            pool.nop(nofuse=True)
                            for c in range(G):
                                nc.gpsimd.indirect_dma_start(
                                    out=g_xy[:, u, c, 0, 0:D], out_offset=None, in_=table[k + 1],
                                    in_offset=bass.IndirectOffsetOnAxis(ap=idx_stage[:, u, 0, c:c + 1], axis=0)
                                ).then_inc(l_gathered[k][u], 16)

        @block.scalar
        def _(act):
            def front(n, u):
                act.wait_ge(turned, 2 * n + u + 1)
                nc.scalar.activation(xT[:, u, :], p_tr[u][0:64, :], ACT.Copy).then_inc(x_ready, 1)
                act.wait_ge(pre_ready, 2 * n + u - 1)
                nc.scalar.activation(hidT[:, u, :], p_hid[u][:, :], ACT.Relu,
                                     bias=bias_hid[:, 0:1]).then_inc(hid_ready, 1)

            act.wait_ge(xa_ps, 1)
            nc.scalar.activation(xa[:, :], misc[:, 0:NB], ACT.Copy).then_inc(xa_sb, 1)
            for t in range(NT):
                w = min(P, NB - t * P)
                for h in range(2):
                    k = t * LO + 4 * h
                    act.wait_ge(proj_ps, 2 * t + h + 1)
                    ps = p_tr[h][0:w, :].rearrange("p (a n) -> p a n", a=4)
                    nc.scalar.activation(w_table[0:w, 0, k:k + 4, 0:2 * HID0], ps, ACT.Copy)
                    nc.scalar.activation(w_proj_f[0:w, k:k + 4, :], ps, ACT.Copy).then_inc(win_w, 1)
            act.wait_ge(deg_ready, 1)
            nc.scalar.activation(dinv[:, :, :], dinv[:, :, :], ACT.Sqrt).then_inc(deg_root, 1)
            act.wait_ge(loaded, n_loads[loaded])
            act.wait_ge(flag_ready, 1)
            act.wait_ge(proj_out, PROJ_OUT)
            act.wait_ge(f_tab_out, 32)
            fast = act.value_load(flag[0:1, 0:1], min_val=0, max_val=1)

            def clear_counts(k):
                a, b = shares[k]
                nc.scalar.activation(counts_f[:, a:b], zeros[:, 0:1].to_broadcast([P, b - a]), ACT.Copy).then_inc(zeroed, 1)

            def rows_out(i, m):
                j = i * SLOTS + m
                for gg in range(2):
                    act.wait_ge(f_turned, j * 2 + gg + 1)
                    turned_b = p_tr[gg][:, 0:G * P // 2].bitcast(BF16)
                    nc.scalar.activation(f_xT[:, gg, :], turned_b, ACT.Copy)
                    nc.scalar.activation(f_ohT[P - KLAST:P, 2 * (m % SLOTS) + gg, :], turned_b[P - KLAST:P, :],
                                         ACT.Copy).then_inc(f_xready, 1)

            def fast_front(i, m, ahead=True):
                j, w = i * SLOTS + m, m % 2
                for gg in range(2):
                    act.wait_ge(f_pre, j * 2 + gg + 1)
                    nc.scalar.activation(f_hid[:, gg, :], p_hid[gg][:, :], ACT.Relu,
                                         bias=bias_hid[:, 0:1]).then_inc(f_relu, 1)
                if ahead:
                    rows_out(i, m + 1)
                act.wait_ge(f_ref, j + 1)
                nc.scalar.activation(f_rows[:, m, :, FROW:FROW + D],
                                     p_ref[w][:, 4 * G * D:6 * G * D].rearrange("p (c f) -> p c f", f=D), ACT.Copy).then_inc(f_sqr, 1)
                act.wait_ge(f_sqd, j + 1)
                nc.scalar.activation(f_sq[:, w, :, :], p_ref[w][:, 0:4 * G * D].rearrange("p (c f) -> p c f", f=D),
                                     ACT.Square).then_inc(f_sqr, 1)

            with act.If(fast > 0):
                rows_out(0, 0)
                with act.Fori(0, TURNS) as i:
                    for m in range(SLOTS):
                        fast_front(i, m)
                for m in range(NPAIR - TURNS * SLOTS):
                    fast_front(TURNS, m, TURNS * SLOTS + m + 1 < NPAIR)
                act.wait_ge(acc_ready[3], 1)
                act.wait_ge(dst_added, 1)
                clear_counts(1)
            with act.Else():
                act.wait_ge(tab_out[0], 32)
                with act.Fori(0, NG // 2) as i:
                    front(i + 1, 0)
                    front(i + 1, 1)

            def root(k):
                act.wait_ge(root_in[k], 1)
                nc.scalar.activation(st[:, 2, :], st[:, 2, :], ACT.Sqrt).then_inc(root_out[k], 1)

            def build_counts():
                clear_counts(2)
                with act.Fori(0, NH // 8) as i:
                    for r in range(8):
                        act.wait_ge(c_ps, i * 8 + r + 9)
                        act.nop(nofuse=True)
                        act.wait_ge(c_added, i * 8 + r + 1)
                        nc.scalar.activation(cnt_stage[:, r % 4, :], banks[r][:, 0:NKEY], ACT.Copy).then_inc(c_sb, 1)

            def product(k):
                with act.If(fast > 0):
                    if k == 0:
                        build_counts()
                    for blk in range(1, NBLK, 2):
                        act.wait_ge(sp_ps[k], blk + 1)
                        nc.scalar.activation(agg3[:, blk * BLK:(blk + 1) * BLK], banks[blk][0:3 * D, 0:BLK],
                                             ACT.Copy).then_inc(sp_act[k], 1)

            root(0)
            product(0)
            act.wait_ge(root_in[1], 1)
            nc.scalar.activation(bn[:, 3:4], bn[:, 3:4], ACT.Sqrt).then_inc(root_out[1], 1)
            act.wait_ge(bn_ready, 1)
            for h in range(2):
                nc.scalar.activation(h_al[:, h, :], hc_al[:, h, :], ACT.Relu, scale=bn[:, 5:6],
                                     bias=bn_vec[:, 2:3]).then_inc(relu_ready, 1)
            product(1)
            root(2)

        @block.vector
        def _(vec):
            counted = {dve: 0, dve_fast: 0, dve_general: 0}

            def step(ins, at=None, on=dve):
                counted[on] += 1
                ins.then_inc(on, 1)
                vec.wait_ge(on, counted[on] if at is None else at[0] * at[1] + counted[on])

            def tick(ins, on):
                counted[on] += 1
                ins.then_inc(on, 1)

            def settle(on, at=None):
                vec.wait_ge(on, counted[on] if at is None else at[0] * at[1] + counted[on])

            V = nc.vector

            def cover(tiles):
                for tile, value in tiles:
                    ins = V.memset(tile[tuple(slice(None) for _ in tile.shape)], value)
                return ins

            cover(((rows_i, PAD), (dst_rows, PAD))).then_inc(padded, 1)
            cover(((zeros, 0.0), (ones3, 1.0), (g_base, 0), (f_win, 0.0), (viol, 0.0), (tab, 0.0), (f_tab, 0.0),
                   (s_n, 0.0))).then_inc(padded, 1)
            vec.wait_ge(padded, 2)
            vec.wait_ge(idx_in, n_loads[idx_in])
            V.tensor_copy(rows_f[:, :, :, :], rows_i[:, :, :, :]).then_inc(idx_rows, 1)
            step(V.tensor_copy(iota_q[:, :, :], iota_b[:, 0:QLO].unsqueeze(2).to_broadcast([P, QLO, HG])))
            step(V.tensor_copy(ident_b[:, :], ident))
            halves = NG // 2
            step(V.tensor_reduce(h_base_i[0:halves, :], dst_rows[0:halves, :, :], AX.X, ALU.min))
            V.tensor_reduce(h_top[0:halves, :], dst_rows[0:halves, :, :], AX.X, ALU.max)
            step(V.tensor_scalar(h_base_i[0:halves, :], h_base_i[0:halves, :], -2, None, ALU.bitwise_and))
            step(V.tensor_copy(h_base_f[0:halves, :], h_base_i[0:halves, :]))
            hb = h_base_f[0:halves, :].rearrange("p (g h) -> p g h", h=2)
            ht = h_top[0:halves, :].rearrange("p (g h) -> p g h", h=2)
            V.tensor_tensor(g_top[0:halves, :], ht[:, :, 0], ht[:, :, 1], ALU.max)
            V.tensor_tensor(g_base_i[0:halves, :], hb[:, :, 0], hb[:, :, 1], ALU.min).then_inc(base_ready, 1)
            vec.wait_ge(base_ready, 1)
            V.tensor_tensor(viol[0:halves, 0:4], h_top[0:halves, :], h_base_f[0:halves, :], ALU.subtract)
            step(V.tensor_tensor(viol[0:halves, 4:6], g_top[0:halves, :], g_base_i[0:halves, :], ALU.subtract))
            step(V.tensor_scalar(viol[0:halves, 0:4], viol[0:halves, 0:4], float(WH), None, ALU.is_ge))
            step(V.tensor_scalar(viol[0:halves, 4:6], viol[0:halves, 4:6], float(WG), None, ALU.is_ge))
            step(V.tensor_copy(g_base_f[0:halves, :], g_base_i[0:halves, :]))
            dr = dst_rows[0:halves, :, :].rearrange("p (g h) e -> p g (h e)", h=2)
            V.tensor_tensor(rel_rows[0:halves, :, :], dr, g_base_f[0:halves, :].unsqueeze(2).to_broadcast([halves, 2, G * P]),
                            ALU.subtract).then_inc(rel_ready, 1)
            vec.wait_ge(idx_cols, 1)
            for s in range(2):
                for t in range(2):
                    w = min(4 * P, NCH - t * 4 * P)
                    ins = V.tensor_copy(node_i[:, s, t * 4 * P:t * 4 * P + w], banks[1 + 2 * s + t][:, 0:w])
            ins.then_inc(q_ready, 1)
            vec.wait_ge(q_ready, 1)
            def part_of_node(side, mask, shift, to, on=dve):
                some = part_i[:, side, :]
                if shift is None:
                    step(V.tensor_scalar(some, node_i[:, side, :], mask, None, ALU.bitwise_and), on=on)
                else:
                    step(V.tensor_scalar(some, node_i[:, side, :], shift, None, ALU.logical_shift_right), on=on)
                step(V.tensor_copy(to[:, side, :], some), on=on)

            both = slice(0, 2)
            part_of_node(both, QLO - 1, None, q_bf)
            part_of_node(both, None, 6, p_bf)
            vec.wait_ge(nodes_in, n_loads[nodes_in])
            step(V.tensor_copy(w_parts[:, 0, :], w_f32[:, :]))
            step(V.tensor_tensor(w_f32[:, :], w_f32[:, :], w_parts[:, 0, :], ALU.subtract))
            step(V.tensor_copy(w_parts[:, 1, :], w_f32[:, :]))
            step(V.tensor_tensor(w_parts[:, 2, :], w_f32[:, :], w_parts[:, 1, :], ALU.subtract))
            step(V.tensor_scalar(w_all[:, :], w_parts[:, 0, :], part_of[:, 0:1], None, ALU.mult))
            for r in (1, 2):
                step(V.scalar_tensor_tensor(w_all[:, :], w_parts[:, r, :], part_of[:, r:r + 1], w_all[:, :], ALU.mult, ALU.add))
            step(V.tensor_copy(f_win[P - KLAST:P, :, 0:2 * HID0],
                               w_parts[P - KLAST:P, 2, :].unsqueeze(1).to_broadcast([KLAST, 2 * SLOTS, 2 * HID0])))
            with vec.Fori(0, NCH // HG) as i:
                for s in range(2):
                    vec.wait_ge(hist_used[s], i + 1)
                    V.tensor_tensor(oh_q[:, s, :, :], q_bf[:, s, bass.ds(i * HG, HG)].unsqueeze(1).to_broadcast([P, QLO, HG]),
                                    iota_q[:, :, :], ALU.is_equal)
                    V.tensor_tensor(oh_p[:, s, :, :], p_bf[:, s, bass.ds(i * HG, HG)].unsqueeze(1).to_broadcast([P, NQ, HG]),
                                    iota_q[:, 0:NQ, :], ALU.is_equal).then_inc(oh_hist[s], 1)
            vec.wait_ge(hist_done, 1)
            V.tensor_copy(hist[:, :, :], misc[0:NQ, 0:2 * QLO].rearrange("p (s q) -> p s q", s=2)).then_inc(hist_sb, 1)
            part_of_node(0, LO - 1, None, a_f)
            part_of_node(0, None, 3, b_f)
            step(V.tensor_scalar(part_i[:, 0, :], node_i[:, 0, :], LANES - 1, None, ALU.bitwise_and))
            step(V.tensor_copy(lo_f[:, :], part_i[:, 0, :]))
            step(V.tensor_scalar(part_i[:, 0, :], node_i[:, 0, :], 7, None, ALU.logical_shift_right))
            vec.wait_ge(base_in, 32)
            step(V.tensor_tensor(dst_rel[:, :].rearrange("p (h c) -> p h c", c=2),
                                 node_i[:, 1, :].rearrange("p (h c) -> p h c", c=2),
                                 h_base[:, :].unsqueeze(2).to_broadcast([P, NH, 2]), ALU.subtract))
            step(V.scalar_tensor_tensor(key_f[:, :], part_i[:, 0, :], float(WH), dst_rel[:, :], ALU.mult, ALU.add))
            V.tensor_tensor(dst_rel[:, :].rearrange("p (g c) -> p g c", c=G),
                            node_i[:, 1, :].rearrange("p (g c) -> p g c", c=G),
                            g_base[:, GP:].unsqueeze(2).to_broadcast([P, NG, G]), ALU.subtract)
            V.tensor_copy(iota_h[:, :], iota_k[:, 0:NKEY]).then_inc(parts, 1)
            vec.wait_ge(hist_in, 96)
            c2 = cnt[:, :, :, :].rearrange("p s t a -> p s (t a)")
            step(V.tensor_reduce(viol[:, 6:7], c2[:, 1, :], AX.X, ALU.max))
            step(V.tensor_scalar(viol[:, 6:7], viol[:, 6:7], MAX_COUNT + 0.5, None, ALU.is_ge))
            V.tensor_reduce(viol[:, 7:8], viol[:, 0:7], AX.X, ALU.add).then_inc(viol_ready, 1)
            step(V.tensor_tensor(dinv[:, 0, :], c2[:, 0, :], c2[:, 1, :], ALU.add))
            V.tensor_scalar(dinv[:, 0, :], dinv[:, 0, :], 1e-5, None, ALU.max)
            V.tensor_scalar(dinv[:, 1, :], c2[:, 1, :], 1.0, None, ALU.add).then_inc(deg_ready, 1)
            vec.wait_ge(deg_root, 1)
            step(V.reciprocal(dinv[:, :, :], dinv[:, :, :]))
            d0 = dinv[:, 0, :].unsqueeze(2).to_broadcast([P, NT * LO, D])
            d1 = dinv[:, 1, :].unsqueeze(2).to_broadcast([P, NT * LO, D])
            y_f = f_tab[:, :, YS:FROW]
            V.tensor_tensor(y_f, x_n[:, :, :], d0, ALU.mult).then_inc(tab_ready[0], 1)
            vec.wait_ge(tab_ready[0], 1)
            part_y = w_table[:, :, :, 2 * HID0:]
            step(V.tensor_copy(part_y[:, 0, :, :], y_f))
            step(V.tensor_tensor(x_rest[:, :, :], y_f, part_y[:, 0, :, :], ALU.subtract))
            step(V.tensor_copy(part_y[:, 1, :, :], x_rest[:, :, :]))
            vec.wait_ge(parts_ready, 1)
            V.tensor_tensor(part_y[:, 2, :, :], x_rest[:, :, :], part_y[:, 1, :, :], ALU.subtract).then_inc(proj_sb, 1)
            tabv = tab[:, :, :, :].rearrange("p t a f -> p (t a) f")
            V.tensor_copy(tabv[:, :, 0:D], x_n[:, :, :])
            V.tensor_copy(tabv[:, :, D:2 * D], y_f).then_inc(tab_ready[0], 1)
            vec.wait_ge(viol_sum, 1)
            V.tensor_scalar(flag[0:1, 0:1], p_hid[0][0:1, 0:1], 0.5, None, ALU.is_le).then_inc(flag_ready, 1)
            vec.wait_ge(flag_ready, 1)
            vec.wait_ge(loaded, n_loads[loaded])
            step(V.tensor_copy(bias_parts[:, 0, :], bias_f[:, :]))
            step(V.tensor_tensor(bias_rest[:, :], bias_f[:, :], bias_parts[:, 0, :], ALU.subtract))
            step(V.tensor_copy(bias_parts[:, 1, :], bias_rest[:, :]))
            step(V.tensor_tensor(bias_parts[:, 2, :], bias_rest[:, :], bias_parts[:, 1, :], ALU.subtract))
            step(V.tensor_scalar(bias_parts[:, 0, :], bias_parts[:, 0, :], ident[0:3, 0:1], None, ALU.mult))
            for r in (1, 2):
                step(V.scalar_tensor_tensor(bias_parts[:, 0, :], bias_parts[:, r, :], ident[0:3, r:r + 1], bias_parts[:, 0, :], ALU.mult, ALU.add))
            V.tensor_copy(bias3[:, :].rearrange("p (c f) -> p c f", f=D),
                          bias_parts[:, 0, :].unsqueeze(1).to_broadcast([3, 4 * G, D])).then_inc(w_ready, 1)
            vec.wait_ge(proj_out, PROJ_OUT)
            vec.wait_ge(f_tab_out, 32)
            fast = vec.value_load(flag[0:1, 0:1], min_val=0, max_val=1)

            def bcast(t):
                return t.unsqueeze(2).to_broadcast([P, G * 2, D])

            def reflect(n, u, at):
                vec.wait_ge(ref_ready, 2 * n + u - 1)
                ins = V.tensor_tensor(v[:, :, :], p_ref[u][:, 0:G * 2 * D].rearrange("p (c f) -> p c f", f=D),
                                      bias_rep[:, 0:2 * G, :], ALU.add)
                ins.then_inc(v_taken, 1)
                vec.wait_ge(v_taken, 2 * n + u + 1)
                step(V.tensor_tensor(prod[:, :, :], v[:, :, :], v[:, :, :], ALU.mult), at, dve_general)
                step(V.tensor_reduce(n2[:, :], prod[:, :, :], AX.X, ALU.add), at, dve_general)
                step(V.tensor_scalar(n2[:, :], n2[:, :], 1e-24, 0.5, ALU.max, ALU.mult), at, dve_general)
                step(V.reciprocal(cc[:, :], n2[:, :]), at, dve_general)
                vec.wait_ge(gathered[u], n * (16 * 2 * G))
                y = g_xy[:, u, :, :, D:2 * D].rearrange("p c s f -> p (c s) f")
                step(V.tensor_tensor(prod[:, :, :], v[:, :, :], y, ALU.mult), at, dve_general)
                step(V.tensor_reduce(dots[:, :], prod[:, :, :], AX.X, ALU.add), at, dve_general)
                step(V.tensor_tensor(dots[:, :], dots[:, :], cc[:, :], ALU.mult), at, dve_general)
                step(V.tensor_tensor(prod[:, :, :], v[:, :, :], bcast(dots[:, :]), ALU.mult), at, dve_general)
                for s in range(2):
                    ins = V.tensor_tensor(z[:, :, 1 - s, :], g_xy[:, u, :, s, D:2 * D],
                                          prod[:, :, :].rearrange("p (c s) f -> p c s f", s=2)[:, :, s, :], ALU.subtract)
                ins.then_inc(g_free_dve, 1)
                vec.wait_ge(g_free_dve, 2 * n + u + 1)
                zz = z[:, :, :, :].rearrange("p c s f -> p (c s) f")
                step(V.tensor_tensor(prod[:, :, :], v[:, :, :], zz, ALU.mult), at, dve_general)
                step(V.tensor_reduce(dots[:, :], prod[:, :, :], AX.X, ALU.add), at, dve_general)
                step(V.tensor_tensor(dots[:, :], dots[:, :], cc[:, :], ALU.mult), at, dve_general)
                step(V.tensor_tensor(prod[:, :, :], v[:, :, :], bcast(dots[:, :]), ALU.mult), at, dve_general)
                V.tensor_tensor(msg[:, u, :, :], zz, prod[:, :, :], ALU.subtract)
                for s in range(2):
                    ins = V.tensor_tensor(oh_a[:, u, :, :].rearrange("p (c s) a -> p c s a", s=2)[:, :, s, :],
                                          a_f[:, s, bass.ds(at[2], G)].unsqueeze(2).to_broadcast([P, G, LO]),
                                          iota_b[:, 0:LO].unsqueeze(1).to_broadcast([P, G, LO]), ALU.is_equal)
                step(ins, at, dve_general)
                V.tensor_tensor(m8[:, u, :, :, :], oh_a[:, u, :, :].unsqueeze(3).to_broadcast([P, G * 2, LO, D]),
                                msg[:, u, :, :].unsqueeze(2).to_broadcast([P, G * 2, LO, D]),
                                ALU.mult).then_inc(m_ready, 1)

            def one_hots(n, r0, sides, chunk, ready, used):
                for c in range(G):
                    for s in sides:
                        r = r0 % RING
                        vec.wait_ge(used, n + r0)
                        V.tensor_scalar(oh_b[:, r, :], iota_b, b_f[:, s, bass.ds(chunk + c, 1)], None,
                                        ALU.is_equal).then_inc(ready, 1)
                        r0 += 1
                return r0

            def fb(t):
                return t.unsqueeze(2).to_broadcast([P, 4 * G, D])

            def dst_one_hots(i, m, gg):
                q, turn = 2 * (m % SLOTS) + gg, i + m // SLOTS
                vec.wait_ge(f_in[q], turn * 32 + 32)
                V.tensor_scalar(f_ohT[0:KDST, q, :], f_dst[0:KDST, q, :], lane32[0:KDST, :], None, ALU.is_equal).then_inc(f_ohdt, 1)

            def add_window(j, w, gg, base):
                vec.wait_ge(f_wadd, j * 2 + gg + 1)
                k = 2 * (1 - w) + gg
                V.tensor_tensor(acc_dst[:, bass.ds(base, WG)], acc_dst[:, bass.ds(base, WG)],
                                misc[0:D, k * WG:(k + 1) * WG], ALU.add).then_inc(f_wadd, 1)

            def src_one_hot(j, m, c):
                vec.wait_ge(f_ohu, j * (2 * G) + c + 1)
                V.tensor_scalar(f_ohb[:, (m * 2 * G + c) % FRING, :], iota_b, b_f[:, 0, bass.ds(j * (2 * G) + c, 1)], None,
                                ALU.is_equal).then_inc(f_oh, 1)

            def fast_pair(i, m, ahead, bases, at):
                j, w, on = i * SLOTS + m, m % 2, dve_fast
                v_ps = p_ref[w][:, 0:4 * G * D].rearrange("p (c f) -> p c f", f=D)
                prod2 = f_prod[:, :, :].rearrange("p (c s) f -> p c s f", s=2)
                zz = f_z[:, :, :, :].rearrange("p c s f -> p (c s) f")
                vec.wait_ge(f_sqr, j * 2 + 2)
                V.tensor_reduce(f_n2[:, :], f_sq[:, w, :, :], AX.X, ALU.add).then_inc(f_sqd, 1)
                src_one_hot(j, m, 0)
                vec.wait_ge(f_sqd, j + 3)
                tick(V.tensor_scalar(f_n2[:, :], f_n2[:, :], 1e-24, 0.5, ALU.max, ALU.mult), on)
                V.tensor_tensor(f_prod[:, :, :].rearrange("p (c s) f -> p c (s f)", s=2),
                                p_ref[w][:, 0:4 * G * D].rearrange("p (c n) -> p c n", n=2 * D),
                                f_rows[:, m, :, YS:YS + 2 * D], ALU.mult)
                settle(on, at)
                tick(V.reciprocal(f_cc[:, :], f_n2[:, :]), on)
                settle(on, at)
                tick(V.tensor_reduce(f_dots[:, :], f_prod[:, :, :], AX.X, ALU.add), on)
                src_one_hot(j, m, 1)
                settle(on, at)
                tick(V.tensor_tensor(f_dots[:, :], f_dots[:, :], f_cc[:, :], ALU.mult), on)
                if ahead:
                    dst_one_hots(i, m + 2, 0)
                else:
                    src_one_hot(j, m, 2)
                settle(on, at)
                tick(V.tensor_tensor(f_prod[:, :, :], v_ps, fb(f_dots[:, :]), ALU.mult), on)
                if ahead:
                    dst_one_hots(i, m + 2, 1)
                    src_one_hot(j, m, 2)
                src_one_hot(j, m, 3)
                settle(on, at)
                V.tensor_tensor(f_z[:, :, 1, :], f_rows[:, m, :, YS:YS + D], prod2[:, :, 0, :], ALU.subtract)
                V.tensor_tensor(f_z[:, :, 0, :], f_rows[:, m, :, YS + D:YS + 2 * D], prod2[:, :, 1, :], ALU.subtract).then_inc(f_free, 1)
                src_one_hot(j, m, 4)
                vec.wait_ge(f_free, j + SLOTS + 1)
                tick(V.tensor_tensor(f_prod[:, :, :], v_ps, zz, ALU.mult), on)
                src_one_hot(j, m, 5)
                settle(on, at)
                tick(V.tensor_reduce(f_dots[:, :], f_prod[:, :, :], AX.X, ALU.add), on)
                src_one_hot(j, m, 6)
                settle(on, at)
                tick(V.tensor_tensor(f_dots[:, :], f_dots[:, :], f_cc[:, :], ALU.mult), on)
                src_one_hot(j, m, 7)
                settle(on, at)
                V.tensor_tensor(f_prod[:, :, :], v_ps, fb(f_dots[:, :]), ALU.mult).then_inc(f_done, 1)
                V.tensor_tensor(f_oha[:, :, :], a_f[:, 0, bass.ds(j * (2 * G), 2 * G)].unsqueeze(2).to_broadcast([P, 2 * G, LO]),
                                iota_k[:, 0:LO].unsqueeze(1).to_broadcast([P, 2 * G, LO]), ALU.is_equal)
                vec.wait_ge(f_winps, j + 1)
                add_window(j, w, 0, bases[0])
                vec.wait_ge(f_done, j + 3)
                tick(V.tensor_tensor(f_msg[:, w, :, :], zz, f_prod[:, :, :], ALU.subtract), on)
                V.tensor_tensor(f_ohd[:, w, :, :], dst_rel[:, bass.ds(j * (2 * G), 2 * G)].unsqueeze(2).to_broadcast([P, 2 * G, WG]),
                                iota_k[:, 0:WG].unsqueeze(1).to_broadcast([P, 2 * G, WG]), ALU.is_equal)
                add_window(j, w, 1, bases[1])
                settle(on, at)
                V.tensor_tensor(f_m8[:, w, :, :, :], f_oha[:, :, :].unsqueeze(3).to_broadcast([P, 2 * G, LO, D]),
                                f_msg[:, w, :, :].rearrange("p (c s) f -> p c s f", s=2)[:, :, 0, :]
                                .unsqueeze(2).to_broadcast([P, 2 * G, LO, D]), ALU.mult).then_inc(f_mready, 1)

            def add_bases(i, n):
                _, bases = nc.values_load_multi_w_load_instructions(
                    g_base[0:1, bass.ds(i * (2 * SLOTS), n)], engines=(DVE,), min_val=0, max_val=NB * LO - 1,
                    skip_runtime_bounds_check_because=BASES_ARE_NODES)
                return bases

            def half_one_hots(first, r):
                h = first + r
                vec.wait_ge(c_ps, h + 1)
                for c in range(2):
                    ins = V.tensor_scalar(oh_key[:, r % 8, c, :], iota_h[:, :], key_f[:, bass.ds(h * 2 + c, 1)], None,
                                          ALU.is_equal)
                if r % 8 not in POOLS_HALVES:
                    ins = V.tensor_scalar(oh_lo[:, r % 8, 1, :], iota_h[:, 0:LANES], lo_f[:, bass.ds(h * 2 + 1, 1)], None,
                                          ALU.is_equal)
                ins.then_inc(c_key, 1)

            def half_bases(first, n):
                _, bases = nc.values_load_multi_w_load_instructions(
                    h_base[0:1, bass.ds(first, n)], engines=(DVE,), min_val=0, max_val=NB * LO - 1,
                    skip_runtime_bounds_check_because=BASES_ARE_NODES)
                return bases

            def half_add(first, r, base):
                h = first + r
                vec.wait_ge(c_sb, h + 9)
                vec.wait_ge(c_added, h + 4)
                V.tensor_tensor(counts[:, :, bass.ds(base, WH)], counts[:, :, bass.ds(base, WH)],
                                cnt_stage[:, r % 4, :].rearrange("p (h d) -> p h d", d=WH), ALU.add).then_inc(c_added, 1)

            def nodes_from(bank, on):
                w = (NT - 1) * LO
                V.tensor_copy(s_n[:, 0:w, :], bank[:, 0:w * D].rearrange("p (c f) -> p c f", f=D))
                step(V.tensor_copy(s_n[0:TAIL, w:w + LO, :],
                                   bank[0:TAIL, w * D:(w + LO) * D].rearrange("p (c f) -> p c f", f=D)), on=on)

            def to_nodes(k):
                vec.wait_ge(acc_ready[k], 1)
                V.tensor_copy(al[:, :], acc[:, 0:NB]).then_inc(al_ready[k], 1)
                vec.wait_ge(nl_ready[k], 1)
                nodes_from(misc, dve_general)

            FSP = 9
            SPG = 13
            with vec.If(fast > 0):
                for _ in range(2):
                    vec.sem_inc(f_done, 1)
                    vec.sem_inc(f_sqd, 1)
                vec.sem_inc(f_wadd, 1)
                for m in range(2):
                    for gg in range(2):
                        dst_one_hots(0, m, gg)
                V.memset(acc_dst[:, :], 0.0)
                step(V.memset(counts_f[:, edge_words:table_words], 0.0), on=dve_fast)
                before = counted[dve_fast]
                with vec.Fori(0, TURNS) as i:
                    bases = add_bases(i, 2 * SLOTS)
                    for m in range(SLOTS):
                        fast_pair(i, m, True, bases[2 * m:2 * m + 2], (i, SLOTS * FSP))
                assert counted[dve_fast] == before + SLOTS * FSP, counted[dve_fast] - before
                counted[dve_fast] = before + TURNS * SLOTS * FSP
                rest = NPAIR - TURNS * SLOTS
                bases = add_bases(TURNS, 2 * rest + 2)
                for m in range(rest):
                    fast_pair(TURNS, m, False, bases[2 * m:2 * m + 2], None)
                vec.wait_ge(f_winps, NPAIR + 1)
                for gg in range(2):
                    add_window(NPAIR, NPAIR % 2, gg, bases[2 * rest + gg])
                vec.wait_ge(acc_ready[3], 1)
                V.tensor_copy(al[:, :], acc[:, 0:NB]).then_inc(al_ready[0], 1)
                vec.wait_ge(nl_ready[0], 1)
                nodes_from(misc, dve_fast)
                vec.wait_ge(dst_nl, 1)
                w = (NT - 1) * LO
                V.tensor_tensor(s_n[:, 0:w, :], s_n[:, 0:w, :], p_ref[0][:, 0:w * D].rearrange("p (c f) -> p c f", f=D), ALU.add)
                V.tensor_tensor(s_n[0:TAIL, w:w + LO, :], s_n[0:TAIL, w:w + LO, :],
                                p_ref[0][0:TAIL, w * D:(w + LO) * D].rearrange("p (c f) -> p c f", f=D),
                                ALU.add).then_inc(dst_added, 1)
                vec.wait_ge(dst_added, 1)
            with vec.Else():
                part_of_node(1, LO - 1, None, a_f, dve_general)
                part_of_node(1, None, 3, b_f, dve_general)
                vec.wait_ge(tab_out[0], 32)
                step(V.tensor_copy(bias_rep[:, :, :].rearrange("p (g s) f -> p g (s f)", s=2),
                                   bias_ref[:, :, :].rearrange("p s f -> p (s f)").unsqueeze(1).to_broadcast([P, 2 * G, 2 * D])), on=dve_general)
                before = counted[dve_general]
                with vec.Fori(0, NG // 2) as i:
                    for u in range(2):
                        chunk = i * (2 * G) + u * G
                        reflect(i + 1, u, (i, 2 * SPG, chunk))
                        one_hots(i * (2 * 2 * G) + 1, u * 2 * G, (0, 1), chunk, oh_ready, oh_used)
                assert counted[dve_general] == before + 2 * SPG
                counted[dve_general] = before + NG * SPG
                to_nodes(0)

            def nbc(t):
                return t.unsqueeze(2).to_broadcast([P, NT * LO, D])

            def layer_norm(k, to, last=None):
                step(V.tensor_reduce(st[:, 0, :], s_n[:, :, :], AX.X, ALU.add))
                step(V.tensor_scalar(st[:, 1, :], st[:, 0, :], 1.0 / D, None, ALU.mult))
                step(V.tensor_tensor(s_n[:, :, :], s_n[:, :, :], nbc(st[:, 1, :]), ALU.subtract))
                step(V.tensor_tensor(t_n[:, :, :], s_n[:, :, :], s_n[:, :, :], ALU.mult))
                step(V.tensor_reduce(st[:, 0, :], t_n[:, :, :], AX.X, ALU.add))
                V.tensor_scalar(st[:, 2, :], st[:, 0, :], 1.0 / D, LN_EPS, ALU.mult, ALU.add).then_inc(root_in[k], 1)
                vec.wait_ge(root_out[k], 1)
                step(V.reciprocal(st[:, 3, :], st[:, 2, :]))
                ins = V.tensor_tensor(to[:, :, :], s_n[:, :, :], nbc(st[:, 3, :]), ALU.mult)
                if last is None:
                    step(ins)
                else:
                    ins.then_inc(last, 1)

            step(V.tensor_tensor(s_n[:, :, :], s_n[:, :, :], d0, ALU.mult))
            step(V.tensor_tensor(s_n[:, :, :], s_n[:, :, :], x_n[:, :, :], ALU.add))
            step(V.scalar_tensor_tensor(s_n[:, :, :].rearrange("p c f -> p (c f)"),
                                        s_n[:, :, :].rearrange("p c f -> p (c f)"), 0.0,
                                        x_n[:, :, :].rearrange("p c f -> p (c f)"), ALU.max, ALU.add))
            layer_norm(0, x1_n)
            V.memset(y_hl, 0.0)
            V.tensor_tensor(y_n[:, :, :], x1_n[:, :, :], d1, ALU.mult).then_inc(tab_ready[1], 1)
            vec.wait_ge(tab_ready[1], 1)

            def aggregate(k):
                with vec.Fori(0, NG // 2) as i:
                    for u in range(2):
                        chunk = i * (2 * G) + u * G
                        V.tensor_tensor(oh_a[:, u, 0:G, :], a_f[:, 1, bass.ds(chunk, G)].unsqueeze(2).to_broadcast([P, G, LO]),
                                        iota_b[:, 0:LO].unsqueeze(1).to_broadcast([P, G, LO]), ALU.is_equal).then_inc(l_oha[k], 1)
                        vec.wait_ge(l_oha[k], i * 2 + u + 1)
                        vec.wait_ge(l_gathered[k][u], i * (16 * G) + 16 * G)
                        V.tensor_tensor(m8[:, u, 0:G, :, :], oh_a[:, u, 0:G, :].unsqueeze(3).to_broadcast([P, G, LO, D]),
                                        g_xy[:, u, :, 0, 0:D].unsqueeze(2).to_broadcast([P, G, LO, D]),
                                        ALU.mult).then_inc(l_ready[k], 1)
                        vec.wait_ge(l_ready[k], 2 * i + u + 1)
                        V.tensor_copy(st[0:1, 0, 0:1], st[0:1, 1, 0:1]).then_inc(l_free[k], 1)
                        one_hots(i * (2 * G) + 1, u * G, (1,), chunk, l_oh[k], l_ohu[k])

            def build_counts():
                for _ in range(4):
                    vec.sem_inc(c_added, 1)
                vec.wait_ge(zeroed, 3)
                for r in range(AHEAD):
                    half_one_hots(0, r)
                turns = (NH - AHEAD) // HALVES
                with vec.Fori(0, turns) as i:
                    bases = half_bases(i * HALVES, HALVES)
                    for r in range(HALVES):
                        half_one_hots(i * HALVES, r + AHEAD)
                        half_add(i * HALVES, r, bases[r])
                first = turns * HALVES
                bases = half_bases(first, NH - first)
                for r in range(NH - first):
                    if first + r + AHEAD < NH:
                        half_one_hots(first, r + AHEAD)
                    half_add(first, r, bases[r])

            def product(k):
                if k == 0:
                    build_counts()
                vec.wait_ge(hl_in[k], 32)
                step(V.tensor_copy(y3[:, :, 0, :], y_hl[:, :, :]), on=dve_fast)
                step(V.tensor_tensor(r_hl[:, :, :], y_hl[:, :, :], y3[:, :, 0, :], ALU.subtract), on=dve_fast)
                step(V.tensor_copy(y3[:, :, 1, :], r_hl[:, :, :]), on=dve_fast)
                V.tensor_tensor(y3[:, :, 2, :], r_hl[:, :, :], y3[:, :, 1, :], ALU.subtract).then_inc(y3_ready[k], 1)
                for blk in range(0, NBLK, 2):
                    vec.wait_ge(sp_ps[k], blk + 1)
                    V.tensor_copy(agg3[:, blk * BLK:(blk + 1) * BLK], banks[blk][0:3 * D, 0:BLK]).then_inc(sp_sb[k], 1)
                vec.wait_ge(nl_ready[k + 1], 1)
                nodes_from(misc, dve_fast)

            def sum_over_edges(k):
                with vec.If(fast > 0):
                    product(k)
                with vec.Else():
                    aggregate(k)
                    to_nodes(k + 1)

            sum_over_edges(0)
            step(V.tensor_tensor(s_n[:, :, :], s_n[:, :, :], y_n[:, :, :], ALU.add))
            V.tensor_tensor(s_n[:, :, :], s_n[:, :, :], d1, ALU.mult).then_inc(agg_ready, 1)
            vec.wait_ge(al_ready[3], 1)
            V.tensor_copy(al[:, :], misc[:, 0:NB]).then_inc(al_ready[4], 1)
            vec.wait_ge(h_ready, 1)
            for h in range(2):
                ins = V.tensor_scalar(h_al[:, h, :], banks[1 + h][:, 0:NB], bn_vec[:, 0:1], None, ALU.add)
            step(ins)

            def zero_padding(t):
                for a in range(N_NODES - (NB - 1) * LO, LO):
                    r = (a - 4) * HID1
                    ins = V.memset(t[r:r + HID1, 1, NB - 1:NB], 0.0)
                step(ins)

            zero_padding(h_al)
            hf = h_al[:, :, :].rearrange("p h b -> p (h b)")
            hcf = hc_al[:, :, :].rearrange("p h b -> p (h b)")
            V.tensor_reduce(bn[:, 0:1], hf, AX.X, ALU.add).then_inc(sum_in[0], 1)
            vec.wait_ge(sum_out[0], 1)
            step(V.tensor_scalar(bn[:, 1:2], p_hid[0][:, 0:1], 1.0 / N_NODES, None, ALU.mult))
            step(V.tensor_scalar(hcf, hf, bn[:, 1:2], None, ALU.subtract))
            zero_padding(hc_al)
            step(V.tensor_tensor(hf, hcf, hcf, ALU.mult))
            V.tensor_reduce(bn[:, 2:3], hf, AX.X, ALU.add).then_inc(sum_in[1], 1)
            vec.wait_ge(sum_out[1], 1)
            V.tensor_scalar(bn[:, 3:4], p_hid[1][:, 0:1], 1.0 / N_NODES, LN_EPS, ALU.mult, ALU.add).then_inc(root_in[1], 1)
            vec.wait_ge(root_out[1], 1)
            step(V.reciprocal(bn[:, 4:5], bn[:, 3:4]))
            V.tensor_tensor(bn[:, 5:6], bn[:, 4:5], bn_vec[:, 1:2], ALU.mult).then_inc(bn_ready, 1)
            vec.wait_ge(u_ready, 1)
            V.tensor_copy(al[:, :], misc[:, 0:NB]).then_inc(u_sb, 1)
            vec.wait_ge(nl_ready[3], 1)
            w = (NT - 1) * LO
            V.tensor_tensor(y_n[:, 0:w, :], p_ref[0][:, 0:w * D].rearrange("p (c f) -> p c f", f=D), d1[:, 0:w, :], ALU.mult)
            V.tensor_tensor(y_n[0:TAIL, w:w + LO, :], p_ref[0][0:TAIL, w * D:(w + LO) * D].rearrange("p (c f) -> p c f", f=D),
                            d1[0:TAIL, w:w + LO, :], ALU.mult).then_inc(tab_ready[2], 1)
            vec.wait_ge(tab_ready[2], 1)
            step(V.tensor_tensor(x1_n[:, :, :], x1_n[:, :, :],
                                 bias_out[:, :].unsqueeze(1).to_broadcast([P, NT * LO, D]), ALU.add))
            sum_over_edges(1)
            step(V.tensor_tensor(s_n[:, :, :], s_n[:, :, :], y_n[:, :, :], ALU.add))
            step(V.tensor_tensor(s_n[:, :, :], s_n[:, :, :], d1, ALU.mult))
            step(V.tensor_tensor(s_n[:, :, :], s_n[:, :, :], x1_n[:, :, :], ALU.add))
            layer_norm(2, s_n, out_ready)

        @block.tensor
        def _(pe):
            M = nc.tensor.matmul
            pe.wait_ge(idx_rows, 1)
            for s in range(2):
                for t in range(RT):
                    r = min(P, NCH - t * P)
                    ins = nc.tensor.transpose(banks[1 + 2 * s + t // 4][:, (t % 4) * P:(t % 4) * P + r],
                                              rows_f[0:r, s, t, :], ident[0:r, 0:r])
            ins.then_inc(idx_cols, 1)
            pe.wait_ge(nodes_in, n_loads[nodes_in])
            for t in range(NT):
                w = min(P, NB - t * P)
                ins = nc.tensor.transpose(misc[:, t * P:t * P + w],
                                          x_n[0:w, t * LO:(t + 1) * LO, :].rearrange("p a f -> p (a f)"), ident[0:w, 0:w])
            ins.then_inc(xa_ps, 1)
            pe.wait_ge(xa_sb, 1)
            pe.wait_ge(q_ready, 1)
            for t in range(NT):
                w = min(P, NB - t * P)
                for h in range(2):
                    if t:
                        pe.wait_ge(win_w, 2 * (t - 1) + h + 1)
                    M(p_tr[h][0:w, :], xa[:, t * P:t * P + w], w_proj[:, 4 * h:4 * h + 4, :].rearrange("p a n -> p (a n)"),
                      start=True, stop=True).then_inc(proj_ps, 1)
            M(misc[0:NQ, 0:2 * QLO], zeros[:, 0:NQ], zeros[:, 0:2 * QLO], start=True, stop=False, skip_group_check=True)
            for s in range(2):
                pe.sem_inc(hist_used[s], 1)
            with pe.Fori(0, NCH // HG) as i:
                for s in range(2):
                    pe.wait_ge(oh_hist[s], i + 1)
                    for c in range(HG):
                        ins = M(misc[0:NQ, s * QLO:(s + 1) * QLO], oh_p[:, s, :, c], oh_q[:, s, :, c], start=False, stop=False,
                                skip_group_check=True)
                    ins.then_inc(hist_used[s], 1)
            M(misc[0:NQ, 0:2 * QLO], zeros[:, 0:NQ], zeros[:, 0:2 * QLO], start=False, stop=True,
              skip_group_check=True).then_inc(hist_done, 1)

            pe.wait_ge(viol_ready, 1)
            M(p_hid[0][0:1, 0:1], viol[:, 7:8], ones_col, start=True, stop=True).then_inc(viol_sum, 1)

            def turn(i, m):
                slot, time = m % SLOTS, i + m // SLOTS
                pe.wait_ge(f_gath[slot], time * (16 * 2 * G) + 16 * 2 * G)
                pe.nop(nofuse=True)
                for gg in range(2):
                    out_b = p_tr[gg][:, 0:G * P // 2].bitcast(BF16)
                    for c in range(G):
                        ins = nc.tensor.transpose(out_b[:, c * P:(c + 1) * P],
                                                  f_rows[:, slot, gg * G + c, 0:YS].bitcast(BF16), ident_b[:, :])
                    ins.then_inc(f_turned, 1)

            def fast_front(i, m, ahead=True):
                j, w, slot = i * SLOTS + m, m % 2, m % SLOTS
                for gg in range(2):
                    q = 2 * slot + gg
                    pe.wait_ge(f_ohdt, j * 2 + gg + 1)
                    pe.wait_ge(f_xready, j * 2 + gg + 1)
                    M(p_hid[gg][:, :], w_all[:, :], f_xT[:, gg, :], start=True, stop=False)
                    M(p_hid[gg][:, :], f_win[:, q, 0:2 * HID0], f_ohT[:, q, :], start=False, stop=True).then_inc(f_pre, 1)
                pe.wait_ge(f_done, j + 1)
                for gg in range(2):
                    q = 2 * slot + gg
                    for c in range(G):
                        k = 4 * G * D + (gg * G + c) * D
                        ins = M(p_ref[w][:, k:k + D], f_ohT[:, q, c * P:(c + 1) * P], f_win[:, q, 2 * HID0:WROW],
                                start=True, stop=True)
                    ins.then_inc(f_front, 1)
                if ahead:
                    turn(i, m + 1)

            def reflections(j, w, c):
                if c == 0:
                    M(p_ref[w][:, 0:4 * G * D], ones3[:, :], bias3[:, :], start=True, stop=False, skip_group_check=True)
                if c % G == 0:
                    pe.wait_ge(f_relu, j * 2 + c // G + 1)
                ins = M(p_ref[w][:, c * 2 * D:(c + 1) * 2 * D], f_hid[:, c // G, (c % G) * P:(c % G + 1) * P], w_ref[:, :],
                        start=False, stop=(c == 2 * G - 1), skip_group_check=True)
                if c == 2 * G - 1:
                    ins.then_inc(f_ref, 1)

            def scatter_windows(j, w):
                pe.wait_ge(f_mready, j + 1)
                for gg in range(2):
                    k = 2 * w + gg
                    for c in range(gg * G, gg * G + G):
                        ins = M(misc[0:D, k * WG:(k + 1) * WG], f_msg[:, w, 2 * c + 1, :], f_ohd[:, w, c, :],
                                start=(c % G == 0), stop=(c % G == G - 1))
                ins.then_inc(f_winps, 1)

            def scatter_chunk(j, m, c):
                pe.wait_ge(f_oh, j * (2 * G) + c + 1)
                M(acc[:, 0:NB], f_m8[:, m % 2, c, :, :].rearrange("p a f -> p (a f)"), f_ohb[:, (m * 2 * G + c) % FRING, :],
                  start=False, stop=False, skip_group_check=True).then_inc(f_ohu, 1)

            def count_half(i, r):
                h = i * 8 + r
                pe.wait_ge(c_sb, h + 1)
                pe.wait_ge(c_lo, h + 9)
                pe.wait_ge(c_key, h + 1)
                for c in range(2):
                    ins = M(banks[r][:, 0:NKEY], oh_lo[:, r, c, :], oh_key[:, r % 8, c, :], start=(c == 0), stop=(c == 1))
                ins.then_inc(c_ps, 1)

            def front(n, u):
                pe.wait_ge(gathered[u], n * (16 * 2 * G))
                pe.nop(nofuse=True)
                for c in range(G):
                    ins = nc.tensor.transpose(p_tr[u][0:64, c * P:(c + 1) * P],
                                              g_xy[:, u, c, :, :].rearrange("p s f -> p (s f)"), ident)
                ins.then_inc(turned, 1)
                pe.wait_ge(x_ready, 2 * n + u - 1)
                M(p_hid[u][:, :], w_hid[:, :], xT[:, u, :], start=True, stop=True).then_inc(pre_ready, 1)
                pe.wait_ge(v_taken, 2 * n + u - 1)
                pe.wait_ge(hid_ready, 2 * n + u - 1)
                for c in range(G):
                    ins = M(p_ref[u][:, c * 2 * D:(c + 1) * 2 * D], hidT[:, u, c * P:(c + 1) * P], w_ref[:, :],
                            start=True, stop=True)
                ins.then_inc(ref_ready, 1)

            def scatter(n, u, i):
                pe.wait_ge(m_ready, 2 * n + u - 1)
                for c in range(2 * G):
                    k = u * 2 * G + c
                    r = k % RING
                    pe.wait_ge(oh_ready, i * (2 * 2 * G) + k + 1)
                    ins = M(acc[:, 0:NB], m8[:, u, c, :, :].rearrange("p a f -> p (a f)"), oh_b[:, r, :],
                            start=False, stop=False, skip_group_check=True)
                    ins.then_inc(oh_used, 1)

            def clear():
                return M(acc[:, 0:NB], zeros[:, :], iota_b, start=True, stop=False, skip_group_check=True)

            def close(k):
                M(acc[:, 0:NB], zeros[:, :], iota_b, start=False, stop=True, skip_group_check=True).then_inc(acc_ready[k], 1)

            def to_tiles(bank, src_t, done):
                for t in range(NT):
                    w = min(P, NB - t * P)
                    ins = nc.tensor.transpose(bank[0:w, t * P:(t + 1) * P], src_t[:, t * P:t * P + w], ident)
                ins.then_inc(done, 1)

            pe.wait_ge(flag_ready, 1)
            fast = pe.value_load(flag[0:1, 0:1], min_val=0, max_val=1)
            with pe.If(fast > 0):
                clear()
                for r in range(FRING):
                    pe.sem_inc(f_ohu, 1)
                for q in range(2 * SLOTS):
                    pe.sem_inc(f_front, 1)
                M(misc[0:D, 0:4 * WG], zeros[:, 0:D], zeros[:, 0:4 * WG], start=True, stop=True).then_inc(f_winps, 1)
                pe.wait_ge(w_ready, 1)
                turn(0, 0)
                for m in range(2):
                    fast_front(0, m)
                    for c in range(2 * G):
                        reflections(m, m, c)

                def front_and_scatter(i, m, ahead=True):
                    j = i * SLOTS + m
                    fast_front(i, m, ahead)
                    scatter_windows(j - 2, m % 2)
                    for c in range(2 * G):
                        scatter_chunk(j - 2, m - 2, c)
                        reflections(j, m % 2, c)

                turns = (NPAIR - 3) // SLOTS
                with pe.Fori(0, turns) as i:
                    for m in range(SLOTS):
                        front_and_scatter(i, m + 2)
                for m in range(2, NPAIR - turns * SLOTS):
                    front_and_scatter(turns, m, turns * SLOTS + m + 1 < NPAIR)
                for j in (NPAIR - 2, NPAIR - 1):
                    scatter_windows(j, j % 2)
                    for c in range(2 * G):
                        scatter_chunk(j, j, c)
                close(3)
                pe.wait_ge(f_wadd, NG + 3)
                for t in range(NT):
                    w = min(P, NB - t * P)
                    for a in range(LO):
                        k = t * P * LO + a
                        ins = nc.tensor.transpose(p_ref[0][0:w, (t * LO + a) * D:(t * LO + a + 1) * D],
                                                  acc_dst[:, k:k + LO * (w - 1) + 1:LO], ident[0:D, 0:D])
                ins.then_inc(dst_nl, 1)
                pe.wait_ge(al_ready[0], 1)
                to_tiles(misc, al, nl_ready[0])
            with pe.Else():
                clear()
                for r in range(RING):
                    pe.sem_inc(oh_used, 1)
                for u in range(2):
                    pe.sem_inc(turned, 1)
                    pe.sem_inc(v_taken, 1)
                front(1, 0)
                with pe.Fori(0, NG // 2 - 1) as i:
                    front(i + 1, 1)
                    scatter(i + 1, 0, i)
                    front(i + 2, 0)
                    scatter(i + 1, 1, i)
                n = NG // 2
                front(n, 1)
                scatter(n, 0, n - 1)
                scatter(n, 1, n - 1)
                close(0)

                pe.wait_ge(al_ready[0], 1)
                to_tiles(misc, al, nl_ready[0])

            def aggregate(k):
                clear()
                for r in range(RING):
                    pe.sem_inc(l_ohu[k], 1)
                with pe.Fori(0, NG // 2) as i:
                    for u in range(2):
                        pe.wait_ge(l_ready[k], 2 * i + u + 1)
                        for c in range(G):
                            j = u * G + c
                            r = j % RING
                            pe.wait_ge(l_oh[k], i * (2 * G) + j + 1)
                            ins = M(acc[:, 0:NB], m8[:, u, c, :, :].rearrange("p a f -> p (a f)"), oh_b[:, r, :],
                                    start=False, stop=False, skip_group_check=True)
                            ins.then_inc(l_ohu[k], 1)
                close(k + 1)

            def build_counts():
                for _ in range(8):
                    pe.sem_inc(c_ps, 1)
                    pe.sem_inc(c_sb, 1)
                with pe.Fori(0, NH // 8) as i:
                    for r in range(8):
                        count_half(i, r)

            def product(k):
                if k == 0:
                    build_counts()
                pe.wait_ge(y3_ready[k], 1)
                if k == 0:
                    pe.wait_ge(c_added, NH + 4)
                for blk in range(NBLK):
                    for hi in range(NHI):
                        ins = M(banks[blk][0:3 * D, 0:BLK], y3[:, hi, :, :].rearrange("p s f -> p (s f)"),
                                counts[:, hi, blk * BLK:(blk + 1) * BLK], start=(hi == 0), stop=(hi == NHI - 1))
                    ins.then_inc(sp_ps[k], 1)
                pe.wait_ge(sp_sb[k], (NBLK + 1) // 2)
                pe.wait_ge(sp_act[k], NBLK // 2)
                for t in range(NT):
                    w = min(P, NB - t * P)
                    for a in range(LO):
                        n0 = t * P * LO + a
                        ins = M(misc[0:w, (t * LO + a) * D:(t * LO + a + 1) * D], agg3[:, n0:n0 + LO * (w - 1) + 1:LO],
                                same_feat[0:3 * D, :], start=True, stop=True)
                ins.then_inc(nl_ready[k + 1], 1)

            def sum_over_edges(k):
                with pe.If(fast > 0):
                    product(k)
                with pe.Else():
                    aggregate(k)
                    pe.wait_ge(al_ready[k + 1], 1)
                    to_tiles(misc, al, nl_ready[k + 1])

            sum_over_edges(0)
            pe.wait_ge(agg_ready, 1)
            for t in range(NT):
                w = min(P, NB - t * P)
                ins = nc.tensor.transpose(misc[:, t * P:t * P + w],
                                          s_n[0:w, t * LO:(t + 1) * LO, :].rearrange("p a f -> p (a f)"), ident[0:w, 0:w])
            ins.then_inc(al_ready[3], 1)
            pe.wait_ge(al_ready[4], 1)
            for h in range(2):
                ins = M(banks[1 + h][:, 0:NB], w1_diag[:, h, :], al[:, :], start=True, stop=True)
            ins.then_inc(h_ready, 1)
            for k, col in ((0, 0), (1, 2)):
                pe.wait_ge(sum_in[k], 1)
                M(p_hid[k][:, 0:1], same_unit, bn[:, col:col + 1], start=True, stop=True).then_inc(sum_out[k], 1)
            pe.wait_ge(relu_ready, 2)
            for h in range(2):
                ins = M(misc[:, 0:NB], w2_diag[:, h, :], h_al[:, h, :], start=(h == 0), stop=(h == 1))
            ins.then_inc(u_ready, 1)
            pe.wait_ge(u_sb, 1)
            to_tiles(p_ref[0], al, nl_ready[3])
            sum_over_edges(1)


def kernel(**inputs):
    import numpy as _np
    import concourse.bacc as _bacc
    from concourse import mybir as _mybir
    from concourse.bass_utils import run_bass_kernel_spmd as _run

    nc = _bacc.Bacc("TRN2", target_bir_lowering=False, num_devices=1)
    lane = _np.arange(P)
    shape_consts = _np.concatenate([
        _np.eye(P), lane[:, None] % HID1 == lane[None, :] % HID1, lane[:, None] % 32,
        lane[:, None] % D == _np.arange(D)[None, :],
        _np.array(PIECE_WEIGHTS)[lane // D][:, None] == _np.arange(SPLIT)[None, :], _np.tile(_np.arange(NIOTA), (P, 1)),
    ], axis=1, dtype=_np.float32)
    given = {
        "x": inputs["x"], "src": inputs["src"], "dst": inputs["dst"],
        "w0_in": _np.asarray(inputs["L0_gnn_W1"]).T, "b0_in": inputs["L0_gnn_b1"],
        "w0_out": _np.asarray(inputs["L0_gnn_W2"]).T, "b0_out": inputs["L0_gnn_b2"],
        "w1": inputs["L1_gnn_W1"], "b1": inputs["L1_gnn_b1"], "gamma": inputs["L1_gnn_gamma"],
        "beta": inputs["L1_gnn_beta"], "w2": inputs["L1_gnn_W2"], "b2": inputs["L1_gnn_b2"],
        "shape_consts": shape_consts,
    }
    arrays, args = {}, []
    for name, a in given.items():
        a = _np.ascontiguousarray(a)
        arrays[f"in_{name}"] = a
        args.append(nc.dram_tensor(f"in_{name}", a.shape, _mybir.dt.from_np(a.dtype), kind="ExternalInput").ap())
    args.append(nc.dram_tensor("out_0", (N_NODES, D), F32, kind="ExternalOutput").ap())
    gnn(nc, *args)
    r = _run(nc, [arrays], core_ids=[0])
    return r.results[0]["out_0"]
```
